# Optimizing a Trainium2 kernel written in Bass

```python
import numpy as np
import jax
import jax.numpy as jnp

def _softmax(x, axis=-1):
    return jax.nn.softmax(x, axis=axis)

def _gelu(x):
    return jax.nn.gelu(x, approximate=True)

def _silu(x):
    return jax.nn.silu(x)

def _sigmoid(x):
    return jax.nn.sigmoid(x)

def _layernorm(x, axis=-1, eps=1e-05):
    m = jnp.mean(x, axis=axis, keepdims=True)
    v = jnp.var(x, axis=axis, keepdims=True)
    return (x - m) / jnp.sqrt(v + eps)

def _scatter_add(tgt, idx, src, axis=0):
    return tgt.at[idx].add(src)

def _segment_sum(src, seg, n):
    return jax.ops.segment_sum(src, seg, n)
kernel_name = 'mk_vit_tower_d2_tok_img1024_r4_19e65e'

def setup_inputs(seed: int=0):
    np.random.seed(seed)
    _w = jnp.asarray

    def _rec_inputs():
        import jax
        import jax.numpy as jnp
        _rk = jax.random.key(seed)
        x = -0.000392918 + 0.999932 * jax.random.normal(jax.random.fold_in(_rk, 1), (16, 256, 256, 1), jnp.float32)
        return x
    x = _rec_inputs()

    def _L0_tok_setup():
        import jax, jax.numpy as jnp
        import numpy as np
        INV_SQRT2 = 0.7071067811865476
        LEVEL = 3

        def _split(x, axis):
            ax = axis % x.ndim
            sl0 = [slice(None)] * x.ndim
            sl0[ax] = slice(0, None, 2)
            sl1 = [slice(None)] * x.ndim
            sl1[ax] = slice(1, None, 2)
            x0, x1 = (x[tuple(sl0)], x[tuple(sl1)])
            return ((x0 + x1) * INV_SQRT2, (x0 - x1) * INV_SQRT2)

        def _merge(lo, hi, axis):
            ax = axis % lo.ndim
            e = (lo + hi) * INV_SQRT2
            o = (lo - hi) * INV_SQRT2
            s = jnp.stack([e, o], axis=ax + 1)
            shape = list(lo.shape)
            shape[ax] *= 2
            return s.reshape(shape)

        def _dwt2(x):
            lo, hi = _split(x, -1)
            a, h = _split(lo, -2)
            v, d = _split(hi, -2)
            return (a, h, v, d)

        def _idwt2(a, h, v, d):
            lo = _merge(a, h, -2)
            hi = _merge(v, d, -2)
            return _merge(lo, hi, -1)
        key = jax.random.key(seed)
        ks = jax.random.split(key, 8)
        B, H, W = (16, 256, 256)
        x = jax.random.normal(ks[0], (B, H, W, 1), dtype=jnp.float32)
        na = H // 8 * (W // 8)
        n2 = H // 4 * (W // 4)
        n1 = H // 2 * (W // 2)
        scale = 0.02
        Wa = jax.random.normal(ks[1], (na, 1), dtype=jnp.float32) * scale
        ba = jnp.zeros((1,), jnp.float32)
        Wd1 = jax.random.normal(ks[2], (3 * na, 3), dtype=jnp.float32) * scale
        bd1 = jnp.zeros((3,), jnp.float32)
        Wd2 = jax.random.normal(ks[3], (3 * n2, 3), dtype=jnp.float32) * scale
        bd2 = jnp.zeros((3,), jnp.float32)
        Wd3 = jax.random.normal(ks[4], (3 * n1, 3), dtype=jnp.float32) * scale
        bd3 = jnp.zeros((3,), jnp.float32)
        return {'x': x, 'Wa': Wa, 'ba': ba, 'Wd1': Wd1, 'bd1': bd1, 'Wd2': Wd2, 'bd2': bd2, 'Wd3': Wd3, 'bd3': bd3}
    _L0_tok_all = _L0_tok_setup()
    _L0_tok_in = {k: v for k, v in _L0_tok_all.items() if k in ('Wa', 'ba', 'Wd1', 'bd1', 'Wd2', 'bd2', 'Wd3', 'bd3')}
    del _L0_tok_all

    def _L0_attn_setup():
        import jax, jax.numpy as jnp
        import numpy as np
        B, T, C = (4, 512, 256)
        N_HEAD = 16
        HEAD_DIM = C // N_HEAD
        key = jax.random.key(seed)
        k1, k2, k3, k4, k5 = jax.random.split(key, 5)
        sigma = (1.0 / C) ** 0.5
        return {'x': jax.random.normal(k1, (B, T, C), dtype=jnp.float32), 'W_attn': jax.random.normal(k2, (3 * C, C), dtype=jnp.float32) * sigma, 'b_attn': jax.random.normal(k3, (3 * C,), dtype=jnp.float32), 'W_proj': jax.random.normal(k4, (C, C), dtype=jnp.float32) * sigma, 'b_proj': jax.random.normal(k5, (C,), dtype=jnp.float32)}
    _L0_attn_all = _L0_attn_setup()
    _L0_attn_in = {k: v for k, v in _L0_attn_all.items() if k in ('W_attn', 'b_attn', 'W_proj', 'b_proj')}
    del _L0_attn_all

    def _L0_ffn_setup():
        import jax, jax.numpy as jnp
        import numpy as np
        B, S, H, F, G = (8, 512, 256, 1024, 128)
        EPS = 1e-05

        def _dequant(q, scales, g):
            K, N = q.shape
            w = (q.astype(jnp.float32) - 128.0).reshape(K // g, g, N) * scales[:, None, :]
            return w.reshape(K, N)
        key = jax.random.key(seed)
        ks = jax.random.split(key, 8)
        x = jax.random.normal(ks[0], (B, S, H), dtype=jnp.float32)
        ln_gamma = jnp.ones((H,), jnp.float32)
        ln_beta = jnp.zeros((H,), jnp.float32)
        fc1_q = jax.random.randint(ks[1], (H, F), 0, 64, dtype=jnp.int32)
        fc2_q = jax.random.randint(ks[2], (F, H), 0, 64, dtype=jnp.int32)
        fc1_scales = jax.random.uniform(ks[3], (H // G, F), jnp.float32) * 0.02 + 0.001
        fc2_scales = jax.random.uniform(ks[4], (F // G, H), jnp.float32) * 0.02 + 0.001
        fc1_bias = jax.random.normal(ks[5], (F,), jnp.float32) * 0.02
        fc2_bias = jax.random.normal(ks[6], (H,), jnp.float32) * 0.02
        return {'x': x, 'ln_gamma': ln_gamma, 'ln_beta': ln_beta, 'fc1_q': fc1_q, 'fc1_scales': fc1_scales, 'fc1_bias': fc1_bias, 'fc2_q': fc2_q, 'fc2_scales': fc2_scales, 'fc2_bias': fc2_bias}
    _L0_ffn_all = _L0_ffn_setup()
    _L0_ffn_in = {k: v for k, v in _L0_ffn_all.items() if k in ('ln_gamma', 'ln_beta', 'fc1_q', 'fc1_scales', 'fc1_bias', 'fc2_q', 'fc2_scales', 'fc2_bias')}
    del _L0_ffn_all

    def _L1_attn_setup():
        import jax, jax.numpy as jnp
        import numpy as np
        B, N, DIM = (4, 256, 256)
        H, DH, ORDER = (16, 64, 3)
        MAXREL = 64
        INNER = H * DH
        VOCAB = 2 * MAXREL + 1
        SCALE = DH ** (-0.5)
        TOPK = int(0.25 * N)
        key = jax.random.key(seed)
        ks = jax.random.split(key, 8)
        s = 0.02
        return {'x': jax.random.normal(ks[0], (B, N, DIM), jnp.float32), 'Wqkv': jax.random.normal(ks[1], (3 * INNER, DIM), jnp.float32) * s, 'bqkv': jnp.zeros((3 * INNER,), jnp.float32), 'Wout': jax.random.normal(ks[2], (DIM, INNER), jnp.float32) * s, 'bout': jnp.zeros((DIM,), jnp.float32), 'rel_k_emb': jax.random.normal(ks[3], (VOCAB, DH), jnp.float32) * s, 'rel_v_emb': jax.random.normal(ks[4], (VOCAB, DH), jnp.float32) * s, 'alphas_raw': jax.random.normal(ks[5], (ORDER, H), jnp.float32) * 0.5}
    _L1_attn_all = _L1_attn_setup()
    _L1_attn_in = {k: v for k, v in _L1_attn_all.items() if k in ('Wqkv', 'bqkv', 'Wout', 'bout', 'rel_k_emb', 'rel_v_emb', 'alphas_raw')}
    del _L1_attn_all

    def _L1_ffn_setup():
        import jax, jax.numpy as jnp
        import numpy as np
        B, S, D, E, H, K = (64, 512, 256, 32, 1024, 8)
        key = jax.random.key(seed)
        k0, k1, k2, k3 = jax.random.split(key, 4)
        x = jax.random.normal(k0, (B, S, D), jnp.float32)
        gate_w = jax.random.normal(k1, (E, D), jnp.float32) * (1.0 / np.sqrt(D))
        gate_b = jnp.zeros((E,), jnp.float32)
        w1 = jax.random.normal(k2, (E, D + 1, H), jnp.float32) * (1.0 / np.sqrt(D + 1))
        w2 = jax.random.normal(k3, (E, H + 1, D), jnp.float32) * (1.0 / np.sqrt(H + 1))
        return {'x': x, 'gate_w': gate_w, 'gate_b': gate_b, 'w1': w1, 'w2': w2}
    _L1_ffn_all = _L1_ffn_setup()
    _L1_ffn_in = {k: v for k, v in _L1_ffn_all.items() if k in ('gate_w', 'gate_b', 'w1', 'w2')}
    del _L1_ffn_all
    return {'x': x, 'L0_tok_Wa': _L0_tok_in['Wa'], 'L0_tok_ba': _L0_tok_in['ba'], 'L0_tok_Wd1': _L0_tok_in['Wd1'], 'L0_tok_bd1': _L0_tok_in['bd1'], 'L0_tok_Wd2': _L0_tok_in['Wd2'], 'L0_tok_bd2': _L0_tok_in['bd2'], 'L0_tok_Wd3': _L0_tok_in['Wd3'], 'L0_tok_bd3': _L0_tok_in['bd3'], 'L0_attn_W_attn': _L0_attn_in['W_attn'], 'L0_attn_b_attn': _L0_attn_in['b_attn'], 'L0_attn_W_proj': _L0_attn_in['W_proj'], 'L0_attn_b_proj': _L0_attn_in['b_proj'], 'L0_ffn_ln_gamma': _L0_ffn_in['ln_gamma'], 'L0_ffn_ln_beta': _L0_ffn_in['ln_beta'], 'L0_ffn_fc1_q': _L0_ffn_in['fc1_q'], 'L0_ffn_fc1_scales': _L0_ffn_in['fc1_scales'], 'L0_ffn_fc1_bias': _L0_ffn_in['fc1_bias'], 'L0_ffn_fc2_q': _L0_ffn_in['fc2_q'], 'L0_ffn_fc2_scales': _L0_ffn_in['fc2_scales'], 'L0_ffn_fc2_bias': _L0_ffn_in['fc2_bias'], 'L1_attn_Wqkv': _L1_attn_in['Wqkv'], 'L1_attn_bqkv': _L1_attn_in['bqkv'], 'L1_attn_Wout': _L1_attn_in['Wout'], 'L1_attn_bout': _L1_attn_in['bout'], 'L1_attn_rel_k_emb': _L1_attn_in['rel_k_emb'], 'L1_attn_rel_v_emb': _L1_attn_in['rel_v_emb'], 'L1_attn_alphas_raw': _L1_attn_in['alphas_raw'], 'L1_ffn_gate_w': _L1_ffn_in['gate_w'], 'L1_ffn_gate_b': _L1_ffn_in['gate_b'], 'L1_ffn_w1': _L1_ffn_in['w1'], 'L1_ffn_w2': _L1_ffn_in['w2']}

def reference(x, L0_tok_Wa, L0_tok_ba, L0_tok_Wd1, L0_tok_bd1, L0_tok_Wd2, L0_tok_bd2, L0_tok_Wd3, L0_tok_bd3, L0_attn_W_attn, L0_attn_b_attn, L0_attn_W_proj, L0_attn_b_proj, L0_ffn_ln_gamma, L0_ffn_ln_beta, L0_ffn_fc1_q, L0_ffn_fc1_scales, L0_ffn_fc1_bias, L0_ffn_fc2_q, L0_ffn_fc2_scales, L0_ffn_fc2_bias, L1_attn_Wqkv, L1_attn_bqkv, L1_attn_Wout, L1_attn_bout, L1_attn_rel_k_emb, L1_attn_rel_v_emb, L1_attn_alphas_raw, L1_ffn_gate_w, L1_ffn_gate_b, L1_ffn_w1, L1_ffn_w2):
    import jax
    import jax.numpy as jnp

    def _L0_tok_ref(x, Wa, ba, Wd1, bd1, Wd2, bd2, Wd3, bd3):
        import jax, jax.numpy as jnp
        import numpy as np
        INV_SQRT2 = 0.7071067811865476
        LEVEL = 3

        def _split(x, axis):
            ax = axis % x.ndim
            sl0 = [slice(None)] * x.ndim
            sl0[ax] = slice(0, None, 2)
            sl1 = [slice(None)] * x.ndim
            sl1[ax] = slice(1, None, 2)
            x0, x1 = (x[tuple(sl0)], x[tuple(sl1)])
            return ((x0 + x1) * INV_SQRT2, (x0 - x1) * INV_SQRT2)

        def _merge(lo, hi, axis):
            ax = axis % lo.ndim
            e = (lo + hi) * INV_SQRT2
            o = (lo - hi) * INV_SQRT2
            s = jnp.stack([e, o], axis=ax + 1)
            shape = list(lo.shape)
            shape[ax] *= 2
            return s.reshape(shape)

        def _dwt2(x):
            lo, hi = _split(x, -1)
            a, h = _split(lo, -2)
            v, d = _split(hi, -2)
            return (a, h, v, d)

        def _idwt2(a, h, v, d):
            lo = _merge(a, h, -2)
            hi = _merge(v, d, -2)
            return _merge(lo, hi, -1)
        img = x[..., 0]
        B = img.shape[0]
        details = []
        cur = img
        for _ in range(LEVEL):
            cur, h, v, d = _dwt2(cur)
            details.append((h, v, d))
        aw = jax.nn.sigmoid(cur.reshape(B, -1) @ Wa + ba)
        rec = cur * aw[:, :, None]
        det_params = [(Wd1, bd1), (Wd2, bd2), (Wd3, bd3)]
        for (h, v, d), (Wd, bd) in zip(reversed(details), det_params):
            flat = jnp.stack([h, v, d], axis=1).reshape(B, -1)
            w = jax.nn.softmax(flat @ Wd + bd, axis=-1)
            rec = _idwt2(rec, h * w[:, 0, None, None], v * w[:, 1, None, None], d * w[:, 2, None, None])
        return rec

    def _L0_attn_ref(x, W_attn, b_attn, W_proj, b_proj):
        import jax, jax.numpy as jnp
        import numpy as np
        B, T, C = (4, 512, 256)
        N_HEAD = 16
        HEAD_DIM = C // N_HEAD
        Bq, Tq, Cq = x.shape
        qkv = x @ W_attn.T + b_attn
        q, k, v = jnp.split(qkv, 3, axis=-1)

        def to_heads(t):
            return t.reshape(Bq, Tq, N_HEAD, HEAD_DIM).transpose(0, 2, 1, 3)
        q, k, v = (to_heads(q), to_heads(k), to_heads(v))
        att = jnp.einsum('bhqd,bhkd->bhqk', q, k) * (1.0 / HEAD_DIM)
        causal = jnp.tril(jnp.ones((Tq, Tq), dtype=bool))
        att = jnp.where(causal[None, None], att, -jnp.inf)
        att = jax.nn.softmax(att, axis=-1)
        y = jnp.einsum('bhqk,bhkd->bhqd', att, v)
        y = y.transpose(0, 2, 1, 3).reshape(Bq, Tq, Cq)
        return y @ W_proj.T + b_proj

    def _L0_ffn_ref(x, ln_gamma, ln_beta, fc1_q, fc1_scales, fc1_bias, fc2_q, fc2_scales, fc2_bias):
        import jax, jax.numpy as jnp
        import numpy as np
        B, S, H, F, G = (8, 512, 256, 1024, 128)
        EPS = 1e-05

        def _dequant(q, scales, g):
            K, N = q.shape
            w = (q.astype(jnp.float32) - 128.0).reshape(K // g, g, N) * scales[:, None, :]
            return w.reshape(K, N)
        residual = x
        mu = jnp.mean(x, axis=-1, keepdims=True)
        var = jnp.mean(jnp.square(x - mu), axis=-1, keepdims=True)
        h = (x - mu) * jax.lax.rsqrt(var + EPS) * ln_gamma + ln_beta
        hf = h.reshape(-1, H)
        w1 = _dequant(fc1_q, fc1_scales, G)
        y = hf @ w1 + fc1_bias
        y = jax.nn.silu(y)
        w2 = _dequant(fc2_q, fc2_scales, G)
        z = y @ w2 + fc2_bias
        return residual + 0.5 * z.reshape(residual.shape)

    def _L1_attn_ref(x, Wqkv, bqkv, Wout, bout, rel_k_emb, rel_v_emb, alphas_raw):
        import jax, jax.numpy as jnp
        import numpy as np
        B, N, DIM = (4, 256, 256)
        H, DH, ORDER = (16, 64, 3)
        MAXREL = 64
        INNER = H * DH
        VOCAB = 2 * MAXREL + 1
        SCALE = DH ** (-0.5)
        TOPK = int(0.25 * N)
        b, n, _ = x.shape
        qkv = x @ Wqkv.T + bqkv
        q, k, v = jnp.split(qkv, 3, axis=-1)
        to_heads = lambda t: t.reshape(b, n, H, DH).transpose(0, 2, 1, 3)
        q, k, v = (to_heads(q), to_heads(k), to_heads(v))
        scores = jnp.einsum('bhid,bhjd->bhij', q, k) * SCALE
        coords = jnp.arange(n)
        dist = jnp.clip(coords[:, None] - coords[None, :], -MAXREL, MAXREL) + MAXREL
        rel_k = rel_k_emb[dist]
        scores = scores + jnp.einsum('bhid,ijd->bhij', q, rel_k)
        top_vals = jax.lax.top_k(scores, TOPK)[0]
        threshold = top_vals[..., -1:]
        scores = jnp.where(scores < threshold, -jnp.inf, scores)
        attn = jax.nn.softmax(scores, axis=-1)
        rel_v = rel_v_emb[dist]
        alphas = jax.nn.sigmoid(alphas_raw)
        res = jnp.zeros_like(v)
        v_curr = v
        for i in range(ORDER):
            a_v = jnp.einsum('bhij,bhjd->bhid', attn, v_curr)
            if i == 0:
                a_v = a_v + jnp.einsum('bhij,ijd->bhid', attn, rel_v)
            v_curr = a_v
            res = res + alphas[i][None, :, None, None] * v_curr
        out = res.transpose(0, 2, 1, 3).reshape(b, n, INNER)
        return out @ Wout.T + bout

    def _L1_ffn_ref(x, gate_w, gate_b, w1, w2):
        import jax, jax.numpy as jnp
        import numpy as np
        B, S, D, E, H, K = (64, 512, 256, 32, 1024, 8)
        b, s, d = x.shape
        logits = jnp.einsum('bsd,ed->bse', x, gate_w) + gate_b
        probs = jax.nn.softmax(logits, axis=-2)
        vals_t, idx_t = jax.lax.top_k(probs.transpose(0, 2, 1), K)
        vals = vals_t.transpose(0, 2, 1)
        idx = idx_t.transpose(0, 2, 1)
        flat_idx = idx.reshape(b, K * E)
        tok = jnp.take_along_axis(x, flat_idx[:, :, None], axis=1)
        tok = tok.reshape(b, K, E, d)
        merged = jnp.einsum('bked,bke->bed', tok, vals)
        ones = jnp.ones(merged.shape[:-1] + (1,), merged.dtype)
        h = jnp.einsum('bei,eih->beh', jnp.concatenate([merged, ones], -1), w1)
        h = jax.nn.gelu(h, approximate=False)
        o = jnp.einsum('bej,ejo->beo', jnp.concatenate([h, ones], -1), w2)
        out_tok = jnp.einsum('beo,bke->bkeo', o, vals).reshape(b, K * E, d)
        out = jnp.zeros_like(x).at[jnp.arange(b)[:, None], flat_idx].add(out_tok)
        return out
    h = _L0_tok_ref(x, L0_tok_Wa, L0_tok_ba, L0_tok_Wd1, L0_tok_bd1, L0_tok_Wd2, L0_tok_bd2, L0_tok_Wd3, L0_tok_bd3)
    h = h + _L0_attn_ref(_layernorm(h, axis=-1), L0_attn_W_attn, L0_attn_b_attn, L0_attn_W_proj, L0_attn_b_proj)
    h = h + _L0_ffn_ref(_layernorm(h, axis=-1), L0_ffn_ln_gamma, L0_ffn_ln_beta, L0_ffn_fc1_q, L0_ffn_fc1_scales, L0_ffn_fc1_bias, L0_ffn_fc2_q, L0_ffn_fc2_scales, L0_ffn_fc2_bias)
    h = h + _L1_attn_ref(_layernorm(h, axis=-1), L1_attn_Wqkv, L1_attn_bqkv, L1_attn_Wout, L1_attn_bout, L1_attn_rel_k_emb, L1_attn_rel_v_emb, L1_attn_alphas_raw)
    h = h + _L1_ffn_ref(_layernorm(h, axis=-1), L1_ffn_gate_w, L1_ffn_gate_b, L1_ffn_w1, L1_ffn_w2)
    return h

_drawn_inputs = setup_inputs


def setup_inputs(seed=0):
    import zlib

    import numpy as np

    out = dict(_drawn_inputs(seed))
    spreads = {'L0_tok_bd1': (0.0, 0.732),
     'L0_tok_bd2': (0.0, 0.8),
     'L0_tok_bd3': (0.0, 0.8),
     'L0_ffn_ln_gamma': (1.0, 0.2),
     'L0_ffn_ln_beta': (0.0, 0.1),
     'L1_attn_bqkv': (0.0, 2.0),
     'L1_attn_bout': (0.0, 2.0),
     'L1_ffn_gate_b': (0.0, 0.8)}
    factors = {'L0_ffn_fc1_bias': 64.0,
     'L0_ffn_fc2_bias': 64.0,
     'L1_attn_Wqkv': 8.0,
     'L1_attn_Wout': 8.0,
     'L1_attn_rel_k_emb': 64.0,
     'L1_attn_rel_v_emb': 64.0,
     'L1_attn_alphas_raw': 27.459,
     'L1_ffn_gate_w': 64.0,
     'L1_ffn_w1': 64.0,
     'L1_ffn_w2': 64.0}
    for name, (base, spread) in spreads.items():
        noise = np.random.default_rng([zlib.crc32(name.encode()), seed]).standard_normal(out[name].shape)
        drawn = base * np.exp(spread * noise) if base else spread * noise
        out[name] = jnp.asarray(drawn.astype(out[name].dtype))
    for name, factor in factors.items():
        out[name] = (out[name] * factor).astype(out[name].dtype)
    return out
```

```python
from contextlib import ExitStack

import concourse.bass as bass
from concourse import mybir

ALU = mybir.AluOpType
ACT = mybir.ActivationFunctionType
AX = mybir.AxisListType
F32 = mybir.dt.float32
BF16 = mybir.dt.bfloat16
I32 = mybir.dt.int32

P = 128
B = 16
T = 256
C = 256
NT = T // P
NC = C // P
EPS = 1e-5
NEG = -1e30

IMGS = 4
GROUPS = B // IMGS
RB = 32
BR = T // RB
LEVELS = 3

H0, D0, SLOT = 16, 16, 32
HPM = P // SLOT
MQ = H0 // HPM

F0 = 1024
NF = F0 // P

H1, D1 = 16, 64
INNER = H1 * D1
MAXREL = 64
TOPK = T // 4
ROUNDS = TOPK // 8
EXTW = 3 * P - 1
EXTN = 2 * T - 1
PITCH = 3 * P
BAND = 2 * MAXREL - 1
ORDER = 3

E1, HID, K1 = 32, 1024, 8
NH = HID // P
WBUFS = 4


class Chain:

    def __init__(self, eng, sem):
        self.eng, self.sem, self.n = eng, sem, 0

    def step(self, ins):
        self.n += 1
        ins.then_inc(self.sem, 1)
        return self.n

    def link(self, ins):
        self.step(ins)
        self.eng.wait_ge(self.sem, self.n)

    def after(self, n):
        self.eng.wait_ge(self.sem, n)


def build(nc, A, out, stop="", dbg=None):
    with ExitStack() as ctx:
        def sb(name, shape, dt=F32):
            return ctx.enter_context(nc.sbuf_tensor(name, shape, dt))

        def sem(name):
            return ctx.enter_context(nc.semaphore(name))

        def dram(name, shape):
            return nc.dram_tensor(name, shape, F32, kind="Internal").ap()

        bank = [ctx.enter_context(nc.psum_tensor(f"bank{i}", [P, 512], F32)) for i in range(8)]

        h_tok = dram("h_tok", (B * T, C))
        h_att = dram("h_att", (B * T, C))
        rel_scr = dram("rel_scr", (2, NT, P, PITCH))
        att_scr = dram("att_scr", (2, NT, P, PITCH))

        ident = sb("ident", [P, P])
        ident_b = sb("ident_b", [P, P], BF16)
        causal = sb("causal", [P, P], BF16)
        ones = sb("ones", [P, P])
        zeros = sb("zeros", [P, P])
        block_ones = sb("block_ones", [P, P])
        mhalf = sb("mhalf", [P, NT])
        low_mask = sb("low_mask", [P, NT, 192])

        wqk0 = sb("wqk0", [P, NC, 2 * MQ * P])
        wv0 = sb("wv0", [P, NC, C])
        wp0 = sb("wp0", [P, NC, C])
        bqk0 = sb("bqk0", [P, 2 * MQ])
        bv0 = sb("bv0", [P, C])
        bp0 = sb("bp0", [1, C])
        gamma = sb("gamma", [P, NC])
        beta = sb("beta", [P, NC])
        fc1 = sb("fc1", [P, NC, F0])
        fc2 = sb("fc2", [P, NF, C])
        fc1b = sb("fc1b", [P, NF])
        fc2b = sb("fc2b", [1, C])
        wqk1 = sb("wqk1", [P, NC, 2 * INNER])
        wv1 = sb("wv1", [P, NC, INNER])
        bqk1 = sb("bqk1", [P, 2 * (INNER // P)])
        bv1 = sb("bv1", [P, INNER])
        wo1 = sb("wo1", [P, INNER // P, C])
        bo1 = sb("bo1", [1, C])
        rel_k = sb("rel_k", [P, EXTN])
        rel_v = sb("rel_v", [P, D1])
        relv0 = sb("relv0", [P, D1])
        alphas = sb("alphas", [P, ORDER, H1])
        gate = sb("gate", [P, NC, E1])
        gate_b = sb("gate_b", [E1, 1])
        b1_all = sb("b1_all", [P, E1, NH])
        b2_all = sb("b2_all", [P, E1, NC])

        cur = sb("cur", [P, NT, C])
        stats = sb("stats", [P, NT, 6])
        meanvar = sb("meanvar", [P, NT, 2])
        vareps = sb("vareps", [P, NT])
        rstd = sb("rstd", [P, NT])
        xn = sb("xn", [P, NT, C])
        xn2 = sb("xn2", [P, NT, C])
        xnT = sb("xnT", [P, NC, T])

        s_load = sem("weights_loaded")
        s_const = sem("consts_ready")

        def bcast(ap, n=P):
            return ap.partition_broadcast(n)

        loads = [
            (wqk0[:, :, :], A["wqk0"].rearrange("(c p) n -> p c n", p=P)),
            (wv0[:, :, :], A["wv0"].rearrange("(c p) n -> p c n", p=P)),
            (wp0[:, :, :], A["wp0"].rearrange("(c p) n -> p c n", p=P)),
            (bqk0[:, :], A["bqk0"]),
            (bv0[:, :], bcast(A["bv0"])),
            (bp0[:, :], A["bp0"].rearrange("(a n) -> a n", a=1)),
            (gamma[:, :], A["gamma"]),
            (beta[:, :], A["beta"]),
            (fc1b[:, :], A["fc1b"]),
            (fc2b[:, :], A["fc2b"].rearrange("(a n) -> a n", a=1)),
            (wqk1[:, :, :], A["wqk1"].rearrange("(c p) n -> p c n", p=P)),
            (wv1[:, :, :], A["wv1"].rearrange("(c p) n -> p c n", p=P)),
            (bqk1[:, :], A["bqk1"]),
            (bv1[:, :], bcast(A["bv1"])),
            (wo1[:, :, :], A["wo1"].rearrange("(c p) n -> p c n", p=P)),
            (bo1[:, :], A["bo1"].rearrange("(a n) -> a n", a=1)),
            (rel_k[:, :], A["rel_k"]),
            (rel_v[:, :], A["rel_v"]),
            (relv0[:, :], bcast(A["relv0"])),
            (alphas[:, :, :], bcast(A["alphas"])),
            (gate[:, :, :], A["gate_w"].rearrange("(c p) n -> p c n", p=P)),
            (gate_b[:, :], A["gate_b"].rearrange("(a n) -> a n", n=1)),
            (b1_all[:, :, :], A["b1"]),
            (b2_all[:, :, :], A["b2"]),
        ]

        with ExitStack() as stage:
            def ssb(name, shape, dt=F32):
                return stage.enter_context(nc.sbuf_tensor(name, shape, dt))

            q1 = ssb("q1", [P, NC, F0], I32)
            q2 = ssb("q2", [P, NF, C], I32)
            sc1 = ssb("sc1", [P, NC, F0])
            sc2 = ssb("sc2", [P, NF, C])
            wdet = [None] + [ssb(f"wdet{j}", [P, 3, 3 * BR * C >> 2 * j]) for j in (1, 2, 3)]
            wapp = ssb("wapp", [P, BR * C >> 6])
            dbias = ssb("dbias", [P, 10])
            img = ssb("img", [P, 2, BR, C])
            lo = ssb("lo", [P, BR * C // 2])
            hi = ssb("hi", [P, BR * C // 2])
            app = [None] + [ssb(f"app{j}", [P, BR * C >> 2 * j]) for j in (1, 2, 3)]
            det = [None] + [ssb(f"det{j}", [P, 3, BR * C >> 2 * j]) for j in (1, 2, 3)]
            junk = ssb("junk", [P, 3 * BR * C // 4])
            dots = ssb("dots", [P, 10])
            logit = ssb("logit", [P, 10])
            top3 = ssb("top3", [P, 3])
            expo = ssb("expo", [P, 10])
            den = ssb("den", [P, 4])
            wts = ssb("wts", [P, 10])
            wpos = ssb("wpos", [P, 10])
            wneg = ssb("wneg", [P, 10])
            s_img = [sem(f"image_loaded{i}") for i in range(2)]
            s_dots = sem("dots_ready")
            s_sums = sem("dot_sums_ready")
            s_logit = sem("logits_ready")
            s_exp = sem("tok_exp_ready")
            s_rec = sem("image_rebuilt")
            s_saved = sem("image_saved")
            s_dve = sem("tok_vector_steps")
            s_q = sem("quantized_loaded")

            tok_loads = [
                (wdet[j][RB * i:RB * i + RB, :, :], A[f"wdet{j}"]) for j in (1, 2, 3) for i in range(IMGS)
            ] + [(wapp[RB * i:RB * i + RB, :], A["wapp"]) for i in range(IMGS)] + [
                (dbias[:, :], bcast(A["dbias"]))
            ]
            q_loads = [
                (q1[:, :, :], A["fc1_q"].rearrange("(c p) n -> p c n", p=P)),
                (q2[:, :, :], A["fc2_q"].rearrange("(c p) n -> p c n", p=P)),
                (sc1[:, :, :], bcast(A["fc1_s"])),
                (sc2[:, :, :], bcast(A["fc2_s"])),
            ]
            s_tokw = sem("tok_weights_loaded")

            block = stage.enter_context(nc.Block())

            @block.sync
            def _(sp):
                def load(g):
                    sp.dma_start(img[:, g % 2, :, :], A["x"][IMGS * g:IMGS * (g + 1)].rearrange(
                        "i (r k) c -> (i r) k c", k=BR)).then_inc(s_img[g % 2], 16)
                load(0)
                for dst, src in tok_loads:
                    sp.dma_start(dst, src).then_inc(s_tokw, 16)
                load(1)
                for dst, src in q_loads:
                    sp.dma_start(dst, src).then_inc(s_q, 16)
                for dst, src in loads:
                    sp.dma_start(dst, src).then_inc(s_load, 16)
                for g in range(GROUPS):
                    sp.wait_ge(s_rec, g + 1)
                    sp.dma_start(h_tok[g * IMGS * T:(g + 1) * IMGS * T, :].rearrange(
                        "(q k) c -> q k c", k=BR), img[:, g % 2, :, :]).then_inc(s_saved, 16)
                    if g + 2 < GROUPS:
                        sp.wait_ge(s_saved, 16 * (g + 1))
                        load(g + 2)
                sp.wait_ge(s_const, 3)
                for par in range(2):
                    for t in range(NT):
                        for off in (0, PITCH - MAXREL):
                            sp.dma_start(att_scr[par, t, :, off:off + MAXREL],
                                         zeros[:, 0:MAXREL]).then_inc(s_saved, 16)
                sp.wait_ge(s_saved, 16 * (GROUPS + 4 * NT))
                sp.wait_ge(s_load, 16 * len(loads))

            @block.gpsimd
            def _(pool):
                pool.memset(ident[:, :], 0.0).then_inc(s_const, 1)
                pool.memset(ones[:, :], 1.0).then_inc(s_const, 1)
                pool.memset(zeros[:, :], 0.0).then_inc(s_const, 1)
                pool.memset(block_ones[:, :], 0.0).then_inc(s_const, 1)
                pool.memset(mhalf[:, :], -0.5).then_inc(s_const, 1)
                pool.memset(causal[:, :], 0.0).then_inc(s_const, 1)
                pool.memset(low_mask[:, :, :], 1.0).then_inc(s_const, 1)
                pool.wait_ge(s_const, 7)
                pool.affine_select(out=ident[:, :], in_=ident[:, :], compare_op=ALU.not_equal, fill=1.0,
                                   base=0, pattern=[[-1, P]], channel_multiplier=1).then_inc(s_const, 1)
                pool.affine_select(out=causal[:, :], in_=causal[:, :], compare_op=ALU.is_ge, fill=NEG,
                                   base=0, pattern=[[-1, P]], channel_multiplier=1).then_inc(s_const, 1)
                for t in range(NT):
                    pool.affine_select(out=low_mask[:, t, :], in_=low_mask[:, t, :], compare_op=ALU.is_ge,
                                       fill=0.0, base=P * t - MAXREL, pattern=[[-1, 192]],
                                       channel_multiplier=1).then_inc(s_const, 1)
                for i in range(IMGS):
                    pool.wait_ge(s_const, 11 + i)
                    pool.memset(block_ones[RB * i:RB * (i + 1), RB * i:RB * (i + 1)], 1.0).then_inc(s_const, 1)
                pool.wait_ge(s_const, 15)
                pool.tensor_copy(ident_b[:, :], ident[:, :]).then_inc(s_const, 1)

            @block.tensor
            def _(pe):
                pe.wait_ge(s_const, 16)
                for g in range(GROUPS):
                    pe.wait_ge(s_dots, g + 1)
                    pe.matmul(bank[0][:, 0:10], block_ones[:, :], dots[:, :], start=True,
                              stop=True).then_inc(s_sums, 1)

            @block.scalar
            def _(act):
                for g in range(GROUPS):
                    act.wait_ge(s_logit, g + 1)
                    act.activation(expo[:, :], logit[:, :], ACT.Exp).then_inc(s_exp, 1)
                act.wait_ge(s_load, 16 * len(loads))
                flat = alphas[:, :, :].rearrange("p k h -> p (k h)")
                act.activation(flat, flat, ACT.Exp, scale=-1.0).then_inc(s_exp, 1)

            @block.vector
            def _(dve):
                ch = Chain(dve, s_dve)
                dve.wait_ge(s_tokw, 16 * len(tok_loads))
                for g in range(GROUPS):
                    dve.wait_ge(s_img[g % 2], 16 * (g // 2 + 1))
                    cur_a, rows, cols = img[:, g % 2, :, :].rearrange("p k c -> p (k c)"), BR, C
                    for j in (1, 2, 3):
                        n = rows * cols
                        pair = cur_a.rearrange("p (n e) -> p n e", e=2)
                        ch.step(dve.tensor_tensor(lo[:, 0:n // 2], pair[:, :, 0], pair[:, :, 1], ALU.add))
                        ch.link(dve.tensor_tensor(hi[:, 0:n // 2], pair[:, :, 0], pair[:, :, 1], ALU.subtract))
                        rows, cols = rows // 2, cols // 2
                        for src, dst_sum, dst_dif in ((lo, app[j][:, :], det[j][:, 0, :]),
                                                      (hi, det[j][:, 1, :], det[j][:, 2, :])):
                            v = src[:, 0:n // 2].rearrange("p (r e c) -> p r e c", e=2, c=cols)
                            for dst, op in ((dst_sum, ALU.add), (dst_dif, ALU.subtract)):
                                ch.step(dve.tensor_tensor(dst.rearrange("p (r c) -> p r c", c=cols),
                                                          v[:, :, 0, :], v[:, :, 1, :], op))
                        ch.after(ch.n)
                        cur_a = app[j][:, :]
                    for j in (1, 2, 3):
                        for o in range(3):
                            ch.link(dve.tensor_tensor_reduce(
                                junk[:, 0:3 * rows_of(j)], det[j][:, :, :].rearrange("p b n -> p (b n)"),
                                wdet[j][:, o, :], 0.5 ** j, 0.0, ALU.mult, ALU.add,
                                dots[:, 3 * (j - 1) + o:3 * (j - 1) + o + 1]))
                    dve.tensor_tensor_reduce(junk[:, 0:rows_of(3)], app[3][:, :], wapp[:, :], 0.125, 0.0,
                                             ALU.mult, ALU.add, dots[:, 9:10]).then_inc(s_dots, 1)
                    dve.wait_ge(s_sums, g + 1)
                    ch.link(dve.tensor_tensor(logit[:, :], bank[0][:, 0:10], dbias[:, :], ALU.add))
                    ch.link(dve.tensor_reduce(top3[:, :], logit[:, 0:9].rearrange("p (j o) -> p j o", o=3),
                                              AX.X, ALU.max))
                    ch.step(dve.tensor_tensor(logit[:, 0:9].rearrange("p (j o) -> p j o", o=3),
                                              logit[:, 0:9].rearrange("p (j o) -> p j o", o=3),
                                              top3[:, :].unsqueeze(2).to_broadcast([P, 3, 3]), ALU.subtract))
                    ch.link(dve.tensor_scalar(logit[:, 9:10], logit[:, 9:10], -1.0, None, ALU.mult))
                    dve.tensor_copy(top3[:, 0:1], logit[:, 9:10]).then_inc(s_logit, 1)
                    dve.wait_ge(s_exp, g + 1)
                    ch.step(dve.tensor_reduce(den[:, 0:3], expo[:, 0:9].rearrange("p (j o) -> p j o", o=3),
                                              AX.X, ALU.add))
                    ch.link(dve.tensor_scalar(den[:, 3:4], expo[:, 9:10], 1.0, None, ALU.add))
                    ch.link(dve.reciprocal(den[:, :], den[:, :]))
                    ch.step(dve.tensor_tensor(wts[:, 0:9].rearrange("p (j o) -> p j o", o=3),
                                              expo[:, 0:9].rearrange("p (j o) -> p j o", o=3),
                                              den[:, 0:3].unsqueeze(2).to_broadcast([P, 3, 3]), ALU.mult))
                    ch.link(dve.tensor_scalar(wts[:, 9:10], den[:, 3:4], 1.0, None, ALU.mult))
                    for j in (1, 2, 3):
                        for sign, dst in ((1.0, wpos), (-1.0, wneg)):
                            ch.step(dve.tensor_scalar(dst[:, 3 * (j - 1):3 * j], wts[:, 3 * (j - 1):3 * j],
                                                      sign * 0.25 ** j, None, ALU.mult))
                    ch.link(dve.tensor_scalar(wpos[:, 9:10], wts[:, 9:10], 0.25 ** 3, None, ALU.mult))
                    ch.link(dve.tensor_scalar(app[3][:, :], app[3][:, :], wpos[:, 9:10], None, ALU.mult))
                    for j in (3, 2, 1):
                        rows, cols = BR >> j, C >> j
                        a = app[j][:, :].rearrange("p (r c) -> p r c", c=cols)
                        w = [(wpos[:, 3 * (j - 1) + o:3 * (j - 1) + o + 1],
                              wneg[:, 3 * (j - 1) + o:3 * (j - 1) + o + 1]) for o in range(3)]
                        h, v, d = (det[j][:, o, :].rearrange("p (r c) -> p r c", c=cols) for o in range(3))
                        lov = lo[:, 0:2 * rows * cols].rearrange("p (r e c) -> p r e c", e=2, c=cols)
                        hiv = hi[:, 0:2 * rows * cols].rearrange("p (r e c) -> p r e c", e=2, c=cols)
                        ch.step(dve.tensor_scalar(v, v, w[1][0], None, ALU.mult))
                        for e in range(2):
                            ch.step(dve.scalar_tensor_tensor(out=lov[:, :, e, :], in0=h, scalar=w[0][e], in1=a,
                                                             op0=ALU.mult, op1=ALU.add))
                        ch.after(ch.n)
                        for e in range(2):
                            ch.step(dve.scalar_tensor_tensor(out=hiv[:, :, e, :], in0=d, scalar=w[2][e], in1=v,
                                                             op0=ALU.mult, op1=ALU.add))
                        ch.after(ch.n)
                        if j > 1:
                            up = app[j - 1][:, :].rearrange("p (n e) -> p n e", e=2)
                        else:
                            up = img[:, g % 2, :, :].rearrange("p k (c e) -> p (k c) e", e=2)
                        n = 2 * rows * cols
                        ch.step(dve.tensor_tensor(up[:, :, 0], lo[:, 0:n], hi[:, 0:n], ALU.add))
                        ins = dve.tensor_tensor(up[:, :, 1], lo[:, 0:n], hi[:, 0:n], ALU.subtract)
                        if j > 1:
                            ch.link(ins)
                    ins.then_inc(s_rec, 1)
                    dve.wait_ge(s_rec, g + 1)
                    ch.after(ch.n)
                dve.wait_ge(s_q, 16 * len(q_loads))
                for w, q, s in ((fc1, q1, sc1), (fc2, q2, sc2)):
                    ch.link(dve.tensor_scalar(w[:, :, :], q[:, :, :], -128.0, None, ALU.add))
                    ch.link(dve.tensor_tensor(w[:, :, :], w[:, :, :], s[:, :, :], ALU.mult))
                dve.wait_ge(s_load, 16 * len(loads))
                ch.link(dve.tensor_scalar(bqk0[:, 0:MQ], bqk0[:, 0:MQ], 1.0 / D0, None, ALU.mult))
                n1 = INNER // P
                ch.link(dve.tensor_scalar(bqk1[:, n1:2 * n1], bqk1[:, n1:2 * n1], D1 ** -0.5, None, ALU.mult))
                rv = bv1[:, :].rearrange("p (h d) -> p h d", d=D1)
                ch.step(dve.tensor_tensor(rv, rv, relv0[:, :].unsqueeze(1).to_broadcast([P, H1, D1]), ALU.add))
                ch.step(dve.tensor_tensor(rel_v[:, :], rel_v[:, :], relv0[:, :], ALU.subtract))
                dve.wait_ge(s_exp, GROUPS + 1)
                ch.link(dve.tensor_scalar(alphas[:, :, :], alphas[:, :, :], 1.0, None, ALU.add))
                ch.link(dve.reciprocal(alphas[:, :, :], alphas[:, :, :]))

        if stop == "tok":
            return finish_copy(nc, ctx, h_tok, out, sem)
        body = {}

        def bsem(name):
            body[name] = sem(name)
            return body[name]

        load_cur = bsem("cur_loaded")
        stats_ready = bsem("stats_ready")
        rstd_ready = bsem("rstd_ready")
        xn_ready = bsem("xn_ready")
        xnT_ps = bsem("xnT_in_psum")
        xnT_ready = bsem("xnT_ready")
        pool_steps = bsem("pool_steps")
        dve_steps = bsem("vector_steps")
        qk0_ps = bsem("qk0_in_psum")
        qk0_ready = bsem("qk0_ready")
        v0_ps = bsem("v0_in_psum")
        v0_ready = bsem("v0_ready")
        s0_ps = bsem("scores0_in_psum")
        max0_ready = bsem("rowmax0_ready")
        p0_ready = bsem("probs0_ready")
        pT0_ps = bsem("probsT0_in_psum")
        pT0_ready = bsem("probsT0_ready")
        o0_ps = bsem("heads0_in_psum")
        y0_ready = bsem("attended0_ready")
        yT0_ps = bsem("attendedT0_in_psum")
        yT0_ready = bsem("attendedT0_ready")
        r0_ps = bsem("projected0_in_psum")
        f1_ps = bsem("hidden_in_psum")
        f1_ready = bsem("hidden_ready")
        f2_ps = bsem("ffn_in_psum")
        v1_ps = bsem("v1_in_psum")
        v1_ready = bsem("v1_ready")
        qk1_ps = bsem("qk1_in_psum")
        qk1_ready = bsem("qk1_ready")
        rel_ps = bsem("rel_in_psum")
        rel_ready = bsem("rel_ready")
        rel_out = [bsem(f"rel_written{i}") for i in range(2)]
        rel_back = [bsem(f"rel_read{i}") for i in range(2)]
        s1_ps = bsem("scores1_in_psum")
        s1_ready = bsem("scores1_ready")
        max1_ready = bsem("rowmax1_ready")
        e1_ready = bsem("exp1_ready")
        p1_ready = bsem("probs1_ready")
        low_ready = bsem("low_clip_ready")
        att_out = [bsem(f"att_written{i}") for i in range(2)]
        att_back = [bsem(f"att_read{i}") for i in range(2)]
        pT1_ps = bsem("probsT1_in_psum")
        pT1_ready = bsem("probsT1_ready")
        wT_ps = bsem("bandT_in_psum")
        wT_ready = bsem("bandT_ready")
        av_ps = bsem("av_in_psum")
        av_ready = bsem("av_ready")
        mix_ready = bsem("orders_mixed")
        mT_ps = bsem("mixedT_in_psum")
        mT_ready = bsem("mixedT_ready")
        r1_ps = bsem("projected1_in_psum")
        cur_done = bsem("cur_final")
        cur_saved = bsem("cur_saved")
        lg_ps = bsem("gate_logits_in_psum")
        gmax_ready = bsem("gate_max_ready")
        gexp_ready = bsem("gate_exp_ready")
        g_ready = bsem("gates_ready")
        gT_ps = bsem("gatesT_in_psum")
        gT_ready = bsem("gatesT_ready")
        mg_ps = bsem("merged_in_psum")
        body_sems = sorted(s.num for s in body.values())
        assert body_sems == list(range(body_sems[0], body_sems[0] + len(body_sems)))
        arrived = sem("engines_at_turn_end")
        go = {n: sem(f"next_turn_{n}") for n in ("pool", "act", "dve", "pe")}

        merged = sb("merged", [P, NC, E1, B])
        gates = sb("gates", [E1, B, T])

        def turn_end(eng, name):
            eng.drain().then_inc(arrived, 1)
            eng.wait_ge(go[name], 1)
            eng.sem_clear(go[name])

        with ExitStack() as stage:
            def ssb(name, shape, dt=F32):
                return stage.enter_context(nc.sbuf_tensor(name, shape, dt))

            qkT0 = ssb("qkT0", [P, 2 * MQ, T])
            v0 = ssb("v0", [P, NT, C])
            nmax0 = ssb("nmax0", [P, 2, NT])
            sum0 = ssb("sum0", [P, NT, H0])
            rsum0 = ssb("rsum0", [P, NT, H0])
            probs0 = ssb("probs0", [P, 2, 3 * P])
            probsT0 = ssb("probsT0", [P, 2, 3 * P])
            y0 = ssb("y0", [P, NT, C])
            yT0 = ssb("yT0", [P, NC, T])
            hid = ssb("hid", [P, NF, T])
            qkT1 = ssb("qkT1", [P, 2, 2, T])
            v1 = ssb("v1", [P, NT, INNER])
            rel_sb = ssb("rel_sb", [P, 2, NT, PITCH])
            rel_in = ssb("rel_in", [P, 2, NT, T])
            scores = ssb("scores", [P, 2, NT, T])
            work = ssb("work", [P, NT, T])
            top = ssb("top", [P, 2, NT, ROUNDS, 8])
            nmax1 = ssb("nmax1", [P, 2, NT])
            probs1 = ssb("probs1", [P, 2, NT, T])
            sum1 = ssb("sum1", [P, 2, NT])
            rsum1 = ssb("rsum1", [P, 2, NT])
            band = ssb("band", [P, 2, NT, P])
            bandT = ssb("bandT", [P, 2, NT, P])
            probsT1 = ssb("probsT1", [P, 2, NT, T])
            av = ssb("av", [P, ORDER, NT, INNER])
            mixT = hid
            lg = ssb("lg", [E1, T])
            gsum = ssb("gsum", [E1, 4])
            top_g = ssb("top_g", [E1, 8])
            rest = ssb("rest", [E1, T])
            g_cur = ssb("g_cur", [E1, T])
            gT = ssb("gT", [P, NT, E1])

            block = stage.enter_context(nc.Block())

            def norm_stats(dve, ch, n, src, dst):
                for t in range(NT):
                    ch.step(dve.bn_stats(stats[:, t, :], src[:, t, :]))
                ch.after(ch.n)
                for t in range(NT):
                    ch.step(dve.bn_aggr(meanvar[:, t, :], stats[:, t, :]))
                ch.after(ch.n)
                dve.tensor_scalar(vareps[:, :], meanvar[:, :, 1], EPS, None, ALU.add).then_inc(stats_ready, 1)
                dve.wait_ge(rstd_ready, n + 1)
                for t in range(NT):
                    ins = dve.tensor_scalar(dst[:, t, :], src[:, t, :], meanvar[:, t, 0:1], rstd[:, t:t + 1],
                                            ALU.subtract, ALU.mult)
                    ins.then_inc(xn_ready, 1)
                dve.wait_ge(xn_ready, NT * (n + 1))

            def norm_rstd(pool, n):
                pool.wait_ge(stats_ready, n + 1)
                pool.tensor_tensor(rstd[:, :], vareps[:, :], mhalf[:, :], ALU.pow).then_inc(rstd_ready, 1)

            def norm_turn(pe, k, n, src):
                pe.wait_ge(xn_ready, NT * (n + 1))
                for c in range(NC):
                    for t in range(NT):
                        ins = pe.transpose(bank[0][:, c * T + t * P:c * T + (t + 1) * P],
                                           src[:, t, c * P:(c + 1) * P], ident[:, :])
                ins.then_inc(xnT_ps, 1)

            @block.sync
            def _(sp):
                with sp.Fori(0, B) as b:
                    sp.dma_start(cur[:, :, :], h_tok[bass.ds(b * T, T), :].rearrange("(t p) c -> p t c", p=P))\
                        .then_inc(load_cur, 16)

                    def rel_trip(h):
                        sp.wait_ge(rel_ready, h + 1)
                        if h >= 2:
                            sp.wait_ge(s1_ready, h - 1)
                        sp.dma_start(rel_scr[h % 2].rearrange("t p x -> p t x")[:, :, 0:EXTW],
                                     rel_sb[:, h % 2, :, 0:EXTW]).then_inc(rel_out[h % 2], 16)
                        sp.wait_ge(rel_out[h % 2], 16 * (h // 2 + 1))
                        sp.dma_start(rel_in[:, h % 2, :, :], skewed(rel_scr, h % 2, P - 1, -1, T))\
                            .then_inc(rel_back[h % 2], 16)

                    def att_trip(h):
                        sp.wait_ge(p1_ready, h + 1)
                        if h >= 2:
                            sp.wait_ge(att_back[h % 2], 16 * (h // 2))
                            sp.wait_ge(wT_ps, h - 1)
                        sp.dma_start(att_scr[h % 2].rearrange("t p x -> p t x")[:, :, MAXREL:MAXREL + T],
                                     probs1[:, h % 2, :, :]).then_inc(att_out[h % 2], 16)
                        sp.wait_ge(att_out[h % 2], 16 * (h // 2 + 1))
                        sp.dma_start(band[:, h % 2, :, 0:BAND], skewed(att_scr, h % 2, 1, 1, BAND, P))\
                            .then_inc(att_back[h % 2], 16)

                    rel_trip(0)
                    rel_trip(1)
                    for h in range(H1):
                        att_trip(h)
                        if h + 2 < H1:
                            rel_trip(h + 2)
                    sp.wait_ge(cur_done, 1)
                    sp.dma_start(h_att[bass.ds(b * T, T), :].rearrange("(t p) c -> p t c", p=P), cur[:, :, :])\
                        .then_inc(cur_saved, 16)
                    sp.wait_ge(cur_saved, 16)
                    sp.wait_ge(arrived, 4)
                    sp.sem_clear(range(body_sems[0], body_sems[-1] + 1))
                    sp.sem_clear(arrived)
                    for n in go:
                        sp.sem_inc(go[n], 1)

            @block.gpsimd
            def _(pool):
                with pool.Fori(0, B) as b:
                    for n in range(4):
                        norm_rstd(pool, n)
                    steps = 0
                    for g in range(H1 // 4):
                        pool.wait_ge(av_ready, ORDER * 4 * (g + 1))
                        part = [av[:, k, :, :].rearrange("p t (h d) -> p t h d", d=D1)[:, :, 4 * g:4 * g + 4, :]
                                for k in range(ORDER)]
                        for k in range(ORDER):
                            for t in range(NT):
                                al = alphas[:, k, 4 * g:4 * g + 4].unsqueeze(2).to_broadcast([P, 4, D1])
                                pool.tensor_tensor(part[k][:, t], part[k][:, t], al, ALU.mult)\
                                    .then_inc(pool_steps, 1)
                        steps += ORDER * NT
                        for k in range(1, ORDER):
                            pool.wait_ge(pool_steps, steps)
                            for t in range(NT):
                                pool.tensor_tensor(part[0][:, t], part[0][:, t], part[k][:, t], ALU.add)\
                                    .then_inc(mix_ready if k == ORDER - 1 else pool_steps, 1)
                            steps += NT if k < ORDER - 1 else 0
                    norm_rstd(pool, 4)
                    turn_end(pool, "pool")

            @block.tensor
            def _(pe):
                with pe.Fori(0, B) as b:
                    norm_turn(pe, 0, 0, xn)
                    pe.wait_ge(xnT_ready, 1)
                    for m in range(2 * MQ):
                        ps = bank[1 + m // 2][:, T * (m % 2):T * (m % 2 + 1)]
                        for c in range(NC):
                            ins = pe.matmul(ps, wqk0[:, c, m * P:(m + 1) * P], xnT[:, c, :],
                                            start=(c == 0), stop=(c == NC - 1))
                        if m % 2:
                            ins.then_inc(qk0_ps, 1)
                    for t in range(NT):
                        for c in range(NC):
                            ins = pe.matmul(bank[5][:, t * C:(t + 1) * C], xnT[:, c, t * P:(t + 1) * P],
                                            wv0[:, c, :], start=(c == 0), stop=(c == NC - 1))
                    ins.then_inc(v0_ps, 1)

                    def scores0(h):
                        m, at = h // HPM, SLOT * (h % HPM)
                        if h == 0:
                            pe.wait_ge(qk0_ready, MQ)
                        if h >= 2:
                            pe.wait_ge(p0_ready, h - 1)
                        ps = bank[6 + h % 2]
                        q = qkT0[at:at + D0, m, :]
                        k = qkT0[at:at + D0, MQ + m, :]
                        for col, tq, tk in ((0, 0, 0), (P, 1, 0), (2 * P, 1, 1)):
                            ins = pe.matmul(ps[:, col:col + P], q[:, tq * P:(tq + 1) * P],
                                            k[:, tk * P:(tk + 1) * P], start=True, stop=tq != tk)
                            if tq == tk:
                                ins = pe.matmul(ps[:, col:col + P], ident_b[:, :], causal[:, :],
                                                start=False, stop=True)
                        ins.then_inc(s0_ps, 1)

                    def attend0(h):
                        pe.wait_ge(p0_ready, h + 1)
                        if h >= 2:
                            pe.wait_ge(pT0_ready, h - 1)
                        if h < 2:
                            pe.wait_ge(qk0_ready, MQ)
                        for i in range(3):
                            ins = pe.transpose(bank[1 + h % 2][:, i * P:(i + 1) * P],
                                               probs0[:, h % 2, i * P:(i + 1) * P], ident[:, :])
                        ins.then_inc(pT0_ps, 1)
                        pe.wait_ge(pT0_ready, h + 1)
                        if h == 0:
                            pe.wait_ge(v0_ready, 1)
                        o = [bank[3][:, t * C + h * D0:t * C + (h + 1) * D0] for t in range(NT)]
                        v = [v0[:, t, h * D0:(h + 1) * D0] for t in range(NT)]
                        pT = probsT0[:, h % 2, :]
                        pe.matmul(o[0], pT[:, 0:P], v[0], start=True, stop=True)
                        pe.matmul(o[1], pT[:, P:2 * P], v[0], start=True, stop=False)
                        pe.matmul(o[1], pT[:, 2 * P:3 * P], v[1], start=False, stop=True).then_inc(o0_ps, 1)

                    scores0(0)
                    for h in range(H0):
                        if h + 1 < H0:
                            scores0(h + 1)
                        attend0(h)
                    pe.wait_ge(y0_ready, 1)
                    for c in range(NC):
                        for t in range(NT):
                            ins = pe.transpose(bank[0][:, c * T + t * P:c * T + (t + 1) * P],
                                               y0[:, t, c * P:(c + 1) * P], ident[:, :])
                    ins.then_inc(yT0_ps, 1)
                    pe.wait_ge(yT0_ready, 1)
                    for t in range(NT):
                        for c in range(NC):
                            pe.matmul(bank[4][:, t * C:(t + 1) * C], yT0[:, c, t * P:(t + 1) * P], wp0[:, c, :],
                                      start=(c == 0), stop=False)
                        ins = pe.matmul(bank[4][:, t * C:(t + 1) * C], ones[0:1, :], bp0[:, :],
                                        start=False, stop=True)
                    ins.then_inc(r0_ps, 1)

                    norm_turn(pe, 1, 2, xn2)
                    pe.wait_ge(xnT_ready, 2)
                    for f in range(NF):
                        ps = bank[1 + f // 2][:, T * (f % 2):T * (f % 2 + 1)]
                        for c in range(NC):
                            ins = pe.matmul(ps, fc1[:, c, f * P:(f + 1) * P], xnT[:, c, :],
                                            start=(c == 0), stop=(c == NC - 1))
                        if f % 2:
                            ins.then_inc(f1_ps, 1)
                    for t in range(NT):
                        for f in range(NF):
                            if t == 0:
                                pe.wait_ge(f1_ready, f + 1)
                            pe.matmul(bank[5][:, t * C:(t + 1) * C], hid[:, f, t * P:(t + 1) * P], fc2[:, f, :],
                                      start=(f == 0), stop=False)
                        ins = pe.matmul(bank[5][:, t * C:(t + 1) * C], ones[0:1, :], fc2b[:, :],
                                        start=False, stop=True)
                    ins.then_inc(f2_ps, 1)

                    norm_turn(pe, 2, 3, xn)
                    pe.wait_ge(xnT_ready, 3)

                    def qk1(j):
                        if j >= 1:
                            pe.wait_ge(qk1_ready, j)
                        for i in range(2):
                            for c in range(NC):
                                at = i * INNER + j * P
                                ins = pe.matmul(bank[0][:, i * T:(i + 1) * T], wqk1[:, c, at:at + P],
                                                xnT[:, c, :], start=(c == 0), stop=(c == NC - 1))
                        ins.then_inc(qk1_ps, 1)

                    def front1(h):
                        at = D1 * (h % 2)
                        pe.wait_ge(qk1_ready, h // 2 + 1)
                        q = qkT1[at:at + D1, (h // 2) % 2, 0, :]
                        k = qkT1[at:at + D1, (h // 2) % 2, 1, :]
                        if h >= 1:
                            pe.wait_ge(rel_ready, h)
                        for t in range(NT):
                            u = T - 1 - (P - 1) - P * t
                            ins = pe.matmul(bank[2 + t][:, 0:EXTW], q[:, t * P:(t + 1) * P],
                                            rel_k[at:at + D1, u:u + EXTW], start=True, stop=True)
                        ins.then_inc(rel_ps, 1)
                        if h >= 1:
                            pe.wait_ge(s1_ready, h)
                        for t in range(NT):
                            ins = pe.matmul(bank[1][:, t * T:(t + 1) * T], q[:, t * P:(t + 1) * P], k,
                                            start=True, stop=True)
                        ins.then_inc(s1_ps, 1)
                        if h % 2 and h + 1 < H1:
                            qk1((h + 1) // 2)

                    def back1(h):
                        pe.wait_ge(p1_ready, h + 1)
                        if h >= 1:
                            pe.wait_ge(pT1_ready, h)
                            pe.wait_ge(av_ready, ORDER * h)
                        else:
                            pe.wait_ge(v1_ready, 4)
                        for kc in range(NT):
                            for t in range(NT):
                                ins = pe.transpose(bank[4][:, kc * T + t * P:kc * T + (t + 1) * P],
                                                   probs1[:, h % 2, t, kc * P:(kc + 1) * P], ident[:, :])
                        ins.then_inc(pT1_ps, 1)
                        pe.wait_ge(att_back[h % 2], 16 * (h // 2 + 1))
                        pe.wait_ge(low_ready, h + 1)
                        for t in range(NT):
                            ins = pe.transpose(bank[5][:, t * P:(t + 1) * P], band[:, h % 2, t, :], ident[:, :])
                        ins.then_inc(wT_ps, 1)
                        pe.wait_ge(pT1_ready, h + 1)
                        pe.wait_ge(wT_ready, h + 1)
                        for k in range(ORDER):
                            if k:
                                pe.wait_ge(av_ready, ORDER * h + k)
                            for t in range(NT):
                                o = bank[6][:, (k * NT + t) * D1:(k * NT + t + 1) * D1]
                                for kc in range(NT):
                                    r = v1[:, kc, :] if k == 0 else av[:, k - 1, kc, :]
                                    ins = pe.matmul(o, probsT1[:, h % 2, kc, t * P:(t + 1) * P],
                                                    r[:, h * D1:(h + 1) * D1], start=(kc == 0),
                                                    stop=(k > 0 and kc == NT - 1))
                                if k == 0:
                                    ins = pe.matmul(o, bandT[:, h % 2, t, :], rel_v[:, :], start=False, stop=True)
                            ins.then_inc(av_ps, 1)

                    qk1(0)
                    for i in range(4):
                        t, half = i // 2, i % 2
                        for c in range(NC):
                            ins = pe.matmul(bank[4 + i][:, :], xnT[:, c, t * P:(t + 1) * P],
                                            wv1[:, c, half * 512:(half + 1) * 512],
                                            start=(c == 0), stop=(c == NC - 1))
                        ins.then_inc(v1_ps, 1)
                    front1(0)
                    front1(1)
                    for h in range(H1):
                        back1(h)
                        if h + 2 < H1:
                            front1(h + 2)
                    pe.wait_ge(mix_ready, NT * (H1 // 4))
                    for i in range(4):
                        for j in range(2):
                            for t in range(NT):
                                at = (2 * i + j) * P
                                ins = pe.transpose(bank[1 + i][:, j * T + t * P:j * T + (t + 1) * P],
                                                   av[:, 0, t, at:at + P], ident[:, :])
                        ins.then_inc(mT_ps, 1)
                    for t in range(NT):
                        for j in range(INNER // P):
                            if t == 0:
                                pe.wait_ge(mT_ready, j // 2 + 1)
                            pe.matmul(bank[7][:, t * C:(t + 1) * C], mixT[:, j, t * P:(t + 1) * P], wo1[:, j, :],
                                      start=(j == 0), stop=False)
                        ins = pe.matmul(bank[7][:, t * C:(t + 1) * C], ones[0:1, :], bo1[:, :],
                                        start=False, stop=True)
                    ins.then_inc(r1_ps, 1)

                    norm_turn(pe, 3, 4, xn)
                    pe.wait_ge(xnT_ready, 4)
                    for c in range(NC):
                        ins = pe.matmul(bank[1][0:E1, 0:T], gate[:, c, :], xnT[:, c, :],
                                        start=(c == 0), stop=(c == NC - 1))
                    ins.then_inc(lg_ps, 1)
                    pe.wait_ge(g_ready, 1)
                    for t in range(NT):
                        ins = pe.transpose(bank[2][:, t * E1:(t + 1) * E1], g_cur[:, t * P:(t + 1) * P],
                                           ident[0:E1, 0:E1])
                    ins.then_inc(gT_ps, 1)
                    pe.wait_ge(gT_ready, 1)
                    for c in range(NC):
                        for t in range(NT):
                            ins = pe.matmul(bank[3][:, c * E1:(c + 1) * E1], xn[:, t, c * P:(c + 1) * P],
                                            gT[:, t, :], start=(t == 0), stop=(t == NT - 1))
                    ins.then_inc(mg_ps, 1)
                    turn_end(pe, "pe")

            @block.scalar
            def _(act):
                with act.Fori(0, B) as b:
                    def turned(k, scaled=False):
                        act.wait_ge(xnT_ps, k + 1)
                        if scaled:
                            for c in range(NC):
                                ins = act.activation(xnT[:, c, :], bank[0][:, c * T:(c + 1) * T], ACT.Identity,
                                                     bias=beta[:, c:c + 1], scale=gamma[:, c:c + 1])
                        else:
                            ins = act.activation(xnT[:, :, :].rearrange("p c t -> p (c t)"), bank[0][:, :],
                                                 ACT.Copy)
                        ins.then_inc(xnT_ready, 1)

                    turned(0)
                    for m in range(2 * MQ):
                        act.wait_ge(qk0_ps, m // 2 + 1)
                        ins = act.activation(qkT0[:, m, :], bank[1 + m // 2][:, T * (m % 2):T * (m % 2 + 1)],
                                             ACT.Identity, bias=bqk0[:, m:m + 1],
                                             scale=1.0 / D0 if m < MQ else 1.0)
                        if m % 2:
                            ins.then_inc(qk0_ready, 1)
                    for h in range(H0):
                        act.wait_ge(max0_ready, h + 1)
                        if h >= 2:
                            act.wait_ge(pT0_ps, h - 1)
                        ps = bank[6 + h % 2]
                        for t, a, z in ((0, 0, P), (1, P, 3 * P)):
                            ins = act.activation(probs0[:, h % 2, a:z], ps[:, a:z], ACT.Exp,
                                                 bias=nmax0[:, h % 2, t:t + 1], accum_out=sum0[:, t, h:h + 1])
                        ins.then_inc(p0_ready, 1)
                    act.wait_ge(yT0_ps, 1)
                    act.activation(yT0[:, :, :].rearrange("p c t -> p (c t)"), bank[0][:, :], ACT.Copy)\
                        .then_inc(yT0_ready, 1)

                    turned(1, True)
                    for f in range(NF):
                        act.wait_ge(f1_ps, f // 2 + 1)
                        act.activation(hid[:, f, :], bank[1 + f // 2][:, T * (f % 2):T * (f % 2 + 1)],
                                       ACT.Silu, bias=fc1b[:, f:f + 1]).then_inc(f1_ready, 1)

                    turned(2)

                    def qk_out(j):
                        act.wait_ge(qk1_ps, j + 1)
                        if j >= 2:
                            act.wait_ge(s1_ps, 2 * j - 2)
                        for i in range(2):
                            n = i * (INNER // P) + j
                            ins = act.activation(qkT1[:, j % 2, i, :], bank[0][:, i * T:(i + 1) * T],
                                                 ACT.Identity, bias=bqk1[:, n:n + 1],
                                                 scale=1.0 if i == 0 else D1 ** -0.5)
                        ins.then_inc(qk1_ready, 1)

                    def front_out(h):
                        act.wait_ge(rel_ps, h + 1)
                        if h >= 2:
                            act.wait_ge(rel_out[h % 2], 16 * (h // 2))
                        for t in range(NT):
                            ins = act.activation(rel_sb[:, h % 2, t, 0:EXTW], bank[2 + t][:, 0:EXTW], ACT.Copy)
                        ins.then_inc(rel_ready, 1)
                        if h % 2 and h + 1 < H1:
                            qk_out((h + 1) // 2)

                    def exp_out(h):
                        act.wait_ge(max1_ready, h + 1)
                        if h >= 2:
                            act.wait_ge(pT1_ps, h - 1)
                            act.wait_ge(att_out[h % 2], 16 * (h // 2))
                        for t in range(NT):
                            ins = act.activation(probs1[:, h % 2, t, :], scores[:, h % 2, t, :], ACT.Exp,
                                                 bias=nmax1[:, h % 2, t:t + 1])
                        ins.then_inc(e1_ready, 1)

                    def back_out(h):
                        act.wait_ge(pT1_ps, h + 1)
                        act.activation(probsT1[:, h % 2, :, :].rearrange("p k t -> p (k t)"), bank[4][:, :],
                                       ACT.Copy).then_inc(pT1_ready, 1)
                        act.wait_ge(wT_ps, h + 1)
                        act.activation(bandT[:, h % 2, :, :].rearrange("p t q -> p (t q)"), bank[5][:, 0:NT * P],
                                       ACT.Copy).then_inc(wT_ready, 1)
                        for k in range(ORDER):
                            act.wait_ge(av_ps, ORDER * h + k + 1)
                            for t in range(NT):
                                at = (k * NT + t) * D1
                                ins = act.activation(av[:, k, t, h * D1:(h + 1) * D1], bank[6][:, at:at + D1],
                                                     ACT.Copy, scale=rsum1[:, h % 2, t:t + 1])
                            ins.then_inc(av_ready, 1)

                    qk_out(0)
                    front_out(0)
                    front_out(1)
                    exp_out(0)
                    for h in range(H1):
                        if h + 1 < H1:
                            exp_out(h + 1)
                        back_out(h)
                        if h + 2 < H1:
                            front_out(h + 2)
                    for i in range(4):
                        act.wait_ge(mT_ps, i + 1)
                        act.activation(mixT[:, 2 * i:2 * i + 2, :].rearrange("p j t -> p (j t)"), bank[1 + i][:, :],
                                       ACT.Copy).then_inc(mT_ready, 1)

                    turned(3)
                    act.wait_ge(gmax_ready, 1)
                    act.activation(lg[:, :], lg[:, :], ACT.Exp, bias=gsum[:, 0:1], accum_out=gsum[:, 1:2])\
                        .then_inc(gexp_ready, 1)
                    act.wait_ge(gT_ps, 1)
                    act.activation(gT[:, :, :].rearrange("p t e -> p (t e)"), bank[2][:, 0:NT * E1], ACT.Copy)\
                        .then_inc(gT_ready, 1)
                    turn_end(act, "act")

            @block.vector
            def _(dve):
                with dve.Fori(0, B) as b:
                    ch = Chain(dve, dve_steps)
                    dve.wait_ge(load_cur, 16)
                    norm_stats(dve, ch, 0, cur, xn)
                    dve.wait_ge(v0_ps, 1)
                    for t in range(NT):
                        ins = dve.tensor_tensor(v0[:, t, :], bank[5][:, t * C:(t + 1) * C], bv0[:, :], ALU.add)
                    ins.then_inc(v0_ready, 1)

                    def rowmax0(h):
                        dve.wait_ge(s0_ps, h + 1)
                        if h >= 2:
                            dve.wait_ge(p0_ready, h - 1)
                        for t, a, z in ((0, 0, P), (1, P, 3 * P)):
                            ins = dve.tensor_reduce(nmax0[:, h % 2, t:t + 1], bank[6 + h % 2][:, a:z], AX.X,
                                                    ALU.max, negate=True)
                        ins.then_inc(max0_ready, 1)

                    rowmax0(0)
                    for h in range(H0):
                        if h + 1 < H0:
                            rowmax0(h + 1)
                        dve.wait_ge(pT0_ps, h + 1)
                        if h >= 2:
                            dve.wait_ge(o0_ps, h - 1)
                        dve.tensor_copy(probsT0[:, h % 2, :], bank[1 + h % 2][:, 0:3 * P]).then_inc(pT0_ready, 1)
                    dve.wait_ge(p0_ready, H0)
                    ch.link(dve.reciprocal(rsum0[:, :, :], sum0[:, :, :]))
                    dve.wait_ge(o0_ps, H0)
                    for t in range(NT):
                        ins = dve.tensor_tensor(
                            y0[:, t, :].rearrange("p (h d) -> p h d", d=D0),
                            bank[3][:, t * C:(t + 1) * C].rearrange("p (h d) -> p h d", d=D0),
                            rsum0[:, t, :].unsqueeze(2).to_broadcast([P, H0, D0]), ALU.mult)
                    ins.then_inc(y0_ready, 1)
                    dve.wait_ge(r0_ps, 1)
                    flat = cur[:, :, :].rearrange("p t c -> p (t c)")
                    ch.link(dve.tensor_tensor(flat, flat, bank[4][:, :], ALU.add))

                    norm_stats(dve, ch, 1, cur, xn)
                    norm_stats(dve, ch, 2, xn, xn2)
                    ch.link(dve.tensor_tensor(flat, flat, xn[:, :, :].rearrange("p t c -> p (t c)"), ALU.add))
                    dve.wait_ge(f2_ps, 1)
                    ch.link(dve.scalar_tensor_tensor(out=flat, in0=bank[5][:, :], scalar=0.5, in1=flat,
                                                     op0=ALU.mult, op1=ALU.add))

                    norm_stats(dve, ch, 3, cur, xn)
                    for i in range(4):
                        t, half = i // 2, i % 2
                        dve.wait_ge(v1_ps, i + 1)
                        dve.tensor_tensor(v1[:, t, half * 512:(half + 1) * 512], bank[4 + i][:, :],
                                          bv1[:, half * 512:(half + 1) * 512], ALU.add).then_inc(v1_ready, 1)

                    def add_rel(h):
                        dve.wait_ge(s1_ps, h + 1)
                        dve.wait_ge(rel_back[h % 2], 16 * (h // 2 + 1))
                        if h >= 2:
                            dve.wait_ge(e1_ready, h - 1)
                        dve.tensor_tensor(scores[:, h % 2, :, :].rearrange("p t k -> p (t k)"), bank[1][:, :],
                                          rel_in[:, h % 2, :, :].rearrange("p t k -> p (t k)"), ALU.add)\
                            .then_inc(s1_ready, 1)

                    def threshold(h):
                        dve.wait_ge(s1_ready, h + 1)
                        if h >= 2:
                            dve.wait_ge(e1_ready, h - 1)
                        for r in range(ROUNDS):
                            for t in range(NT):
                                src = scores[:, h % 2, t, :] if r == 0 else work[:, t, :]
                                if r:
                                    ch.after(ch.n - 1)
                                ch.step(dve.max(top[:, h % 2, t, r, :], src))
                            if r == 0:
                                ch.after(ch.n)
                                dve.tensor_scalar(nmax1[:, h % 2, :], top[:, h % 2, :, 0, 0], -1.0, None,
                                                  ALU.mult).then_inc(max1_ready, 1)
                            if r < ROUNDS - 1:
                                for t in range(NT):
                                    src = scores[:, h % 2, t, :] if r == 0 else work[:, t, :]
                                    ch.after(ch.n - 1)
                                    ch.step(dve.match_replace(work[:, t, :], top[:, h % 2, t, r, :], src, NEG))

                    def select(h):
                        dve.wait_ge(e1_ready, h + 1)
                        ch.after(ch.n)
                        for t in range(NT):
                            ins = dve.scalar_tensor_tensor(
                                out=probs1[:, h % 2, t, :], in0=scores[:, h % 2, t, :],
                                scalar=top[:, h % 2, t, ROUNDS - 1, 7:8], in1=probs1[:, h % 2, t, :],
                                op0=ALU.is_ge, op1=ALU.mult, accum_out=sum1[:, h % 2, t:t + 1])
                        ins.then_inc(p1_ready, 1)
                        dve.wait_ge(p1_ready, h + 1)
                        if h >= 2:
                            dve.wait_ge(av_ready, ORDER * (h - 1))
                        ch.link(dve.reciprocal(rsum1[:, h % 2, :], sum1[:, h % 2, :]))
                        if h >= 2:
                            dve.wait_ge(wT_ps, h - 1)
                        for t in range(NT):
                            n = MAXREL + P * t
                            ins = dve.tensor_tensor_reduce(
                                work[:, t, 0:n], probs1[:, h % 2, t, 0:n], low_mask[:, t, 0:n], 1.0, 0.0,
                                ALU.mult, ALU.add, band[:, h % 2, t, BAND:P])
                        ins.then_inc(low_ready, 1)
                        dve.wait_ge(low_ready, h + 1)

                    add_rel(0)
                    for h in range(H1):
                        threshold(h)
                        if h + 1 < H1:
                            add_rel(h + 1)
                        select(h)
                    dve.wait_ge(r1_ps, 1)
                    dve.tensor_tensor(flat, flat, bank[7][:, :], ALU.add).then_inc(cur_done, 1)
                    dve.wait_ge(cur_done, 1)

                    norm_stats(dve, ch, 4, cur, xn)
                    dve.wait_ge(lg_ps, 1)
                    ch.link(dve.tensor_scalar(lg[:, :], bank[1][0:E1, 0:T], gate_b[:, :], None, ALU.add))
                    dve.tensor_reduce(gsum[:, 0:1], lg[:, :], AX.X, ALU.max, negate=True).then_inc(gmax_ready, 1)
                    dve.wait_ge(gexp_ready, 1)
                    ch.link(dve.reciprocal(gsum[:, 2:3], gsum[:, 1:2]))
                    ch.link(dve.tensor_scalar(lg[:, :], lg[:, :], gsum[:, 2:3], None, ALU.mult))
                    ch.link(dve.max(top_g[:, :], lg[:, :]))
                    ch.link(dve.match_replace(rest[:, :], top_g[:, :], lg[:, :], 0.0))
                    dve.tensor_tensor(g_cur[:, :], lg[:, :], rest[:, :], ALU.subtract).then_inc(g_ready, 1)
                    dve.wait_ge(g_ready, 1)
                    dve.tensor_copy(gates[:, bass.ds(b, 1), :].rearrange("e b t -> e (b t)"), g_cur[:, :])
                    dve.wait_ge(mg_ps, 1)
                    dve.tensor_copy(merged[:, :, :, bass.ds(b, 1)].rearrange("p c e b -> p (c e) b"),
                                    bank[3][:, 0:NC * E1].rearrange("p (n b) -> p n b", b=1))
                    turn_end(dve, "dve")

        if stop in ("att0", "ffn0", "att1"):
            return finish_copy(nc, ctx, h_att, out, sem)

        expert_out = sb("expert_out", [P, NC, B, E1])
        with ExitStack() as stage:
            def ssb(name, shape, dt=F32):
                return stage.enter_context(nc.sbuf_tensor(name, shape, dt))

            w1 = [ssb(f"w1_{i}", [P, NC, HID]) for i in range(WBUFS)]
            w2 = [ssb(f"w2_{i}", [P, NH, C]) for i in range(WBUFS)]
            act_in = ssb("act_in", [P, 2, NH, B])
            act_out = ssb("act_out", [P, 2, NH, B])
            ex_cur = ssb("ex_cur", [P, 2, NC, E1])
            tokens = ssb("tokens", [P, 4, NT, C])
            o_b = ssb("o_b", [E1, 2, C])
            w1_loaded = [sem(f"w1_loaded{i}") for i in range(WBUFS)]
            w2_loaded = [sem(f"w2_loaded{i}") for i in range(WBUFS)]
            up_ps = sem("expert_hidden_in_psum")
            biased = sem("expert_hidden_biased")
            gelu_ready = sem("expert_hidden_ready")
            down_ps = sem("expert_out_in_psum")
            down_ready = sem("expert_out_ready")
            tok_loaded = [sem(f"tokens_loaded{i}") for i in range(4)]
            picked = sem("outputs_picked")
            ot_ps = sem("outputsT_in_psum")
            ot_ready = sem("outputsT_ready")
            sc_ps = sem("scattered_in_psum")
            sum_ready = sem("tokens_ready")
            saved = sem("tokens_saved")
            TURNS = E1 // WBUFS

            block = stage.enter_context(nc.Block())

            @block.sync
            def _(sp):
                def load_up(j, e):
                    sp.dma_start(w1[j][:, :, :], A["w1"][bass.ds(e, 1), 0:C, :].rearrange(
                        "e (c p) n -> p (e c) n", p=P)).then_inc(w1_loaded[j], 16)

                def load_down(j, e):
                    sp.dma_start(w2[j][:, :, :], A["w2"][bass.ds(e, 1), 0:HID, :].rearrange(
                        "e (c p) n -> p (e c) n", p=P)).then_inc(w2_loaded[j], 16)

                for j in range(WBUFS):
                    load_up(j, j)
                    load_down(j, j)
                with sp.Fori(0, TURNS - 1) as i:
                    for j in range(WBUFS):
                        sp.wait_ge(up_ps, i * WBUFS + j + 1)
                        load_up(j, (i + 1) * WBUFS + j)
                        sp.wait_ge(down_ps, i * WBUFS + j + 1)
                        load_down(j, (i + 1) * WBUFS + j)

                def load_tokens(b):
                    sp.dma_start(tokens[:, b % 4, :, :], h_att[b * T:(b + 1) * T, :].rearrange(
                        "(t p) c -> p t c", p=P)).then_inc(tok_loaded[b % 4], 16)
                for b in range(4):
                    load_tokens(b)
                for b in range(B):
                    sp.wait_ge(sum_ready, b + 1)
                    sp.dma_start(out[b].rearrange("(t p) c -> p t c", p=P), tokens[:, b % 4, :, :])\
                        .then_inc(saved, 16)
                    if b + 4 < B:
                        sp.wait_ge(saved, 16 * (b + 1))
                        load_tokens(b + 4)
                sp.wait_ge(saved, 16 * B)

            @block.tensor
            def _(pe):
                with pe.Fori(0, TURNS) as i:
                    def up(j):
                        e = i * WBUFS + j
                        pe.wait_ge(w1_loaded[j], i * 16 + 16)
                        if j >= 2:
                            pe.wait_ge(biased, i * WBUFS + j - 1)
                        for k in range(NH):
                            for c in range(NC):
                                ins = pe.matmul(bank[j % 2][:, k * B:(k + 1) * B], w1[j][:, c, k * P:(k + 1) * P],
                                                merged[:, c, bass.ds(e, 1), :].rearrange("p e b -> p (e b)"),
                                                start=(c == 0), stop=(c == NC - 1))
                        ins.then_inc(up_ps, 1)

                    def down(j):
                        pe.wait_ge(gelu_ready, i * WBUFS + j + 1)
                        pe.wait_ge(w2_loaded[j], i * 16 + 16)
                        if j >= 2:
                            pe.wait_ge(down_ready, i * WBUFS + j - 1)
                        for c in range(NC):
                            for k in range(NH):
                                ins = pe.matmul(bank[2 + j % 2][:, c * B:(c + 1) * B],
                                                w2[j][:, k, c * P:(c + 1) * P], act_out[:, j % 2, k, :],
                                                start=(k == 0), stop=(k == NH - 1))
                        ins.then_inc(down_ps, 1)

                    up(0)
                    for j in range(WBUFS):
                        if j + 1 < WBUFS:
                            up(j + 1)
                        down(j)
                    pe.wait_ge(down_ready, (i + 1) * WBUFS)
                for b in range(B):
                    pe.wait_ge(picked, b + 1)
                    for c in range(NC):
                        ins = pe.transpose(bank[4 + b % 2][0:E1, c * P:(c + 1) * P], ex_cur[:, b % 2, c, :],
                                           ident[:, :])
                    ins.then_inc(ot_ps, 1)
                    pe.wait_ge(ot_ready, b + 1)
                    if b >= 2:
                        pe.wait_ge(sum_ready, b - 1)
                    for t in range(NT):
                        ins = pe.matmul(bank[6 + b % 2][:, t * C:(t + 1) * C], gates[:, b, t * P:(t + 1) * P],
                                        o_b[:, b % 2, :], start=True, stop=True)
                    ins.then_inc(sc_ps, 1)

            @block.vector
            def _(dve):
                with dve.Fori(0, TURNS) as i:
                    def bias_up(j):
                        e = i * WBUFS + j
                        dve.wait_ge(up_ps, e + 1)
                        if j >= 2:
                            dve.wait_ge(gelu_ready, i * WBUFS + j - 1)
                        dve.tensor_tensor(act_in[:, j % 2, :, :],
                                          bank[j % 2][:, 0:NH * B].rearrange("p (k b) -> p k b", b=B),
                                          b1_all[:, bass.ds(e, 1), :].rearrange("p e k -> p (e k)")
                                          .unsqueeze(2).to_broadcast([P, NH, B]), ALU.add).then_inc(biased, 1)

                    bias_up(0)
                    for j in range(WBUFS):
                        e = i * WBUFS + j
                        if j + 1 < WBUFS:
                            bias_up(j + 1)
                        dve.wait_ge(down_ps, e + 1)
                        dve.tensor_tensor(
                            expert_out[:, :, :, bass.ds(e, 1)].rearrange("p c b e -> p c (b e)"),
                            bank[2 + j % 2][:, 0:NC * B].rearrange("p (c b) -> p c b", b=B),
                            b2_all[:, bass.ds(e, 1), :].rearrange("p e c -> p (e c)")
                            .unsqueeze(2).to_broadcast([P, NC, B]), ALU.add).then_inc(down_ready, 1)
                    dve.wait_ge(gelu_ready, (i + 1) * WBUFS)
                dve.wait_ge(down_ready, E1)
                for b in range(B + 1):
                    if b < B:
                        if b >= 2:
                            dve.wait_ge(ot_ps, b - 1)
                        dve.tensor_copy(ex_cur[:, b % 2, :, :], expert_out[:, :, b, :]).then_inc(picked, 1)
                    if b >= 1:
                        a = b - 1
                        dve.wait_ge(sc_ps, a + 1)
                        dve.wait_ge(tok_loaded[a % 4], 16 * (a // 4 + 1))
                        flat = tokens[:, a % 4, :, :].rearrange("p t c -> p (t c)")
                        dve.tensor_tensor(flat, flat, bank[6 + a % 2][:, :], ALU.add).then_inc(sum_ready, 1)

            @block.scalar
            def _(act):
                with act.Fori(0, TURNS) as i:
                    for j in range(WBUFS):
                        act.wait_ge(biased, i * WBUFS + j + 1)
                        if j >= 2:
                            act.wait_ge(down_ps, i * WBUFS + j - 1)
                        act.activation(act_out[:, j % 2, :, :].rearrange("p k b -> p (k b)"),
                                       act_in[:, j % 2, :, :].rearrange("p k b -> p (k b)"), ACT.Gelu)\
                            .then_inc(gelu_ready, 1)
                    act.wait_ge(down_ps, (i + 1) * WBUFS)
                for b in range(B):
                    act.wait_ge(ot_ps, b + 1)
                    if b >= 2:
                        act.wait_ge(sc_ps, b - 1)
                    act.activation(o_b[:, b % 2, :], bank[4 + b % 2][0:E1, 0:C], ACT.Copy).then_inc(ot_ready, 1)


def rows_of(j):
    return BR * C >> 2 * j


def skewed(scr, half, col, step, n, tile_step=0):
    a = scr[half].rearrange("t p x -> p t x")
    return bass.AP(tensor=a.tensor, offset=a.offset + col,
                   ap=[[PITCH + step, P], [P * PITCH + tile_step, NT], [1, n]])


def finish_copy(nc, ctx, src, out, sem):
    s = sem("copied")
    with nc.Block() as block:
        @block.sync
        def _(sp):
            sp.dma_start(out.rearrange("b t c -> (b t) c"), src).then_inc(s, 16)
            sp.wait_ge(s, 16)


def layout(inputs):
    import numpy as np
    f = {k: np.asarray(v) for k, v in inputs.items()}
    a = {}
    a["x"] = f["x"][..., 0]
    for j, name, n in ((1, "Wd3", BR // 2), (2, "Wd2", BR // 4), (3, "Wd1", BR // 8)):
        w = f["L0_tok_" + name].reshape(3, RB, n, C >> j, 3)
        a[f"wdet{j}"] = np.ascontiguousarray(w.transpose(1, 4, 0, 2, 3)).reshape(RB, 3, -1)
    a["wapp"] = f["L0_tok_Wa"].reshape(RB, C >> 3)
    a["dbias"] = np.concatenate([f["L0_tok_bd3"], f["L0_tok_bd2"], f["L0_tok_bd1"], f["L0_tok_ba"]])
    w, b = f["L0_attn_W_attn"], f["L0_attn_b_attn"]
    wqk = np.zeros((C, 2 * MQ * HPM, SLOT), w.dtype)
    wqk[:, :, :D0] = w[:2 * C].T.reshape(C, 2 * H0, D0)
    a["wqk0"] = wqk.reshape(C, -1)
    bqk = np.zeros((2 * H0, SLOT), b.dtype)
    bqk[:, :D0] = b[:2 * C].reshape(2 * H0, D0)
    a["bqk0"] = np.ascontiguousarray(bqk.reshape(2 * MQ, P).T)
    a["wv0"] = np.ascontiguousarray(w[2 * C:].T)
    a["bv0"] = b[2 * C:]
    a["wp0"] = np.ascontiguousarray(f["L0_attn_W_proj"].T)
    a["bp0"] = f["L0_attn_b_proj"]
    a["gamma"] = np.ascontiguousarray(f["L0_ffn_ln_gamma"].reshape(NC, P).T)
    a["beta"] = np.ascontiguousarray(f["L0_ffn_ln_beta"].reshape(NC, P).T)
    a["fc1_q"] = f["L0_ffn_fc1_q"]
    a["fc2_q"] = f["L0_ffn_fc2_q"]
    a["fc1_s"] = f["L0_ffn_fc1_scales"]
    a["fc2_s"] = f["L0_ffn_fc2_scales"]
    a["fc1b"] = np.ascontiguousarray(f["L0_ffn_fc1_bias"].reshape(NF, P).T)
    a["fc2b"] = f["L0_ffn_fc2_bias"]
    w, b = f["L1_attn_Wqkv"], f["L1_attn_bqkv"]
    a["wqk1"] = np.ascontiguousarray(w[:2 * INNER].T)
    a["bqk1"] = np.ascontiguousarray(b[:2 * INNER].reshape(-1, P).T)
    a["wv1"] = np.ascontiguousarray(w[2 * INNER:].T)
    a["bv1"] = b[2 * INNER:]
    a["wo1"] = np.ascontiguousarray(f["L1_attn_Wout"].T)
    a["bo1"] = f["L1_attn_bout"]
    at = np.clip(-(np.arange(EXTN) - (T - 1)), -MAXREL, MAXREL) + MAXREL
    a["rel_k"] = np.ascontiguousarray(np.concatenate([f["L1_attn_rel_k_emb"][at].T] * 2))
    a["rel_v"] = f["L1_attn_rel_v_emb"][np.concatenate([2 * MAXREL - 1 - np.arange(BAND), [2 * MAXREL]])]
    a["relv0"] = f["L1_attn_rel_v_emb"][0]
    a["alphas"] = f["L1_attn_alphas_raw"]
    a["gate_w"] = np.ascontiguousarray(f["L1_ffn_gate_w"].T)
    a["gate_b"] = f["L1_ffn_gate_b"]
    w1, w2 = f["L1_ffn_w1"], f["L1_ffn_w2"]
    a["w1"] = w1
    a["w2"] = w2
    a["b1"] = np.ascontiguousarray(w1[:, C].reshape(E1, NH, P).transpose(2, 0, 1))
    a["b2"] = np.ascontiguousarray(w2[:, HID].reshape(E1, NC, P).transpose(2, 0, 1))
    return {k: np.ascontiguousarray(v) for k, v in a.items()}


def kernel(**inputs):
    import numpy as _np
    import concourse.bacc as _bacc
    from concourse import mybir as _mybir
    from concourse.bass_utils import run_bass_kernel_spmd as _run

    nc = _bacc.Bacc("TRN2", target_bir_lowering=False, num_devices=1)
    arrays = {f"in_{k}": v for k, v in layout(inputs).items()}
    aps = {k[3:]: nc.dram_tensor(k, v.shape, _mybir.dt.from_np(v.dtype), kind="ExternalInput").ap()
           for k, v in arrays.items()}
    out = nc.dram_tensor("out_tokens", (B, T, C), _mybir.dt.from_np(_np.dtype("float32")),
                         kind="ExternalOutput").ap()
    build(nc, aps, out)
    r = _run(nc, [arrays], core_ids=[0])
    return r.results[0]["out_tokens"]
```

```python
from contextlib import ExitStack

import concourse.bass as bass
from concourse import mybir

ALU = mybir.AluOpType
ACT = mybir.ActivationFunctionType
AX = mybir.AxisListType
F32 = mybir.dt.float32
BF16 = mybir.dt.bfloat16
I32 = mybir.dt.int32

P = 128
B = 16
T = 256
C = 256
NT = T // P
NC = C // P
EPS = 1e-5
NEG = -1e30

IMGS = 4
GROUPS = B // IMGS
RB = 32
BR = T // RB
LEVELS = 3

H0, D0, SLOT = 16, 16, 32
HPM = P // SLOT
MQ = H0 // HPM

F0 = 1024
NF = F0 // P

H1, D1 = 16, 64
INNER = H1 * D1
MAXREL = 64
TOPK = T // 4
ROUNDS = TOPK // 8
EXTW = 3 * P - 1
EXTN = 2 * T - 1
PITCH = 3 * P
BAND = 2 * MAXREL - 1
ORDER = 3

E1, HID, K1 = 32, 1024, 8
NH = HID // P
WBUFS = 4


class Chain:

    def __init__(self, eng, sem):
        self.eng, self.sem, self.n = eng, sem, 0

    def step(self, ins):
        self.n += 1
        ins.then_inc(self.sem, 1)
        return self.n

    def link(self, ins):
        self.step(ins)
        self.eng.wait_ge(self.sem, self.n)

    def after(self, n):
        self.eng.wait_ge(self.sem, n)


def build(nc, A, out, stop="", dbg=None):
    with ExitStack() as ctx:
        def sb(name, shape, dt=F32):
            return ctx.enter_context(nc.sbuf_tensor(name, shape, dt))

        def sem(name):
            return ctx.enter_context(nc.semaphore(name))

        def dram(name, shape):
            return nc.dram_tensor(name, shape, F32, kind="Internal").ap()

        bank = [ctx.enter_context(nc.psum_tensor(f"bank{i}", [P, 512], F32)) for i in range(8)]

        h_tok = dram("h_tok", (B * T, C))
        h_mid = dram("h_mid", (B * T, C))
        h_att = dram("h_att", (B * T, C))
        gates_scr = dram("gates_scr", (E1, B, T))
        rel_scr = dram("rel_scr", (2, NT, P, PITCH))
        att_scr = dram("att_scr", (2, NT, P, PITCH))

        ident = sb("ident", [P, P])
        ident_b = sb("ident_b", [P, P], BF16)
        causal = sb("causal", [P, P], BF16)
        ones = sb("ones", [P, P])
        zeros = sb("zeros", [P, P])
        block_ones = sb("block_ones", [P, P])
        mhalf = sb("mhalf", [P, NT])
        low_mask = sb("low_mask", [P, NT, 192])

        wqk0 = sb("wqk0", [P, NC, 2 * MQ * P])
        wv0 = sb("wv0", [P, NC, C])
        wp0 = sb("wp0", [P, NC, C])
        bqk0 = sb("bqk0", [P, 2 * MQ])
        bv0 = sb("bv0", [P, C])
        bp0 = sb("bp0", [1, C])
        gamma = sb("gamma", [P, NC])
        beta = sb("beta", [P, NC])
        fc1 = sb("fc1", [P, NC, F0])
        fc2 = sb("fc2", [P, NF, C])
        fc1b = sb("fc1b", [P, NF])
        fc2b = sb("fc2b", [1, C])
        wqk1 = sb("wqk1", [P, NC, 2 * INNER])
        wv1 = sb("wv1", [P, NC, INNER])
        bqk1 = sb("bqk1", [P, 2 * (INNER // P)])
        bv1 = sb("bv1", [P, INNER])
        wo1 = sb("wo1", [P, INNER // P, C])
        bo1 = sb("bo1", [1, C])
        rel_k = sb("rel_k", [P, EXTN])
        rel_v = sb("rel_v", [P, D1])
        relv0 = sb("relv0", [P, D1])
        alphas = sb("alphas", [P, ORDER, H1])
        gate = sb("gate", [P, NC, E1])
        gate_b = sb("gate_b", [E1, 1])
        b1_all = sb("b1_all", [P, E1, NH])
        b2_all = sb("b2_all", [P, E1, NC])

        cur = sb("cur", [P, NT, C])
        stats = sb("stats", [P, NT, 6])
        meanvar = sb("meanvar", [P, NT, 2])
        vareps = sb("vareps", [P, NT])
        rstd = sb("rstd", [P, NT])
        xn = sb("xn", [P, NT, C])
        xn2 = sb("xn2", [P, NT, C])
        xnT = sb("xnT", [P, NC, T])

        s_load = sem("weights_loaded")
        s_const = sem("consts_ready")

        def bcast(ap, n=P):
            return ap.partition_broadcast(n)

        loads = [
            (wqk0[:, :, :], A["wqk0"].rearrange("(c p) n -> p c n", p=P)),
            (wv0[:, :, :], A["wv0"].rearrange("(c p) n -> p c n", p=P)),
            (wp0[:, :, :], A["wp0"].rearrange("(c p) n -> p c n", p=P)),
            (bqk0[:, :], A["bqk0"]),
            (bv0[:, :], bcast(A["bv0"])),
            (bp0[:, :], A["bp0"].rearrange("(a n) -> a n", a=1)),
            (gamma[:, :], A["gamma"]),
            (beta[:, :], A["beta"]),
            (fc1b[:, :], A["fc1b"]),
            (fc2b[:, :], A["fc2b"].rearrange("(a n) -> a n", a=1)),
            (wqk1[:, :, :], A["wqk1"].rearrange("(c p) n -> p c n", p=P)),
            (wv1[:, :, :], A["wv1"].rearrange("(c p) n -> p c n", p=P)),
            (bqk1[:, :], A["bqk1"]),
            (bv1[:, :], bcast(A["bv1"])),
            (wo1[:, :, :], A["wo1"].rearrange("(c p) n -> p c n", p=P)),
            (bo1[:, :], A["bo1"].rearrange("(a n) -> a n", a=1)),
            (rel_k[:, :], A["rel_k"]),
            (rel_v[:, :], A["rel_v"]),
            (relv0[:, :], bcast(A["relv0"])),
            (alphas[:, :, :], bcast(A["alphas"])),
            (gate[:, :, :], A["gate_w"].rearrange("(c p) n -> p c n", p=P)),
            (gate_b[:, :], A["gate_b"].rearrange("(a n) -> a n", n=1)),
            (b1_all[:, :, :], A["b1"]),
            (b2_all[:, :, :], A["b2"]),
        ]

        with ExitStack() as stage:
            def ssb(name, shape, dt=F32):
                return stage.enter_context(nc.sbuf_tensor(name, shape, dt))

            q1 = ssb("q1", [P, NC, F0], I32)
            q2 = ssb("q2", [P, NF, C], I32)
            sc1 = ssb("sc1", [P, NC, F0])
            sc2 = ssb("sc2", [P, NF, C])
            wdet = [None] + [ssb(f"wdet{j}", [P, 3, 3 * BR * C >> 2 * j]) for j in (1, 2, 3)]
            wapp = ssb("wapp", [P, BR * C >> 6])
            dbias = ssb("dbias", [P, 10])
            img = ssb("img", [P, 2, BR, C])
            lo = ssb("lo", [P, BR * C // 2])
            hi = ssb("hi", [P, BR * C // 2])
            app = [None] + [ssb(f"app{j}", [P, BR * C >> 2 * j]) for j in (1, 2, 3)]
            det = [None] + [ssb(f"det{j}", [P, 3, BR * C >> 2 * j]) for j in (1, 2, 3)]
            junk = ssb("junk", [P, 3 * BR * C // 4])
            dots = ssb("dots", [P, 10])
            logit = ssb("logit", [P, 10])
            top3 = ssb("top3", [P, 3])
            expo = ssb("expo", [P, 10])
            den = ssb("den", [P, 4])
            wts = ssb("wts", [P, 10])
            wpos = ssb("wpos", [P, 10])
            wneg = ssb("wneg", [P, 10])
            s_img = [sem(f"image_loaded{i}") for i in range(2)]
            s_dots = sem("dots_ready")
            s_sums = sem("dot_sums_ready")
            s_logit = sem("logits_ready")
            s_exp = sem("tok_exp_ready")
            s_rec = sem("image_rebuilt")
            s_saved = sem("image_saved")
            s_dve = sem("tok_vector_steps")
            s_q = sem("quantized_loaded")

            tok_loads = [
                (wdet[j][RB * i:RB * i + RB, :, :], A[f"wdet{j}"]) for j in (1, 2, 3) for i in range(IMGS)
            ] + [(wapp[RB * i:RB * i + RB, :], A["wapp"]) for i in range(IMGS)] + [
                (dbias[:, :], bcast(A["dbias"]))
            ]
            q_loads = [
                (q1[:, :, :], A["fc1_q"].rearrange("(c p) n -> p c n", p=P)),
                (q2[:, :, :], A["fc2_q"].rearrange("(c p) n -> p c n", p=P)),
                (sc1[:, :, :], bcast(A["fc1_s"])),
                (sc2[:, :, :], bcast(A["fc2_s"])),
            ]
            s_tokw = sem("tok_weights_loaded")

            block = stage.enter_context(nc.Block())

            @block.sync
            def _(sp):
                def load(g):
                    sp.dma_start(img[:, g % 2, :, :], A["x"][IMGS * g:IMGS * (g + 1)].rearrange(
                        "i (r k) c -> (i r) k c", k=BR)).then_inc(s_img[g % 2], 16)
                load(0)
                for dst, src in tok_loads:
                    sp.dma_start(dst, src).then_inc(s_tokw, 16)
                load(1)
                for dst, src in q_loads:
                    sp.dma_start(dst, src).then_inc(s_q, 16)
                for dst, src in loads:
                    sp.dma_start(dst, src).then_inc(s_load, 16)
                for g in range(GROUPS):
                    sp.wait_ge(s_rec, g + 1)
                    sp.dma_start(h_tok[g * IMGS * T:(g + 1) * IMGS * T, :].rearrange(
                        "(q k) c -> q k c", k=BR), img[:, g % 2, :, :]).then_inc(s_saved, 16)
                    if g + 2 < GROUPS:
                        sp.wait_ge(s_saved, 16 * (g + 1))
                        load(g + 2)
                sp.wait_ge(s_const, 3)
                for par in range(2):
                    for t in range(NT):
                        for off in (0, PITCH - MAXREL):
                            sp.dma_start(att_scr[par, t, :, off:off + MAXREL],
                                         zeros[:, 0:MAXREL]).then_inc(s_saved, 16)
                sp.wait_ge(s_saved, 16 * (GROUPS + 4 * NT))
                sp.wait_ge(s_load, 16 * len(loads))

            @block.gpsimd
            def _(pool):
                pool.memset(ident[:, :], 0.0).then_inc(s_const, 1)
                pool.memset(ones[:, :], 1.0).then_inc(s_const, 1)
                pool.memset(zeros[:, :], 0.0).then_inc(s_const, 1)
                pool.memset(block_ones[:, :], 0.0).then_inc(s_const, 1)
                pool.memset(mhalf[:, :], -0.5).then_inc(s_const, 1)
                pool.memset(causal[:, :], 0.0).then_inc(s_const, 1)
                pool.memset(low_mask[:, :, :], 1.0).then_inc(s_const, 1)
                pool.wait_ge(s_const, 7)
                pool.affine_select(out=ident[:, :], in_=ident[:, :], compare_op=ALU.not_equal, fill=1.0,
                                   base=0, pattern=[[-1, P]], channel_multiplier=1).then_inc(s_const, 1)
                pool.affine_select(out=causal[:, :], in_=causal[:, :], compare_op=ALU.is_ge, fill=NEG,
                                   base=0, pattern=[[-1, P]], channel_multiplier=1).then_inc(s_const, 1)
                for t in range(NT):
                    pool.affine_select(out=low_mask[:, t, :], in_=low_mask[:, t, :], compare_op=ALU.is_ge,
                                       fill=0.0, base=P * t - MAXREL, pattern=[[-1, 192]],
                                       channel_multiplier=1).then_inc(s_const, 1)
                for i in range(IMGS):
                    pool.wait_ge(s_const, 11 + i)
                    pool.memset(block_ones[RB * i:RB * (i + 1), RB * i:RB * (i + 1)], 1.0).then_inc(s_const, 1)
                pool.wait_ge(s_const, 15)
                pool.tensor_copy(ident_b[:, :], ident[:, :]).then_inc(s_const, 1)

            @block.tensor
            def _(pe):
                pe.wait_ge(s_const, 16)
                for g in range(GROUPS):
                    pe.wait_ge(s_dots, g + 1)
                    pe.matmul(bank[0][:, 0:10], block_ones[:, :], dots[:, :], start=True,
                              stop=True).then_inc(s_sums, 1)

            @block.scalar
            def _(act):
                for g in range(GROUPS):
                    act.wait_ge(s_logit, g + 1)
                    act.activation(expo[:, :], logit[:, :], ACT.Exp).then_inc(s_exp, 1)
                act.wait_ge(s_load, 16 * len(loads))
                flat = alphas[:, :, :].rearrange("p k h -> p (k h)")
                act.activation(flat, flat, ACT.Exp, scale=-1.0).then_inc(s_exp, 1)

            @block.vector
            def _(dve):
                ch = Chain(dve, s_dve)
                dve.wait_ge(s_tokw, 16 * len(tok_loads))
                for g in range(GROUPS):
                    dve.wait_ge(s_img[g % 2], 16 * (g // 2 + 1))
                    cur_a, rows, cols = img[:, g % 2, :, :].rearrange("p k c -> p (k c)"), BR, C
                    for j in (1, 2, 3):
                        n = rows * cols
                        pair = cur_a.rearrange("p (n e) -> p n e", e=2)
                        ch.step(dve.tensor_tensor(lo[:, 0:n // 2], pair[:, :, 0], pair[:, :, 1], ALU.add))
                        ch.link(dve.tensor_tensor(hi[:, 0:n // 2], pair[:, :, 0], pair[:, :, 1], ALU.subtract))
                        rows, cols = rows // 2, cols // 2
                        for src, dst_sum, dst_dif in ((lo, app[j][:, :], det[j][:, 0, :]),
                                                      (hi, det[j][:, 1, :], det[j][:, 2, :])):
                            v = src[:, 0:n // 2].rearrange("p (r e c) -> p r e c", e=2, c=cols)
                            for dst, op in ((dst_sum, ALU.add), (dst_dif, ALU.subtract)):
                                ch.step(dve.tensor_tensor(dst.rearrange("p (r c) -> p r c", c=cols),
                                                          v[:, :, 0, :], v[:, :, 1, :], op))
                        ch.after(ch.n)
                        cur_a = app[j][:, :]
                    for j in (1, 2, 3):
                        for o in range(3):
                            ch.link(dve.tensor_tensor_reduce(
                                junk[:, 0:3 * rows_of(j)], det[j][:, :, :].rearrange("p b n -> p (b n)"),
                                wdet[j][:, o, :], 0.5 ** j, 0.0, ALU.mult, ALU.add,
                                dots[:, 3 * (j - 1) + o:3 * (j - 1) + o + 1]))
                    dve.tensor_tensor_reduce(junk[:, 0:rows_of(3)], app[3][:, :], wapp[:, :], 0.125, 0.0,
                                             ALU.mult, ALU.add, dots[:, 9:10]).then_inc(s_dots, 1)
                    dve.wait_ge(s_sums, g + 1)
                    ch.link(dve.tensor_tensor(logit[:, :], bank[0][:, 0:10], dbias[:, :], ALU.add))
                    ch.link(dve.tensor_reduce(top3[:, :], logit[:, 0:9].rearrange("p (j o) -> p j o", o=3),
                                              AX.X, ALU.max))
                    ch.step(dve.tensor_tensor(logit[:, 0:9].rearrange("p (j o) -> p j o", o=3),
                                              logit[:, 0:9].rearrange("p (j o) -> p j o", o=3),
                                              top3[:, :].unsqueeze(2).to_broadcast([P, 3, 3]), ALU.subtract))
                    ch.link(dve.tensor_scalar(logit[:, 9:10], logit[:, 9:10], -1.0, None, ALU.mult))
                    dve.tensor_copy(top3[:, 0:1], logit[:, 9:10]).then_inc(s_logit, 1)
                    dve.wait_ge(s_exp, g + 1)
                    ch.step(dve.tensor_reduce(den[:, 0:3], expo[:, 0:9].rearrange("p (j o) -> p j o", o=3),
                                              AX.X, ALU.add))
                    ch.link(dve.tensor_scalar(den[:, 3:4], expo[:, 9:10], 1.0, None, ALU.add))
                    ch.link(dve.reciprocal(den[:, :], den[:, :]))
                    ch.step(dve.tensor_tensor(wts[:, 0:9].rearrange("p (j o) -> p j o", o=3),
                                              expo[:, 0:9].rearrange("p (j o) -> p j o", o=3),
                                              den[:, 0:3].unsqueeze(2).to_broadcast([P, 3, 3]), ALU.mult))
                    ch.link(dve.tensor_scalar(wts[:, 9:10], den[:, 3:4], 1.0, None, ALU.mult))
                    for j in (1, 2, 3):
                        for sign, dst in ((1.0, wpos), (-1.0, wneg)):
                            ch.step(dve.tensor_scalar(dst[:, 3 * (j - 1):3 * j], wts[:, 3 * (j - 1):3 * j],
                                                      sign * 0.25 ** j, None, ALU.mult))
                    ch.link(dve.tensor_scalar(wpos[:, 9:10], wts[:, 9:10], 0.25 ** 3, None, ALU.mult))
                    ch.link(dve.tensor_scalar(app[3][:, :], app[3][:, :], wpos[:, 9:10], None, ALU.mult))
                    for j in (3, 2, 1):
                        rows, cols = BR >> j, C >> j
                        a = app[j][:, :].rearrange("p (r c) -> p r c", c=cols)
                        w = [(wpos[:, 3 * (j - 1) + o:3 * (j - 1) + o + 1],
                              wneg[:, 3 * (j - 1) + o:3 * (j - 1) + o + 1]) for o in range(3)]
                        h, v, d = (det[j][:, o, :].rearrange("p (r c) -> p r c", c=cols) for o in range(3))
                        lov = lo[:, 0:2 * rows * cols].rearrange("p (r e c) -> p r e c", e=2, c=cols)
                        hiv = hi[:, 0:2 * rows * cols].rearrange("p (r e c) -> p r e c", e=2, c=cols)
                        ch.step(dve.tensor_scalar(v, v, w[1][0], None, ALU.mult))
                        for e in range(2):
                            ch.step(dve.scalar_tensor_tensor(out=lov[:, :, e, :], in0=h, scalar=w[0][e], in1=a,
                                                             op0=ALU.mult, op1=ALU.add))
                        ch.after(ch.n)
                        for e in range(2):
                            ch.step(dve.scalar_tensor_tensor(out=hiv[:, :, e, :], in0=d, scalar=w[2][e], in1=v,
                                                             op0=ALU.mult, op1=ALU.add))
                        ch.after(ch.n)
                        if j > 1:
                            up = app[j - 1][:, :].rearrange("p (n e) -> p n e", e=2)
                        else:
                            up = img[:, g % 2, :, :].rearrange("p k (c e) -> p (k c) e", e=2)
                        n = 2 * rows * cols
                        ch.step(dve.tensor_tensor(up[:, :, 0], lo[:, 0:n], hi[:, 0:n], ALU.add))
                        ins = dve.tensor_tensor(up[:, :, 1], lo[:, 0:n], hi[:, 0:n], ALU.subtract)
                        if j > 1:
                            ch.link(ins)
                    ins.then_inc(s_rec, 1)
                    dve.wait_ge(s_rec, g + 1)
                    ch.after(ch.n)
                dve.wait_ge(s_q, 16 * len(q_loads))
                for w, q, s in ((fc1, q1, sc1), (fc2, q2, sc2)):
                    ch.link(dve.tensor_scalar(w[:, :, :], q[:, :, :], -128.0, None, ALU.add))
                    ch.link(dve.tensor_tensor(w[:, :, :], w[:, :, :], s[:, :, :], ALU.mult))
                dve.wait_ge(s_load, 16 * len(loads))
                ch.link(dve.tensor_scalar(bqk0[:, 0:MQ], bqk0[:, 0:MQ], 1.0 / D0, None, ALU.mult))
                n1 = INNER // P
                ch.link(dve.tensor_scalar(bqk1[:, n1:2 * n1], bqk1[:, n1:2 * n1], D1 ** -0.5, None, ALU.mult))
                rv = bv1[:, :].rearrange("p (h d) -> p h d", d=D1)
                ch.step(dve.tensor_tensor(rv, rv, relv0[:, :].unsqueeze(1).to_broadcast([P, H1, D1]), ALU.add))
                ch.step(dve.tensor_tensor(rel_v[:, :], rel_v[:, :], relv0[:, :], ALU.subtract))
                dve.wait_ge(s_exp, GROUPS + 1)
                ch.link(dve.tensor_scalar(alphas[:, :, :], alphas[:, :, :], 1.0, None, ALU.add))
                ch.link(dve.reciprocal(alphas[:, :, :], alphas[:, :, :]))

        if stop == "tok":
            return finish_copy(nc, ctx, h_tok, out, sem)
        body = {}

        def bsem(name):
            body[name] = sem(name)
            return body[name]

        load_cur = bsem("layer0_tokens_loaded")
        stats_ready = bsem("stats_ready")
        rstd_ready = bsem("rstd_ready")
        xn_ready = bsem("xn_ready")
        xnT_ps = bsem("xnT_in_psum")
        xnT_ready = bsem("xnT_ready")
        pool_steps = bsem("pool_steps")
        dve_steps = bsem("vector_steps")
        qk0_ps = bsem("qk0_in_psum")
        qk0_ready = bsem("qk0_ready")
        v0_ps = bsem("v0_in_psum")
        v0_ready = bsem("v0_ready")
        s0_ps = bsem("scores0_in_psum")
        max0_ready = bsem("rowmax0_ready")
        p0_ready = bsem("probs0_ready")
        pT0_ps = bsem("probsT0_in_psum")
        pT0_ready = bsem("probsT0_ready")
        o0_ps = bsem("heads0_in_psum")
        y0_ready = bsem("attended0_ready")
        yT0_ps = bsem("attendedT0_in_psum")
        yT0_ready = bsem("attendedT0_ready")
        r0_ps = bsem("projected0_in_psum")
        f1_ps = bsem("hidden_in_psum")
        f1_ready = bsem("hidden_ready")
        f2_ps = bsem("ffn_in_psum")
        cur_done = bsem("layer0_done")
        cur_saved = bsem("layer0_saved")
        v1_ps = bsem("v1_in_psum")
        v1_ready = bsem("v1_ready")
        v1_moved = bsem("v1_moved")
        xnT_moved = bsem("xnT_moved")
        qk1_ps = bsem("qk1_in_psum")
        qk1_ready = bsem("qk1_ready")
        rel_ps = bsem("rel_in_psum")
        rel_ready = bsem("rel_ready")
        rel_out = [bsem(f"rel_written{i}") for i in range(2)]
        rel_back = [bsem(f"rel_read{i}") for i in range(2)]
        s1_ps = bsem("scores1_in_psum")
        s1_ready = bsem("scores1_ready")
        max1_ready = bsem("rowmax1_ready")
        e1_ready = bsem("exp1_ready")
        p1_ready = bsem("probs1_ready")
        low_ready = bsem("low_clip_ready")
        att_out = [bsem(f"att_written{i}") for i in range(2)]
        att_back = [bsem(f"att_read{i}") for i in range(2)]
        pT1_ps = bsem("probsT1_in_psum")
        pT1_ready = bsem("probsT1_ready")
        wT_ps = bsem("bandT_in_psum")
        wT_ready = bsem("bandT_ready")
        av_ps = bsem("av_in_psum")
        av_ready = bsem("av_ready")
        mix_ready = bsem("orders_mixed")
        mT_ps = bsem("mixedT_in_psum")
        mT_ready = bsem("mixedT_ready")
        load_end = bsem("tail_tokens_loaded")
        r1_ps = bsem("projected1_in_psum")
        end_done = bsem("attention1_done")
        end_saved = bsem("attention1_saved")
        stats_end = bsem("tail_stats_ready")
        rstd_end_ready = bsem("tail_rstd_ready")
        xn_end_ready = bsem("tail_xn_ready")
        xnT_end_ps = bsem("tail_xnT_in_psum")
        xnT_end_ready = bsem("tail_xnT_ready")
        lg_ps = bsem("gate_logits_in_psum")
        gmax_ready = bsem("gate_max_ready")
        gexp_ready = bsem("gate_exp_ready")
        g_ready = bsem("gates_ready")
        gT_ps = bsem("gatesT_in_psum")
        gT_ready = bsem("gatesT_ready")
        mg_ps = bsem("merged_in_psum")
        mg_kept = bsem("merged_kept")
        body_sems = sorted(s.num for s in body.values())
        assert body_sems == list(range(body_sems[0], body_sems[0] + len(body_sems)))
        arrived = sem("engines_at_turn_end")
        go = {n: sem(f"next_turn_{n}") for n in ("pool", "act", "dve", "pe")}

        merged = sb("merged", [P, NC, E1, B])

        def turn_end(eng, name):
            eng.drain().then_inc(arrived, 1)
            eng.wait_ge(go[name], 1)
            eng.sem_clear(go[name])

        def all_turns(eng, turn):
            turn(0, None, None)
            turn(1, 0, None)
            with eng.Fori(1, B - 1) as b:
                turn(b + 1, b, b - 1)
            turn(None, B - 1, B - 2)
            turn(None, None, B - 1)

        class Counts:

            def __init__(self, nxt, now, old):
                self.f0, self.f1 = (1 if now is not None else H1), (H1 if nxt is not None else H1 - 1)
                self.g0, self.g1 = (-1 if old is not None else 0), (H1 - 2 if now is not None else -1)

            def fronts(self, h):
                return [h + 1] if self.f0 <= h + 1 <= self.f1 else []

            def backs(self, h):
                return [h - 1] if self.g0 <= h - 1 <= self.g1 else []

            def f(self, f):
                return f - self.f0 + 1

            def g(self, g):
                return g - self.g0 + 1

            def f_like(self, f):
                return (f - self.f0) // 2 + 1

            def g_like(self, g):
                return (g - self.g0) // 2 + 1

        NORM0, QK0, V0 = 0, 4, 6
        PROJ1, ADD1, NORM_END, LOGITS, GMAX, GATES, GT, MERGE, MCOPY = 12, 13, 14, 15, 16, 17, 18, 19, 20
        HEADS0 = 21
        TURN_Y, PROJ0, ADD0 = 40, 41, 42
        NORM1, NORM2, TURN2, UP, DOWN, ADDF = 43, 44, 45, 46, 48, 50
        NORM3, TURN3, V1 = 51, 52, 53
        MIX_AT = {1: 3, 5: 0, 9: 1, 13: 2}
        TURN_AT = {2: 3, 7: 0, 11: 1, 15: 2}
        GROUP = H1 // 4

        with ExitStack() as stage:
            def ssb(name, shape, dt=F32):
                return stage.enter_context(nc.sbuf_tensor(name, shape, dt))

            big = ssb("big", [P, NF, T])
            qkT0, hid = big, big
            v1_next = big[:, :, :].rearrange("p (t a) n -> p t (a n)", t=NT)
            v0 = ssb("v0", [P, NT, C])
            nmax0 = ssb("nmax0", [P, 2, NT])
            sum0 = ssb("sum0", [P, NT, H0])
            rsum0 = ssb("rsum0", [P, NT, H0])
            probs0 = ssb("probs0", [P, 2, 3 * P])
            probsT0 = ssb("probsT0", [P, 2, 3 * P])
            y0 = ssb("y0", [P, NT, C])
            yT0 = ssb("yT0", [P, NC, T])
            qkT1 = ssb("qkT1", [P, 2, 2, T])
            v1 = ssb("v1", [P, NT, INNER])
            xnT1 = ssb("xnT1", [P, NC, T])
            rel_sb = ssb("rel_sb", [P, 2, NT, PITCH])
            rel_in = ssb("rel_in", [P, 2, NT, T])
            scores = ssb("scores", [P, 2, NT, T])
            work = ssb("work", [P, NT, T])
            top = ssb("top", [P, 2, NT, ROUNDS, 8])
            nmax1 = ssb("nmax1", [P, 2, NT])
            probs1 = ssb("probs1", [P, 2, NT, T])
            sum1 = ssb("sum1", [P, 2, NT])
            rsum1 = ssb("rsum1", [P, 2, NT])
            band = ssb("band", [P, 2, NT, P])
            bandT = ssb("bandT", [P, 2, NT, P])
            probsT1 = ssb("probsT1", [P, 2, NT, T])
            av = ssb("av", [P, ORDER, NT, INNER])
            mixT = ssb("mixT", [P, INNER // P, T])
            end = ssb("end", [P, NT, C])
            xn_end = ssb("xn_end", [P, NT, C])
            xnT_end = ssb("xnT_end", [P, NC, T])
            stats_e = ssb("stats_e", [P, NT, 6])
            meanvar_e = ssb("meanvar_e", [P, NT, 2])
            vareps_e = ssb("vareps_e", [P, NT])
            rstd_e = ssb("rstd_e", [P, NT])
            lg = ssb("lg", [E1, T])
            gsum = ssb("gsum", [E1, 4])
            top_g = ssb("top_g", [E1, 8])
            rest = ssb("rest", [E1, T])
            g_cur = ssb("g_cur", [E1, T])
            gT = ssb("gT", [P, NT, E1])

            block = stage.enter_context(nc.Block())

            @block.sync
            def _(sp):
                def turn(nxt, now, old):
                    n = Counts(nxt, now, old)

                    def rel_write(f):
                        sp.wait_ge(rel_ready, n.f(f))
                        if f - 2 >= n.f0:
                            sp.wait_ge(s1_ready, n.f(f - 2))
                        sp.dma_start(rel_scr[f % 2].rearrange("t p x -> p t x")[:, :, 0:EXTW],
                                     rel_sb[:, f % 2, :, 0:EXTW]).then_inc(rel_out[f % 2], 16)

                    def rel_read(f):
                        sp.wait_ge(rel_out[f % 2], 16 * n.f_like(f))
                        sp.dma_start(rel_in[:, f % 2, :, :], skewed(rel_scr, f % 2, P - 1, -1, T))\
                            .then_inc(rel_back[f % 2], 16)

                    def att_write(g):
                        if g >= 0:
                            sp.wait_ge(p1_ready, g + 1)
                        if g - 2 >= n.g0:
                            sp.wait_ge(att_back[g % 2], 16 * n.g_like(g - 2))
                            sp.wait_ge(wT_ps, n.g(g - 2))
                        sp.dma_start(att_scr[g % 2].rearrange("t p x -> p t x")[:, :, MAXREL:MAXREL + T],
                                     probs1[:, g % 2, :, :]).then_inc(att_out[g % 2], 16)

                    def att_read(g):
                        sp.wait_ge(att_out[g % 2], 16 * n.g_like(g))
                        sp.dma_start(band[:, g % 2, :, 0:BAND], skewed(att_scr, g % 2, 1, 1, BAND, P))\
                            .then_inc(att_back[g % 2], 16)

                    if nxt is not None:
                        sp.dma_start(cur[:, :, :], rows(h_tok, nxt)).then_inc(load_cur, 16)
                    if old is not None:
                        sp.dma_start(end[:, :, :], rows(h_mid, old)).then_inc(load_end, 16)
                    for h in range(H1):
                        for g in n.backs(h):
                            att_write(g)
                        for f in n.fronts(h):
                            rel_write(f)
                        for g in n.backs(h):
                            att_read(g)
                        for f in n.fronts(h):
                            rel_read(f)
                        if old is not None and h == MCOPY // 4:
                            sp.wait_ge(end_done, 1)
                            sp.dma_start(rows(h_att, old), end[:, :, :]).then_inc(end_saved, 16)
                            sp.wait_ge(g_ready, 1)
                            sp.dma_start(gates_scr[:, bass.ds(old, 1), :].rearrange("e b t -> e (b t)"),
                                         g_cur[:, :]).then_inc(end_saved, 16)
                        if nxt is not None and h == NORM3 // 4:
                            sp.wait_ge(cur_done, 1)
                            sp.dma_start(rows(h_mid, nxt), cur[:, :, :]).then_inc(cur_saved, 16)
                    if nxt is not None:
                        sp.wait_ge(cur_saved, 16)
                    if old is not None:
                        sp.wait_ge(end_saved, 32)
                    sp.wait_ge(arrived, 4)
                    sp.sem_clear(range(body_sems[0], body_sems[-1] + 1))
                    sp.sem_clear(arrived)
                    for name in go:
                        sp.sem_inc(go[name], 1)

                all_turns(sp, turn)

            @block.gpsimd
            def _(pool):
                def turn(nxt, now, old):
                    n = Counts(nxt, now, old)
                    steps = [0]

                    def rstd_of(k):
                        pool.wait_ge(stats_ready, k + 1)
                        pool.tensor_tensor(rstd[:, :], vareps[:, :], mhalf[:, :], ALU.pow)\
                            .then_inc(rstd_ready, 1)

                    def mix(q, after):
                        pool.wait_ge(av_ready, ORDER * n.g(after))
                        part = [av[:, k, :, :].rearrange("p t (h d) -> p t h d", d=D1)[
                            :, :, GROUP * q:GROUP * (q + 1), :] for k in range(ORDER)]
                        for k in range(ORDER):
                            for t in range(NT):
                                al = alphas[:, k, GROUP * q:GROUP * (q + 1)].unsqueeze(2)
                                pool.tensor_tensor(part[k][:, t], part[k][:, t],
                                                   al.to_broadcast([P, GROUP, D1]), ALU.mult)\
                                    .then_inc(pool_steps, 1)
                        steps[0] += ORDER * NT
                        for k in range(1, ORDER):
                            pool.wait_ge(pool_steps, steps[0])
                            for t in range(NT):
                                pool.tensor_tensor(part[0][:, t], part[0][:, t], part[k][:, t], ALU.add)\
                                    .then_inc(mix_ready if k == ORDER - 1 else pool_steps, 1)
                            steps[0] += NT if k < ORDER - 1 else 0

                    for h in range(H1):
                        if h in MIX_AT:
                            q = MIX_AT[h]
                            if q == 3 and old is not None:
                                mix(3, -1)
                            elif q < 3 and now is not None:
                                mix(q, GROUP * q + GROUP - 1)
                        for p in range(4 * h, 4 * h + 4):
                            if nxt is not None:
                                for k, at in enumerate((NORM0, NORM1, NORM2, NORM3)):
                                    if p == at:
                                        rstd_of(k)
                            if old is not None and p == ADD1:
                                pool.wait_ge(stats_end, 1)
                                pool.tensor_tensor(rstd_e[:, :], vareps_e[:, :], mhalf[:, :], ALU.pow)\
                                    .then_inc(rstd_end_ready, 1)
                        if h == 0 and now is not None:
                            if old is not None:
                                pool.wait_ge(av_ps, 1)
                            pool.tensor_copy(v1[:, :, :], v1_next).then_inc(v1_moved, 1)
                    turn_end(pool, "pool")

                all_turns(pool, turn)

            @block.tensor
            def _(pe):
                def turn_over(dst, src, done):
                    for c in range(NC):
                        for t in range(NT):
                            ins = pe.transpose(dst[:, c * T + t * P:c * T + (t + 1) * P],
                                               src(t, c), ident[:, :])
                    ins.then_inc(done, 1)

                def turn(nxt, now, old):
                    n = Counts(nxt, now, old)

                    def scores0(h):
                        m, at = h // HPM, SLOT * (h % HPM)
                        if h == 0:
                            pe.wait_ge(qk0_ready, MQ)
                            if old is not None:
                                pe.wait_ge(mg_kept, 1)
                        if h >= 2:
                            pe.wait_ge(p0_ready, h - 1)
                        ps = bank[6 + h % 2]
                        q = qkT0[at:at + D0, m, :]
                        k = qkT0[at:at + D0, MQ + m, :]
                        for col, tq, tk in ((0, 0, 0), (P, 1, 0), (2 * P, 1, 1)):
                            ins = pe.matmul(ps[:, col:col + P], q[:, tq * P:(tq + 1) * P],
                                            k[:, tk * P:(tk + 1) * P], start=True, stop=tq != tk)
                            if tq == tk:
                                ins = pe.matmul(ps[:, col:col + P], ident_b[:, :], causal[:, :],
                                                start=False, stop=True)
                        ins.then_inc(s0_ps, 1)

                    def probs_over0(h):
                        pe.wait_ge(p0_ready, h + 1)
                        if h == 0:
                            pe.wait_ge(v0_ready, 1)
                        else:
                            pe.wait_ge(pT0_ready, h)
                        if h % HPM == 0 and h:
                            pe.wait_ge(y0_ready, h // HPM)
                        for i in range(3):
                            ins = pe.transpose(bank[0][:, i * P:(i + 1) * P],
                                               probs0[:, h % 2, i * P:(i + 1) * P], ident[:, :])
                        ins.then_inc(pT0_ps, 1)

                    def attend0(h):
                        pe.wait_ge(pT0_ready, h + 1)
                        at = [3 * P + t * HPM * D0 + (h % HPM) * D0 for t in range(NT)]
                        o = [bank[0][:, a:a + D0] for a in at]
                        v = [v0[:, t, h * D0:(h + 1) * D0] for t in range(NT)]
                        pT = probsT0[:, h % 2, :]
                        pe.matmul(o[0], pT[:, 0:P], v[0], start=True, stop=True)
                        pe.matmul(o[1], pT[:, P:2 * P], v[0], start=True, stop=False)
                        pe.matmul(o[1], pT[:, 2 * P:3 * P], v[1], start=False, stop=True).then_inc(o0_ps, 1)

                    def layer0(p):
                        if p == NORM0 + 1:
                            pe.wait_ge(xn_ready, NT)
                            turn_over(bank[0], lambda t, c: xn[:, t, c * P:(c + 1) * P], xnT_ps)
                        if p in (QK0, QK0 + 1):
                            pe.wait_ge(xnT_ready, 1)
                            for i in range(2):
                                j = 2 * (p - QK0) + i
                                if j >= 2:
                                    pe.wait_ge(qk0_ready, j - 1)
                                for m in (2 * j, 2 * j + 1):
                                    for c in range(NC):
                                        ins = pe.matmul(bank[6 + i][:, T * (m % 2):T * (m % 2 + 1)],
                                                        wqk0[:, c, m * P:(m + 1) * P], xnT[:, c, :],
                                                        start=(c == 0), stop=(c == NC - 1))
                                ins.then_inc(qk0_ps, 1)
                        if p == V0:
                            for t in range(NT):
                                for c in range(NC):
                                    ins = pe.matmul(bank[0][:, t * C:(t + 1) * C], xnT[:, c, t * P:(t + 1) * P],
                                                    wv0[:, c, :], start=(c == 0), stop=(c == NC - 1))
                            ins.then_inc(v0_ps, 1)
                        k = p - HEADS0
                        if 0 <= k < H0:
                            scores0(k)
                        if 0 <= k - 3 < H0:
                            attend0(k - 3)
                        if 0 <= k - 2 < H0:
                            probs_over0(k - 2)
                        if p == TURN_Y:
                            pe.wait_ge(y0_ready, MQ)
                            turn_over(bank[6], lambda t, c: y0[:, t, c * P:(c + 1) * P], yT0_ps)
                        if p == PROJ0:
                            pe.wait_ge(yT0_ready, 1)
                            for t in range(NT):
                                for c in range(NC):
                                    pe.matmul(bank[7][:, t * C:(t + 1) * C], yT0[:, c, t * P:(t + 1) * P],
                                              wp0[:, c, :], start=(c == 0), stop=False)
                                ins = pe.matmul(bank[7][:, t * C:(t + 1) * C], ones[0:1, :], bp0[:, :],
                                                start=False, stop=True)
                            ins.then_inc(r0_ps, 1)
                        if p == TURN2:
                            pe.wait_ge(xn_ready, 3 * NT)
                            turn_over(bank[6], lambda t, c: xn2[:, t, c * P:(c + 1) * P], xnT_ps)
                        if p in (UP, UP + 1):
                            pe.wait_ge(xnT_ready, 2)
                            for i in range(2):
                                j = 2 * (p - UP) + i
                                if j >= 2:
                                    pe.wait_ge(f1_ready, 2 * j - 2)
                                for f in (2 * j, 2 * j + 1):
                                    for c in range(NC):
                                        ins = pe.matmul(bank[7 * (1 - i)][:, T * (f % 2):T * (f % 2 + 1)],
                                                        fc1[:, c, f * P:(f + 1) * P], xnT[:, c, :],
                                                        start=(c == 0), stop=(c == NC - 1))
                                ins.then_inc(f1_ps, 1)
                        if p in (DOWN, DOWN + 1):
                            t = p - DOWN
                            for f in range(NF):
                                if t == 0:
                                    pe.wait_ge(f1_ready, f + 1)
                                pe.matmul(bank[6][:, t * C:(t + 1) * C], hid[:, f, t * P:(t + 1) * P],
                                          fc2[:, f, :], start=(f == 0), stop=False)
                            ins = pe.matmul(bank[6][:, t * C:(t + 1) * C], ones[0:1, :], fc2b[:, :],
                                            start=False, stop=True)
                            if t:
                                ins.then_inc(f2_ps, 1)
                        if p == TURN3:
                            pe.wait_ge(xn_ready, 4 * NT)
                            turn_over(bank[7], lambda t, c: xn[:, t, c * P:(c + 1) * P], xnT_ps)
                        if p in (V1, V1 + 2):
                            pe.wait_ge(xnT_ready, 3)
                            for i in range(2):
                                t = (p - V1) // 2
                                if t:
                                    pe.wait_ge(v1_ready, i + 1)
                                for c in range(NC):
                                    ins = pe.matmul(bank[6 * i][:, :], xnT[:, c, t * P:(t + 1) * P],
                                                    wv1[:, c, i * 512:(i + 1) * 512],
                                                    start=(c == 0), stop=(c == NC - 1))
                                ins.then_inc(v1_ps, 1)

                    def tail(p):
                        if p == PROJ1:
                            pe.wait_ge(mT_ready, 1)
                            for t in range(NT):
                                for j in range(INNER // P):
                                    pe.matmul(bank[7][:, t * C:(t + 1) * C], mixT[:, j, t * P:(t + 1) * P],
                                              wo1[:, j, :], start=(j == 0), stop=False)
                                ins = pe.matmul(bank[7][:, t * C:(t + 1) * C], ones[0:1, :], bo1[:, :],
                                                start=False, stop=True)
                            ins.then_inc(r1_ps, 1)
                        if p == NORM_END:
                            pe.wait_ge(xn_end_ready, NT)
                            turn_over(bank[6], lambda t, c: xn_end[:, t, c * P:(c + 1) * P], xnT_end_ps)
                        if p == LOGITS:
                            pe.wait_ge(xnT_end_ready, 1)
                            for c in range(NC):
                                ins = pe.matmul(bank[7][0:E1, 0:T], gate[:, c, :], xnT_end[:, c, :],
                                                start=(c == 0), stop=(c == NC - 1))
                            ins.then_inc(lg_ps, 1)
                        if p == GT:
                            pe.wait_ge(g_ready, 1)
                            for t in range(NT):
                                ins = pe.transpose(bank[6][:, t * E1:(t + 1) * E1], g_cur[:, t * P:(t + 1) * P],
                                                   ident[0:E1, 0:E1])
                            ins.then_inc(gT_ps, 1)
                        if p == MERGE:
                            pe.wait_ge(gT_ready, 1)
                            for c in range(NC):
                                for t in range(NT):
                                    ins = pe.matmul(bank[7][:, c * E1:(c + 1) * E1],
                                                    xn_end[:, t, c * P:(c + 1) * P], gT[:, t, :],
                                                    start=(t == 0), stop=(t == NT - 1))
                            ins.then_inc(mg_ps, 1)

                    def front(f):
                        at, j = D1 * (f % 2), f // 2
                        if now is None or j >= 1:
                            pe.wait_ge(qk1_ready, j if now is not None else 1)
                        q = qkT1[at:at + D1, j % 2, 0, :]
                        k = qkT1[at:at + D1, j % 2, 1, :]
                        if f > n.f0:
                            pe.wait_ge(rel_ready, n.f(f - 1))
                        for t in range(NT):
                            u = T - 1 - (P - 1) - P * t
                            ins = pe.matmul(bank[2 + t][:, 0:EXTW], q[:, t * P:(t + 1) * P],
                                            rel_k[at:at + D1, u:u + EXTW], start=True, stop=True)
                        ins.then_inc(rel_ps, 1)
                        if f > n.f0:
                            pe.wait_ge(s1_ready, n.f(f - 1))
                        for t in range(NT):
                            ins = pe.matmul(bank[1][:, t * T:(t + 1) * T], q[:, t * P:(t + 1) * P], k,
                                            start=True, stop=True)
                        ins.then_inc(s1_ps, 1)

                    def qk1(j, f):
                        if f >= n.f0:
                            pe.wait_ge(rel_ready, n.f(f))
                        if j == 1:
                            pe.wait_ge(xnT_moved, 1)
                        src = xnT1
                        if j == H1 // 2:
                            pe.wait_ge(xnT_ready, 3)
                            src = xnT
                        for i in range(2):
                            for c in range(NC):
                                at = i * INNER + (j % (H1 // 2)) * P
                                ins = pe.matmul(bank[2][:, i * T:(i + 1) * T], wqk1[:, c, at:at + P],
                                                src[:, c, :], start=(c == 0), stop=(c == NC - 1))
                        ins.then_inc(qk1_ps, 1)

                    def probs_over(g):
                        if g >= 0:
                            pe.wait_ge(p1_ready, g + 1)
                        if g > n.g0:
                            pe.wait_ge(pT1_ready, n.g(g - 1))
                        pe.wait_ge(mT_ready, mixes_before(g + 1, old)) if mixes_before(g + 1, old) else None
                        for kc in range(NT):
                            for t in range(NT):
                                ins = pe.transpose(bank[4][:, kc * T + t * P:kc * T + (t + 1) * P],
                                                   probs1[:, g % 2, t, kc * P:(kc + 1) * P], ident[:, :])
                        ins.then_inc(pT1_ps, 1)

                    def band_over(g):
                        pe.wait_ge(att_back[g % 2], 16 * n.g_like(g))
                        if g >= 0:
                            pe.wait_ge(low_ready, g + 1)
                        if g > n.g0:
                            pe.wait_ge(av_ready, ORDER * n.g(g - 1))
                        for t in range(NT):
                            ins = pe.transpose(bank[5][:, t * P:(t + 1) * P], band[:, g % 2, t, :], ident[:, :])
                        ins.then_inc(wT_ps, 1)

                    def order(g, k):
                        done = ORDER * (n.g(g) - 1) + k
                        if k == 0:
                            pe.wait_ge(pT1_ready, n.g(g))
                            pe.wait_ge(wT_ready, n.g(g))
                            if g == 0:
                                pe.wait_ge(v1_moved, 1)
                        if k:
                            pe.wait_ge(av_ready, done)
                        outs = []
                        for t in range(NT):
                            at = 2 * P + (done % 2) * P + t * D1
                            outs.append(bank[5][:, at:at + D1])
                            for kc in range(NT):
                                r = v1[:, kc, :] if k == 0 else av[:, k - 1, kc, :]
                                hh = g % H1
                                ins = pe.matmul(outs[t], probsT1[:, g % 2, kc, t * P:(t + 1) * P],
                                                r[:, hh * D1:(hh + 1) * D1], start=(kc == 0),
                                                stop=(k > 0 and kc == NT - 1))
                            if k == 0:
                                ins = pe.matmul(outs[t], bandT[:, g % 2, t, :], rel_v[:, :],
                                                start=False, stop=True)
                        ins.then_inc(av_ps, 1)

                    def mixed_over(h):
                        q = TURN_AT[h]
                        pe.wait_ge(mix_ready, NT * mixes_before(h + 1, old))
                        pe.wait_ge(pT1_ready, n.g(min(h - 1, n.g1)))
                        turn_over(bank[4], lambda t, c: av[:, 0, t, (2 * q + c) * P:(2 * q + c + 1) * P], mT_ps)

                    def point(p):
                        if old is not None:
                            tail(p)
                        if nxt is not None:
                            layer0(p)

                    for h in range(H1):
                        if nxt is not None and now is None and h == H1 - 1:
                            qk1(H1 // 2, 0)
                        for f in n.fronts(h):
                            front(f)
                        if now is not None and h % 2 == 0 and (h < H1 - 2 or nxt is not None):
                            qk1(h // 2 + 1, h + 1)
                        for g in n.backs(h):
                            probs_over(g)
                        point(4 * h)
                        point(4 * h + 1)
                        for g in n.backs(h):
                            band_over(g)
                            order(g, 0)
                        point(4 * h + 2)
                        for g in n.backs(h):
                            order(g, 1)
                            order(g, 2)
                        point(4 * h + 3)
                        if h in TURN_AT and (old if TURN_AT[h] == 3 else now) is not None:
                            mixed_over(h)
                    turn_end(pe, "pe")

                all_turns(pe, turn)

            @block.scalar
            def _(act):
                def leave(dst, src, done, **kw):
                    act.activation(dst, src, ACT.Copy, **kw).then_inc(done, 1)

                def turn(nxt, now, old):
                    n = Counts(nxt, now, old)

                    def exp0(h):
                        act.wait_ge(max0_ready, h + 1)
                        if h >= 2:
                            act.wait_ge(pT0_ps, h - 1)
                        ps = bank[6 + h % 2]
                        for t, a, z in ((0, 0, P), (1, P, 3 * P)):
                            ins = act.activation(probs0[:, h % 2, a:z], ps[:, a:z], ACT.Exp,
                                                 bias=nmax0[:, h % 2, t:t + 1], accum_out=sum0[:, t, h:h + 1])
                        ins.then_inc(p0_ready, 1)

                    def layer0(p):
                        if p == NORM0 + 1:
                            act.wait_ge(xnT_ps, 1)
                            leave(flat(xnT), bank[0][:, :], xnT_ready)
                        if p in (QK0, QK0 + 1):
                            if p == QK0 and now is not None:
                                act.wait_ge(v1_moved, 1)
                            for i in range(2):
                                j = 2 * (p - QK0) + i
                                act.wait_ge(qk0_ps, j + 1)
                                for m in (2 * j, 2 * j + 1):
                                    ins = act.activation(
                                        qkT0[:, m, :], bank[6 + i][:, T * (m % 2):T * (m % 2 + 1)],
                                        ACT.Identity, bias=bqk0[:, m:m + 1], scale=1.0 / D0 if m < MQ else 1.0)
                                ins.then_inc(qk0_ready, 1)
                        k = p - HEADS0
                        if 0 <= k - 1 < H0:
                            exp0(k - 1)
                        if 0 <= k - 2 < H0:
                            act.wait_ge(pT0_ps, k - 1)
                            if k - 2 >= 2:
                                act.wait_ge(o0_ps, k - 3)
                            leave(probsT0[:, k % 2, :], bank[0][:, 0:3 * P], pT0_ready)
                        if p == TURN_Y:
                            act.wait_ge(yT0_ps, 1)
                            leave(flat(yT0), bank[6][:, :], yT0_ready)
                        if p == TURN2:
                            act.wait_ge(xnT_ps, 2)
                            for c in range(NC):
                                ins = act.activation(xnT[:, c, :], bank[6][:, c * T:(c + 1) * T], ACT.Identity,
                                                     bias=beta[:, c:c + 1], scale=gamma[:, c:c + 1])
                            ins.then_inc(xnT_ready, 1)
                        if p in (UP, UP + 1):
                            for i in range(2):
                                j = 2 * (p - UP) + i
                                act.wait_ge(f1_ps, j + 1)
                                for f in (2 * j, 2 * j + 1):
                                    act.activation(hid[:, f, :], bank[7 * (1 - i)][:, T * (f % 2):T * (f % 2 + 1)],
                                                   ACT.Silu, bias=fc1b[:, f:f + 1]).then_inc(f1_ready, 1)
                        if p == TURN3:
                            act.wait_ge(xnT_ps, 3)
                            leave(flat(xnT), bank[7][:, :], xnT_ready)

                    def tail(p):
                        if p == NORM_END:
                            act.wait_ge(xnT_end_ps, 1)
                            leave(flat(xnT_end), bank[6][:, :], xnT_end_ready)
                        if p == GMAX:
                            act.wait_ge(gmax_ready, 1)
                            act.activation(lg[:, :], lg[:, :], ACT.Exp, bias=gsum[:, 0:1],
                                           accum_out=gsum[:, 1:2]).then_inc(gexp_ready, 1)
                        if p == GT:
                            act.wait_ge(gT_ps, 1)
                            leave(flat(gT), bank[6][:, 0:NT * E1], gT_ready)

                    def front_out(f):
                        act.wait_ge(rel_ps, n.f(f))
                        if f - 2 >= n.f0:
                            act.wait_ge(rel_out[f % 2], 16 * n.f_like(f - 2))
                        for t in range(NT):
                            ins = act.activation(rel_sb[:, f % 2, t, 0:EXTW], bank[2 + t][:, 0:EXTW], ACT.Copy)
                        ins.then_inc(rel_ready, 1)

                    def qk_out(j):
                        act.wait_ge(qk1_ps, j if now is not None else 1)
                        for i in range(2):
                            m = i * (INNER // P) + j % (H1 // 2)
                            ins = act.activation(qkT1[:, j % 2, i, :], bank[2][:, i * T:(i + 1) * T],
                                                 ACT.Identity, bias=bqk1[:, m:m + 1],
                                                 scale=1.0 if i == 0 else D1 ** -0.5)
                        ins.then_inc(qk1_ready, 1)

                    def exp1(h):
                        act.wait_ge(max1_ready, h + 1)
                        if h - 2 >= n.g0:
                            act.wait_ge(pT1_ps, n.g(h - 2))
                            act.wait_ge(att_out[h % 2], 16 * n.g_like(h - 2))
                        for t in range(NT):
                            ins = act.activation(probs1[:, h % 2, t, :], scores[:, h % 2, t, :], ACT.Exp,
                                                 bias=nmax1[:, h % 2, t:t + 1])
                        ins.then_inc(e1_ready, 1)

                    def av_out(g, k):
                        done = ORDER * (n.g(g) - 1) + k
                        act.wait_ge(av_ps, done + 1)
                        for t in range(NT):
                            at = 2 * P + (done % 2) * P + t * D1
                            hh = g % H1
                            ins = act.activation(av[:, k, t, hh * D1:(hh + 1) * D1], bank[5][:, at:at + D1],
                                                 ACT.Copy, scale=rsum1[:, g % 2, t:t + 1])
                        ins.then_inc(av_ready, 1)

                    def point(p):
                        if old is not None:
                            tail(p)
                        if nxt is not None:
                            layer0(p)

                    if now is not None:
                        leave(flat(xnT1), flat(xnT), xnT_moved)
                        if nxt is not None:
                            act.wait_ge(xnT_moved, 1)
                    for h in range(H1):
                        if nxt is not None and now is None and h == H1 - 1:
                            qk_out(H1 // 2)
                        for f in n.fronts(h):
                            front_out(f)
                        if now is not None and h % 2 == 0 and (h < H1 - 2 or nxt is not None):
                            qk_out(h // 2 + 1)
                        for g in n.backs(h):
                            act.wait_ge(pT1_ps, n.g(g))
                            leave(flat(probsT1[:, g % 2]), bank[4][:, :], pT1_ready)
                        point(4 * h)
                        if now is not None:
                            exp1(h)
                        point(4 * h + 1)
                        for g in n.backs(h):
                            act.wait_ge(wT_ps, n.g(g))
                            leave(flat(bandT[:, g % 2]), bank[5][:, 0:NT * P], wT_ready)
                            av_out(g, 0)
                        point(4 * h + 2)
                        for g in n.backs(h):
                            av_out(g, 1)
                            av_out(g, 2)
                        point(4 * h + 3)
                        if h in TURN_AT and (old if TURN_AT[h] == 3 else now) is not None:
                            q = TURN_AT[h]
                            act.wait_ge(mT_ps, mixes_before(h + 1, old))
                            leave(flat(mixT[:, 2 * q:2 * q + 2]), bank[4][:, :], mT_ready)
                    turn_end(act, "act")

                all_turns(act, turn)

            @block.vector
            def _(dve):
                def turn(nxt, now, old):
                    n = Counts(nxt, now, old)
                    ch = Chain(dve, dve_steps)

                    def norm_stats(src, st, mv, ve, done):
                        for t in range(NT):
                            ch.step(dve.bn_stats(st[:, t, :], src[:, t, :]))
                        ch.after(ch.n)
                        for t in range(NT):
                            ch.step(dve.bn_aggr(mv[:, t, :], st[:, t, :]))
                        ch.after(ch.n)
                        dve.tensor_scalar(ve[:, :], mv[:, :, 1], EPS, None, ALU.add).then_inc(done, 1)

                    def norm_apply(k, src, dst, mv, rs, ready, done):
                        dve.wait_ge(ready, k + 1)
                        for t in range(NT):
                            dve.tensor_scalar(dst[:, t, :], src[:, t, :], mv[:, t, 0:1], rs[:, t:t + 1],
                                              ALU.subtract, ALU.mult).then_inc(done, 1)
                        dve.wait_ge(done, NT * (k + 1))

                    def stats0(src):
                        norm_stats(src, stats, meanvar, vareps, stats_ready)

                    def apply0(k, src, dst):
                        norm_apply(k, src, dst, meanvar, rstd, rstd_ready, xn_ready)

                    def layer0(p):
                        if p == NORM0:
                            dve.wait_ge(load_cur, 16)
                            stats0(cur)
                        if p == NORM0 + 1:
                            apply0(0, cur, xn)
                        if p == V0:
                            dve.wait_ge(v0_ps, 1)
                            for t in range(NT):
                                ins = dve.tensor_tensor(v0[:, t, :], bank[0][:, t * C:(t + 1) * C], bv0[:, :],
                                                        ALU.add)
                            ins.then_inc(v0_ready, 1)
                        k = p - HEADS0
                        if 0 <= k - 1 < H0:
                            h = k - 1
                            dve.wait_ge(s0_ps, h + 1)
                            if h >= 2:
                                dve.wait_ge(p0_ready, h - 1)
                            for t, a, z in ((0, 0, P), (1, P, 3 * P)):
                                ins = dve.tensor_reduce(nmax0[:, h % 2, t:t + 1], bank[6 + h % 2][:, a:z], AX.X,
                                                        ALU.max, negate=True)
                            ins.then_inc(max0_ready, 1)
                        if 0 <= k - 3 < H0 and (k - 3) % HPM == HPM - 1:
                            q = (k - 3) // HPM
                            hs = slice(q * HPM, (q + 1) * HPM)
                            dve.wait_ge(p0_ready, (q + 1) * HPM)
                            ch.link(dve.reciprocal(rsum0[:, :, hs], sum0[:, :, hs]))
                            dve.wait_ge(o0_ps, (q + 1) * HPM)
                            dve.tensor_tensor(
                                y0[:, :, :].rearrange("p t (h d) -> p t h d", d=D0)[:, :, hs, :],
                                bank[0][:, 3 * P:4 * P].rearrange("p (t h d) -> p t h d", t=NT, d=D0),
                                rsum0[:, :, hs].unsqueeze(3).to_broadcast([P, NT, HPM, D0]), ALU.mult)\
                                .then_inc(y0_ready, 1)
                        if p == ADD0:
                            dve.wait_ge(r0_ps, 1)
                            ch.link(dve.tensor_tensor(flat(cur), flat(cur), bank[7][:, :], ALU.add))
                            stats0(cur)
                        if p == NORM1:
                            apply0(1, cur, xn)
                            stats0(xn)
                        if p == NORM2:
                            apply0(2, xn, xn2)
                            ch.link(dve.tensor_tensor(flat(cur), flat(cur), flat(xn), ALU.add))
                        if p == ADDF:
                            dve.wait_ge(f2_ps, 1)
                            dve.scalar_tensor_tensor(out=flat(cur), in0=bank[6][:, :], scalar=0.5, in1=flat(cur),
                                                     op0=ALU.mult, op1=ALU.add).then_inc(cur_done, 1)
                            dve.wait_ge(cur_done, 1)
                            stats0(cur)
                        if p == NORM3:
                            apply0(3, cur, xn)
                        if p in (V1 + 1, V1 + 3):
                            t = (p - V1) // 2
                            for i in range(2):
                                dve.wait_ge(v1_ps, 2 * t + i + 1)
                                dve.tensor_tensor(v1_next[:, t, i * 512:(i + 1) * 512], bank[6 * i][:, :],
                                                  bv1[:, i * 512:(i + 1) * 512], ALU.add).then_inc(v1_ready, 1)

                    def tail(p):
                        if p == ADD1:
                            dve.wait_ge(load_end, 16)
                            dve.wait_ge(r1_ps, 1)
                            dve.tensor_tensor(flat(end), flat(end), bank[7][:, :], ALU.add).then_inc(end_done, 1)
                            dve.wait_ge(end_done, 1)
                            norm_stats(end, stats_e, meanvar_e, vareps_e, stats_end)
                        if p == NORM_END:
                            norm_apply(0, end, xn_end, meanvar_e, rstd_e, rstd_end_ready, xn_end_ready)
                        if p == GMAX:
                            dve.wait_ge(lg_ps, 1)
                            ch.link(dve.tensor_scalar(lg[:, :], bank[7][0:E1, 0:T], gate_b[:, :], None, ALU.add))
                            dve.tensor_reduce(gsum[:, 0:1], lg[:, :], AX.X, ALU.max, negate=True)\
                                .then_inc(gmax_ready, 1)
                        if p == GATES:
                            dve.wait_ge(gexp_ready, 1)
                            ch.link(dve.reciprocal(gsum[:, 2:3], gsum[:, 1:2]))
                            ch.link(dve.tensor_scalar(lg[:, :], lg[:, :], gsum[:, 2:3], None, ALU.mult))
                            ch.link(dve.max(top_g[:, :], lg[:, :]))
                            ch.link(dve.match_replace(rest[:, :], top_g[:, :], lg[:, :], 0.0))
                            dve.tensor_tensor(g_cur[:, :], lg[:, :], rest[:, :], ALU.subtract).then_inc(g_ready, 1)
                        if p == MCOPY:
                            dve.wait_ge(mg_ps, 1)
                            dve.tensor_copy(merged[:, :, :, bass.ds(old, 1)].rearrange("p c e b -> p (c e) b"),
                                            bank[7][:, 0:NC * E1].rearrange("p (n b) -> p n b", b=1))\
                                .then_inc(mg_kept, 1)

                    def point(p):
                        if old is not None:
                            tail(p)
                        if nxt is not None:
                            layer0(p)

                    def add_rel(f):
                        dve.wait_ge(s1_ps, n.f(f))
                        dve.wait_ge(rel_back[f % 2], 16 * n.f_like(f))
                        if f >= 2 and now is not None:
                            dve.wait_ge(e1_ready, f - 1)
                        dve.tensor_tensor(flat(scores[:, f % 2]), bank[1][:, :], flat(rel_in[:, f % 2]), ALU.add)\
                            .then_inc(s1_ready, 1)

                    def threshold(h):
                        if h >= 1:
                            dve.wait_ge(s1_ready, n.f(h))
                        if h >= 2:
                            dve.wait_ge(e1_ready, h - 1)
                        last = {}
                        for r in range(ROUNDS):
                            for t in range(NT):
                                src = scores[:, h % 2, t, :] if r == 0 else work[:, t, :]
                                if r:
                                    ch.after(last[t])
                                last[t] = ch.step(dve.max(top[:, h % 2, t, r, :], src))
                            if r == 0:
                                ch.after(ch.n)
                                dve.tensor_scalar(nmax1[:, h % 2, :], top[:, h % 2, :, 0, 0], -1.0, None,
                                                  ALU.mult).then_inc(max1_ready, 1)
                            if r < ROUNDS - 1:
                                for t in range(NT):
                                    src = scores[:, h % 2, t, :] if r == 0 else work[:, t, :]
                                    ch.after(last[t])
                                    last[t] = ch.step(dve.match_replace(work[:, t, :], top[:, h % 2, t, r, :],
                                                                        src, NEG))
                            if r % 2:
                                point(4 * h + r // 2)

                    def select(h):
                        dve.wait_ge(e1_ready, h + 1)
                        ch.after(ch.n)
                        for t in range(NT):
                            ins = dve.scalar_tensor_tensor(
                                out=probs1[:, h % 2, t, :], in0=scores[:, h % 2, t, :],
                                scalar=top[:, h % 2, t, ROUNDS - 1, 7:8], in1=probs1[:, h % 2, t, :],
                                op0=ALU.is_ge, op1=ALU.mult, accum_out=sum1[:, h % 2, t:t + 1])
                        ins.then_inc(p1_ready, 1)
                        dve.wait_ge(p1_ready, h + 1)
                        if h - 2 >= n.g0:
                            dve.wait_ge(av_ready, ORDER * n.g(h - 2))
                            dve.wait_ge(wT_ps, n.g(h - 2))
                        ch.step(dve.reciprocal(rsum1[:, h % 2, :], sum1[:, h % 2, :]))
                        for t in range(NT):
                            m = MAXREL + P * t
                            ins = dve.tensor_tensor_reduce(
                                work[:, t, 0:m], probs1[:, h % 2, t, 0:m], low_mask[:, t, 0:m], 1.0, 0.0,
                                ALU.mult, ALU.add, band[:, h % 2, t, BAND:P])
                        ins.then_inc(low_ready, 1)
                        dve.wait_ge(low_ready, h + 1)

                    for h in range(H1):
                        if now is not None:
                            threshold(h)
                        else:
                            for p in range(4 * h, 4 * h + 4):
                                point(p)
                        for f in n.fronts(h):
                            add_rel(f)
                        if now is not None:
                            select(h)
                    turn_end(dve, "dve")

                all_turns(dve, turn)

        if stop in ("att0", "ffn0", "att1"):
            return finish_copy(nc, ctx, h_mid if stop == "ffn0" else h_att, out, sem)

        expert_out = sb("expert_out", [P, NC, B, E1])
        with ExitStack() as stage:
            def ssb(name, shape, dt=F32):
                return stage.enter_context(nc.sbuf_tensor(name, shape, dt))

            w1 = [ssb(f"w1_{i}", [P, NC, HID]) for i in range(WBUFS)]
            w2 = [ssb(f"w2_{i}", [P, NH, C]) for i in range(WBUFS)]
            act_in = ssb("act_in", [P, 2, NH, B])
            act_out = ssb("act_out", [P, 2, NH, B])
            ex_cur = ssb("ex_cur", [P, 2, NC, E1])
            tokens = ssb("tokens", [P, 4, NT, C])
            o_b = ssb("o_b", [E1, 2, C])
            gates = ssb("gates", [E1, B, T])
            gates_loaded = sem("gates_loaded")
            w1_loaded = [sem(f"w1_loaded{i}") for i in range(WBUFS)]
            w2_loaded = [sem(f"w2_loaded{i}") for i in range(WBUFS)]
            up_ps = sem("expert_hidden_in_psum")
            biased = sem("expert_hidden_biased")
            gelu_ready = sem("expert_hidden_ready")
            down_ps = sem("expert_out_in_psum")
            down_ready = sem("expert_out_ready")
            tok_loaded = [sem(f"tokens_loaded{i}") for i in range(4)]
            picked = sem("outputs_picked")
            ot_ps = sem("outputsT_in_psum")
            ot_ready = sem("outputsT_ready")
            sc_ps = sem("scattered_in_psum")
            sum_ready = sem("tokens_ready")
            saved = sem("tokens_saved")
            TURNS = E1 // WBUFS

            block = stage.enter_context(nc.Block())

            @block.sync
            def _(sp):
                sp.dma_start(gates[:, :, :], gates_scr).then_inc(gates_loaded, 16)

                def load_up(j, e):
                    sp.dma_start(w1[j][:, :, :], A["w1"][bass.ds(e, 1), 0:C, :].rearrange(
                        "e (c p) n -> p (e c) n", p=P)).then_inc(w1_loaded[j], 16)

                def load_down(j, e):
                    sp.dma_start(w2[j][:, :, :], A["w2"][bass.ds(e, 1), 0:HID, :].rearrange(
                        "e (c p) n -> p (e c) n", p=P)).then_inc(w2_loaded[j], 16)

                for j in range(WBUFS):
                    load_up(j, j)
                    load_down(j, j)
                with sp.Fori(0, TURNS - 1) as i:
                    for j in range(WBUFS):
                        sp.wait_ge(up_ps, i * WBUFS + j + 1)
                        load_up(j, (i + 1) * WBUFS + j)
                        sp.wait_ge(down_ps, i * WBUFS + j + 1)
                        load_down(j, (i + 1) * WBUFS + j)

                def load_tokens(b):
                    sp.dma_start(tokens[:, b % 4, :, :], h_att[b * T:(b + 1) * T, :].rearrange(
                        "(t p) c -> p t c", p=P)).then_inc(tok_loaded[b % 4], 16)
                for b in range(4):
                    load_tokens(b)
                for b in range(B):
                    sp.wait_ge(sum_ready, b + 1)
                    sp.dma_start(out[b].rearrange("(t p) c -> p t c", p=P), tokens[:, b % 4, :, :])\
                        .then_inc(saved, 16)
                    if b + 4 < B:
                        sp.wait_ge(saved, 16 * (b + 1))
                        load_tokens(b + 4)
                sp.wait_ge(saved, 16 * B)

            @block.tensor
            def _(pe):
                with pe.Fori(0, TURNS) as i:
                    def up(j):
                        e = i * WBUFS + j
                        pe.wait_ge(w1_loaded[j], i * 16 + 16)
                        if j >= 2:
                            pe.wait_ge(biased, i * WBUFS + j - 1)
                        for k in range(NH):
                            for c in range(NC):
                                ins = pe.matmul(bank[j % 2][:, k * B:(k + 1) * B], w1[j][:, c, k * P:(k + 1) * P],
                                                merged[:, c, bass.ds(e, 1), :].rearrange("p e b -> p (e b)"),
                                                start=(c == 0), stop=(c == NC - 1))
                        ins.then_inc(up_ps, 1)

                    def down(j):
                        pe.wait_ge(gelu_ready, i * WBUFS + j + 1)
                        pe.wait_ge(w2_loaded[j], i * 16 + 16)
                        if j >= 2:
                            pe.wait_ge(down_ready, i * WBUFS + j - 1)
                        for c in range(NC):
                            for k in range(NH):
                                ins = pe.matmul(bank[2 + j % 2][:, c * B:(c + 1) * B],
                                                w2[j][:, k, c * P:(c + 1) * P], act_out[:, j % 2, k, :],
                                                start=(k == 0), stop=(k == NH - 1))
                        ins.then_inc(down_ps, 1)

                    up(0)
                    for j in range(WBUFS):
                        if j + 1 < WBUFS:
                            up(j + 1)
                        down(j)
                    pe.wait_ge(down_ready, (i + 1) * WBUFS)
                pe.wait_ge(gates_loaded, 16)
                for b in range(B):
                    pe.wait_ge(picked, b + 1)
                    for c in range(NC):
                        ins = pe.transpose(bank[4 + b % 2][0:E1, c * P:(c + 1) * P], ex_cur[:, b % 2, c, :],
                                           ident[:, :])
                    ins.then_inc(ot_ps, 1)
                    pe.wait_ge(ot_ready, b + 1)
                    if b >= 2:
                        pe.wait_ge(sum_ready, b - 1)
                    for t in range(NT):
                        ins = pe.matmul(bank[6 + b % 2][:, t * C:(t + 1) * C], gates[:, b, t * P:(t + 1) * P],
                                        o_b[:, b % 2, :], start=True, stop=True)
                    ins.then_inc(sc_ps, 1)

            @block.vector
            def _(dve):
                with dve.Fori(0, TURNS) as i:
                    def bias_up(j):
                        e = i * WBUFS + j
                        dve.wait_ge(up_ps, e + 1)
                        if j >= 2:
                            dve.wait_ge(gelu_ready, i * WBUFS + j - 1)
                        dve.tensor_tensor(act_in[:, j % 2, :, :],
                                          bank[j % 2][:, 0:NH * B].rearrange("p (k b) -> p k b", b=B),
                                          b1_all[:, bass.ds(e, 1), :].rearrange("p e k -> p (e k)")
                                          .unsqueeze(2).to_broadcast([P, NH, B]), ALU.add).then_inc(biased, 1)

                    bias_up(0)
                    for j in range(WBUFS):
                        e = i * WBUFS + j
                        if j + 1 < WBUFS:
                            bias_up(j + 1)
                        dve.wait_ge(down_ps, e + 1)
                        dve.tensor_tensor(
                            expert_out[:, :, :, bass.ds(e, 1)].rearrange("p c b e -> p c (b e)"),
                            bank[2 + j % 2][:, 0:NC * B].rearrange("p (c b) -> p c b", b=B),
                            b2_all[:, bass.ds(e, 1), :].rearrange("p e c -> p (e c)")
                            .unsqueeze(2).to_broadcast([P, NC, B]), ALU.add).then_inc(down_ready, 1)
                    dve.wait_ge(gelu_ready, (i + 1) * WBUFS)
                dve.wait_ge(down_ready, E1)
                for b in range(B + 1):
                    if b < B:
                        if b >= 2:
                            dve.wait_ge(ot_ps, b - 1)
                        dve.tensor_copy(ex_cur[:, b % 2, :, :], expert_out[:, :, b, :]).then_inc(picked, 1)
                    if b >= 1:
                        a = b - 1
                        dve.wait_ge(sc_ps, a + 1)
                        dve.wait_ge(tok_loaded[a % 4], 16 * (a // 4 + 1))
                        flat = tokens[:, a % 4, :, :].rearrange("p t c -> p (t c)")
                        dve.tensor_tensor(flat, flat, bank[6 + a % 2][:, :], ALU.add).then_inc(sum_ready, 1)

            @block.scalar
            def _(act):
                with act.Fori(0, TURNS) as i:
                    for j in range(WBUFS):
                        act.wait_ge(biased, i * WBUFS + j + 1)
                        if j >= 2:
                            act.wait_ge(down_ps, i * WBUFS + j - 1)
                        act.activation(act_out[:, j % 2, :, :].rearrange("p k b -> p (k b)"),
                                       act_in[:, j % 2, :, :].rearrange("p k b -> p (k b)"), ACT.Gelu)\
                            .then_inc(gelu_ready, 1)
                    act.wait_ge(down_ps, (i + 1) * WBUFS)
                for b in range(B):
                    act.wait_ge(ot_ps, b + 1)
                    if b >= 2:
                        act.wait_ge(sc_ps, b - 1)
                    act.activation(o_b[:, b % 2, :], bank[4 + b % 2][0:E1, 0:C], ACT.Copy).then_inc(ot_ready, 1)


def rows_of(j):
    return BR * C >> 2 * j


def flat(x):
    a = x if isinstance(x, bass.AP) else x[tuple(slice(None) for _ in x.shape)]
    return a.rearrange("p a b -> p (a b)")


def rows(x, b):
    return x[bass.ds(b * T, T), :].rearrange("(t p) c -> p t c", p=P)


def mixes_before(h, old):
    return sum(at < h for at in (2, 7, 11, 15)) - (old is None and h > 2)


def skewed(scr, half, col, step, n, tile_step=0):
    a = scr[half].rearrange("t p x -> p t x")
    return bass.AP(tensor=a.tensor, offset=a.offset + col,
                   ap=[[PITCH + step, P], [P * PITCH + tile_step, NT], [1, n]])


def finish_copy(nc, ctx, src, out, sem):
    s = sem("copied")
    with nc.Block() as block:
        @block.sync
        def _(sp):
            sp.dma_start(out.rearrange("b t c -> (b t) c"), src).then_inc(s, 16)
            sp.wait_ge(s, 16)


def layout(inputs):
    import numpy as np
    f = {k: np.asarray(v) for k, v in inputs.items()}
    a = {}
    a["x"] = f["x"][..., 0]
    for j, name, n in ((1, "Wd3", BR // 2), (2, "Wd2", BR // 4), (3, "Wd1", BR // 8)):
        w = f["L0_tok_" + name].reshape(3, RB, n, C >> j, 3)
        a[f"wdet{j}"] = np.ascontiguousarray(w.transpose(1, 4, 0, 2, 3)).reshape(RB, 3, -1)
    a["wapp"] = f["L0_tok_Wa"].reshape(RB, C >> 3)
    a["dbias"] = np.concatenate([f["L0_tok_bd3"], f["L0_tok_bd2"], f["L0_tok_bd1"], f["L0_tok_ba"]])
    w, b = f["L0_attn_W_attn"], f["L0_attn_b_attn"]
    wqk = np.zeros((C, 2 * MQ * HPM, SLOT), w.dtype)
    wqk[:, :, :D0] = w[:2 * C].T.reshape(C, 2 * H0, D0)
    a["wqk0"] = wqk.reshape(C, -1)
    bqk = np.zeros((2 * H0, SLOT), b.dtype)
    bqk[:, :D0] = b[:2 * C].reshape(2 * H0, D0)
    a["bqk0"] = np.ascontiguousarray(bqk.reshape(2 * MQ, P).T)
    a["wv0"] = np.ascontiguousarray(w[2 * C:].T)
    a["bv0"] = b[2 * C:]
    a["wp0"] = np.ascontiguousarray(f["L0_attn_W_proj"].T)
    a["bp0"] = f["L0_attn_b_proj"]
    a["gamma"] = np.ascontiguousarray(f["L0_ffn_ln_gamma"].reshape(NC, P).T)
    a["beta"] = np.ascontiguousarray(f["L0_ffn_ln_beta"].reshape(NC, P).T)
    a["fc1_q"] = f["L0_ffn_fc1_q"]
    a["fc2_q"] = f["L0_ffn_fc2_q"]
    a["fc1_s"] = f["L0_ffn_fc1_scales"]
    a["fc2_s"] = f["L0_ffn_fc2_scales"]
    a["fc1b"] = np.ascontiguousarray(f["L0_ffn_fc1_bias"].reshape(NF, P).T)
    a["fc2b"] = f["L0_ffn_fc2_bias"]
    w, b = f["L1_attn_Wqkv"], f["L1_attn_bqkv"]
    a["wqk1"] = np.ascontiguousarray(w[:2 * INNER].T)
    a["bqk1"] = np.ascontiguousarray(b[:2 * INNER].reshape(-1, P).T)
    a["wv1"] = np.ascontiguousarray(w[2 * INNER:].T)
    a["bv1"] = b[2 * INNER:]
    a["wo1"] = np.ascontiguousarray(f["L1_attn_Wout"].T)
    a["bo1"] = f["L1_attn_bout"]
    at = np.clip(-(np.arange(EXTN) - (T - 1)), -MAXREL, MAXREL) + MAXREL
    a["rel_k"] = np.ascontiguousarray(np.concatenate([f["L1_attn_rel_k_emb"][at].T] * 2))
    a["rel_v"] = f["L1_attn_rel_v_emb"][np.concatenate([2 * MAXREL - 1 - np.arange(BAND), [2 * MAXREL]])]
    a["relv0"] = f["L1_attn_rel_v_emb"][0]
    a["alphas"] = f["L1_attn_alphas_raw"]
    a["gate_w"] = np.ascontiguousarray(f["L1_ffn_gate_w"].T)
    a["gate_b"] = f["L1_ffn_gate_b"]
    w1, w2 = f["L1_ffn_w1"], f["L1_ffn_w2"]
    a["w1"] = w1
    a["w2"] = w2
    a["b1"] = np.ascontiguousarray(w1[:, C].reshape(E1, NH, P).transpose(2, 0, 1))
    a["b2"] = np.ascontiguousarray(w2[:, HID].reshape(E1, NC, P).transpose(2, 0, 1))
    return {k: np.ascontiguousarray(v) for k, v in a.items()}


def kernel(**inputs):
    import numpy as _np
    import concourse.bacc as _bacc
    from concourse import mybir as _mybir
    from concourse.bass_utils import run_bass_kernel_spmd as _run

    nc = _bacc.Bacc("TRN2", target_bir_lowering=False, num_devices=1)
    arrays = {f"in_{k}": v for k, v in layout(inputs).items()}
    aps = {k[3:]: nc.dram_tensor(k, v.shape, _mybir.dt.from_np(v.dtype), kind="ExternalInput").ap()
           for k, v in arrays.items()}
    out = nc.dram_tensor("out_tokens", (B, T, C), _mybir.dt.from_np(_np.dtype("float32")),
                         kind="ExternalOutput").ap()
    build(nc, aps, out)
    r = _run(nc, [arrays], core_ids=[0])
    return r.results[0]["out_tokens"]
```

```python
from contextlib import ExitStack

import concourse.bass as bass
from concourse import mybir

ALU = mybir.AluOpType
ACT = mybir.ActivationFunctionType
AX = mybir.AxisListType
F32 = mybir.dt.float32
BF16 = mybir.dt.bfloat16
I32 = mybir.dt.int32

P = 128
B = 16
T = 256
C = 256
NT = T // P
NC = C // P
EPS = 1e-5
NEG = -1e30

IMGS = 4
GROUPS = B // IMGS
RB = 32
BR = T // RB
LEVELS = 3

H0, D0, SLOT = 16, 16, 32
HPM = P // SLOT
MQ = H0 // HPM

F0 = 1024
NF = F0 // P

H1, D1 = 16, 64
INNER = H1 * D1
MAXREL = 64
TOPK = T // 4
ROUNDS = TOPK // 8
EXTW = 3 * P - 1
NREL = 2 * MAXREL + 1
PITCH = 3 * P
BAND = 2 * MAXREL - 1
ORDER = 3

E1, HID, K1 = 32, 1024, 8
NH = HID // P
WBUFS = 4


class Chain:

    def __init__(self, eng, sem):
        self.eng, self.sem, self.n = eng, sem, 0

    def step(self, ins):
        self.n += 1
        ins.then_inc(self.sem, 1)
        return self.n

    def link(self, ins):
        self.step(ins)
        self.eng.wait_ge(self.sem, self.n)

    def after(self, n):
        self.eng.wait_ge(self.sem, n)


def build(nc, A, out, stop="", dbg=None):
    with ExitStack() as ctx:
        def sb(name, shape, dt=F32):
            return ctx.enter_context(nc.sbuf_tensor(name, shape, dt))

        def sem(name):
            return ctx.enter_context(nc.semaphore(name))

        def dram(name, shape):
            return nc.dram_tensor(name, shape, F32, kind="Internal").ap()

        bank = [ctx.enter_context(nc.psum_tensor(f"bank{i}", [P, 512], F32)) for i in range(8)]

        h_tok = dram("h_tok", (B * T, C))
        h_mid = dram("h_mid", (B * T, C))
        h_att = dram("h_att", (B * T, C))
        gates_scr = dram("gates_scr", (E1, B, T))
        expert_scr = dram("expert_scr", (B, E1, C))
        rel_scr = dram("rel_scr", (2, NT, P, PITCH))
        att_scr = dram("att_scr", (2, NT, P, PITCH))

        ident = sb("ident", [P, P])
        ident_b = sb("ident_b", [P, P], BF16)
        causal = sb("causal", [P, P], BF16)
        ones = sb("ones", [P, P])
        zeros = sb("zeros", [P, P])
        block_ones = sb("block_ones", [P, P])
        mhalf = sb("mhalf", [P, NT])
        low_mask = sb("low_mask", [P, NT, 192])

        wqk0 = sb("wqk0", [P, NC, 2 * MQ * P])
        wv0 = sb("wv0", [P, NC, C])
        wp0 = sb("wp0", [P, NC, C])
        bqk0 = sb("bqk0", [P, 2 * MQ])
        bv0 = sb("bv0", [P, C])
        bp0 = sb("bp0", [1, C])
        gamma = sb("gamma", [P, NC])
        beta = sb("beta", [P, NC])
        fc1 = sb("fc1", [P, NC, F0])
        fc2 = sb("fc2", [P, NF, C])
        fc1b = sb("fc1b", [P, NF])
        fc2b = sb("fc2b", [1, C])
        wqk1 = sb("wqk1", [P, NC, 2 * INNER])
        wv1 = sb("wv1", [P, NC, INNER])
        bqk1 = sb("bqk1", [P, 2 * (INNER // P)])
        bv1 = sb("bv1", [P, INNER])
        wo1 = sb("wo1", [P, INNER // P, C])
        bo1 = sb("bo1", [1, C])
        rel_k = sb("rel_k", [P, NREL])
        rel_v = sb("rel_v", [P, D1])
        relv0 = sb("relv0", [P, D1])
        alphas = sb("alphas", [P, ORDER, H1])
        gate = sb("gate", [P, NC, E1])
        gate_b = sb("gate_b", [E1, 1])
        b1_all = sb("b1_all", [P, E1, NH])

        cur = sb("cur", [P, NT, C])
        stats = sb("stats", [P, NT, 6])
        meanvar = sb("meanvar", [P, NT, 2])
        vareps = sb("vareps", [P, NT])
        rstd = sb("rstd", [P, NT])
        xn = sb("xn", [P, NT, C])
        xn2 = sb("xn2", [P, NT, C])
        xnT = sb("xnT", [P, NC, T])

        s_load = sem("weights_loaded")
        s_const = sem("consts_ready")

        def bcast(ap, n=P):
            return ap.partition_broadcast(n)

        loads = [
            (wqk0[:, :, :], A["wqk0"].rearrange("(c p) n -> p c n", p=P)),
            (wv0[:, :, :], A["wv0"].rearrange("(c p) n -> p c n", p=P)),
            (wp0[:, :, :], A["wp0"].rearrange("(c p) n -> p c n", p=P)),
            (bqk0[:, :], A["bqk0"]),
            (bv0[:, :], bcast(A["bv0"])),
            (bp0[:, :], A["bp0"].rearrange("(a n) -> a n", a=1)),
            (gamma[:, :], A["gamma"]),
            (beta[:, :], A["beta"]),
            (fc1b[:, :], A["fc1b"]),
            (fc2b[:, :], A["fc2b"].rearrange("(a n) -> a n", a=1)),
            (wqk1[:, :, :], A["wqk1"].rearrange("(c p) n -> p c n", p=P)),
            (wv1[:, :, :], A["wv1"].rearrange("(c p) n -> p c n", p=P)),
            (bqk1[:, :], A["bqk1"]),
            (bv1[:, :], bcast(A["bv1"])),
            (wo1[:, :, :], A["wo1"].rearrange("(c p) n -> p c n", p=P)),
            (bo1[:, :], A["bo1"].rearrange("(a n) -> a n", a=1)),
            (rel_k[:, :], A["rel_k"]),
            (rel_v[:, :], A["rel_v"]),
            (relv0[:, :], bcast(A["relv0"])),
            (alphas[:, :, :], bcast(A["alphas"])),
            (gate[:, :, :], A["gate_w"].rearrange("(c p) n -> p c n", p=P)),
            (gate_b[:, :], A["gate_b"].rearrange("(a n) -> a n", n=1)),
            (b1_all[:, :, :], A["b1"]),
        ]

        with ExitStack() as stage:
            def ssb(name, shape, dt=F32):
                return stage.enter_context(nc.sbuf_tensor(name, shape, dt))

            q1 = ssb("q1", [P, NC, F0], I32)
            q2 = ssb("q2", [P, NF, C], I32)
            sc1 = ssb("sc1", [P, NC, F0])
            sc2 = ssb("sc2", [P, NF, C])
            wdet = [None] + [ssb(f"wdet{j}", [P, 3, 3 * BR * C >> 2 * j]) for j in (1, 2, 3)]
            wapp = ssb("wapp", [P, BR * C >> 6])
            dbias = ssb("dbias", [P, 10])
            img = ssb("img", [P, 2, BR, C])
            lo = ssb("lo", [P, BR * C // 2])
            hi = ssb("hi", [P, BR * C // 2])
            app = [None] + [ssb(f"app{j}", [P, BR * C >> 2 * j]) for j in (1, 2, 3)]
            det = [None] + [ssb(f"det{j}", [P, 3, BR * C >> 2 * j]) for j in (1, 2, 3)]
            junk = ssb("junk", [P, 3 * BR * C // 4])
            dots = ssb("dots", [P, 10])
            logit = ssb("logit", [P, 10])
            top3 = ssb("top3", [P, 3])
            expo = ssb("expo", [P, 10])
            den = ssb("den", [P, 4])
            wts = ssb("wts", [P, 10])
            wpos = ssb("wpos", [P, 10])
            wneg = ssb("wneg", [P, 10])
            s_img = [sem(f"image_loaded{i}") for i in range(2)]
            s_dots = sem("dots_ready")
            s_sums = sem("dot_sums_ready")
            s_logit = sem("logits_ready")
            s_exp = sem("tok_exp_ready")
            s_rec = sem("image_rebuilt")
            s_saved = sem("image_saved")
            s_dve = sem("tok_vector_steps")
            s_q = sem("quantized_loaded")

            tok_loads = [
                (wdet[j][RB * i:RB * i + RB, :, :], A[f"wdet{j}"]) for j in (1, 2, 3) for i in range(IMGS)
            ] + [(wapp[RB * i:RB * i + RB, :], A["wapp"]) for i in range(IMGS)] + [
                (dbias[:, :], bcast(A["dbias"]))
            ]
            q_loads = [
                (q1[:, :, :], A["fc1_q"].rearrange("(c p) n -> p c n", p=P)),
                (q2[:, :, :], A["fc2_q"].rearrange("(c p) n -> p c n", p=P)),
                (sc1[:, :, :], bcast(A["fc1_s"])),
                (sc2[:, :, :], bcast(A["fc2_s"])),
            ]
            s_tokw = sem("tok_weights_loaded")

            block = stage.enter_context(nc.Block())

            @block.sync
            def _(sp):
                def load(g):
                    sp.dma_start(img[:, g % 2, :, :], A["x"][IMGS * g:IMGS * (g + 1)].rearrange(
                        "i (r k) c -> (i r) k c", k=BR)).then_inc(s_img[g % 2], 16)
                load(0)
                for dst, src in tok_loads:
                    sp.dma_start(dst, src).then_inc(s_tokw, 16)
                load(1)
                for dst, src in q_loads:
                    sp.dma_start(dst, src).then_inc(s_q, 16)
                for dst, src in loads:
                    sp.dma_start(dst, src).then_inc(s_load, 16)
                for g in range(GROUPS):
                    sp.wait_ge(s_rec, g + 1)
                    sp.dma_start(h_tok[g * IMGS * T:(g + 1) * IMGS * T, :].rearrange(
                        "(q k) c -> q k c", k=BR), img[:, g % 2, :, :]).then_inc(s_saved, 16)
                    if g + 2 < GROUPS:
                        sp.wait_ge(s_saved, 16 * (g + 1))
                        load(g + 2)
                sp.wait_ge(s_const, 3)
                for par in range(2):
                    for t in range(NT):
                        for off in (0, PITCH - MAXREL):
                            sp.dma_start(att_scr[par, t, :, off:off + MAXREL],
                                         zeros[:, 0:MAXREL]).then_inc(s_saved, 16)
                sp.wait_ge(s_saved, 16 * (GROUPS + 4 * NT))
                sp.wait_ge(s_load, 16 * len(loads))

            @block.gpsimd
            def _(pool):
                pool.memset(ident[:, :], 0.0).then_inc(s_const, 1)
                pool.memset(ones[:, :], 1.0).then_inc(s_const, 1)
                pool.memset(zeros[:, :], 0.0).then_inc(s_const, 1)
                pool.memset(block_ones[:, :], 0.0).then_inc(s_const, 1)
                pool.memset(mhalf[:, :], -0.5).then_inc(s_const, 1)
                pool.memset(causal[:, :], 0.0).then_inc(s_const, 1)
                pool.memset(low_mask[:, :, :], 1.0).then_inc(s_const, 1)
                pool.wait_ge(s_const, 7)
                pool.affine_select(out=ident[:, :], in_=ident[:, :], compare_op=ALU.not_equal, fill=1.0,
                                   base=0, pattern=[[-1, P]], channel_multiplier=1).then_inc(s_const, 1)
                pool.affine_select(out=causal[:, :], in_=causal[:, :], compare_op=ALU.is_ge, fill=NEG,
                                   base=0, pattern=[[-1, P]], channel_multiplier=1).then_inc(s_const, 1)
                for t in range(NT):
                    pool.affine_select(out=low_mask[:, t, :], in_=low_mask[:, t, :], compare_op=ALU.is_ge,
                                       fill=0.0, base=P * t - MAXREL, pattern=[[-1, 192]],
                                       channel_multiplier=1).then_inc(s_const, 1)
                for i in range(IMGS):
                    pool.wait_ge(s_const, 11 + i)
                    pool.memset(block_ones[RB * i:RB * (i + 1), RB * i:RB * (i + 1)], 1.0).then_inc(s_const, 1)
                pool.wait_ge(s_const, 15)
                pool.tensor_copy(ident_b[:, :], ident[:, :]).then_inc(s_const, 1)

            @block.tensor
            def _(pe):
                pe.wait_ge(s_const, 16)
                for g in range(GROUPS):
                    pe.wait_ge(s_dots, g + 1)
                    pe.matmul(bank[0][:, 0:10], block_ones[:, :], dots[:, :], start=True,
                              stop=True).then_inc(s_sums, 1)

            @block.scalar
            def _(act):
                for g in range(GROUPS):
                    act.wait_ge(s_logit, g + 1)
                    act.activation(expo[:, :], logit[:, :], ACT.Exp).then_inc(s_exp, 1)
                act.wait_ge(s_load, 16 * len(loads))
                flat = alphas[:, :, :].rearrange("p k h -> p (k h)")
                act.activation(flat, flat, ACT.Exp, scale=-1.0).then_inc(s_exp, 1)

            @block.vector
            def _(dve):
                ch = Chain(dve, s_dve)
                dve.wait_ge(s_tokw, 16 * len(tok_loads))
                for g in range(GROUPS):
                    dve.wait_ge(s_img[g % 2], 16 * (g // 2 + 1))
                    cur_a, rows, cols = img[:, g % 2, :, :].rearrange("p k c -> p (k c)"), BR, C
                    for j in (1, 2, 3):
                        n = rows * cols
                        pair = cur_a.rearrange("p (n e) -> p n e", e=2)
                        ch.step(dve.tensor_tensor(lo[:, 0:n // 2], pair[:, :, 0], pair[:, :, 1], ALU.add))
                        ch.link(dve.tensor_tensor(hi[:, 0:n // 2], pair[:, :, 0], pair[:, :, 1], ALU.subtract))
                        rows, cols = rows // 2, cols // 2
                        for src, dst_sum, dst_dif in ((lo, app[j][:, :], det[j][:, 0, :]),
                                                      (hi, det[j][:, 1, :], det[j][:, 2, :])):
                            v = src[:, 0:n // 2].rearrange("p (r e c) -> p r e c", e=2, c=cols)
                            for dst, op in ((dst_sum, ALU.add), (dst_dif, ALU.subtract)):
                                ch.step(dve.tensor_tensor(dst.rearrange("p (r c) -> p r c", c=cols),
                                                          v[:, :, 0, :], v[:, :, 1, :], op))
                        ch.after(ch.n)
                        cur_a = app[j][:, :]
                    for j in (1, 2, 3):
                        for o in range(3):
                            ch.link(dve.tensor_tensor_reduce(
                                junk[:, 0:3 * rows_of(j)], det[j][:, :, :].rearrange("p b n -> p (b n)"),
                                wdet[j][:, o, :], 0.5 ** j, 0.0, ALU.mult, ALU.add,
                                dots[:, 3 * (j - 1) + o:3 * (j - 1) + o + 1]))
                    dve.tensor_tensor_reduce(junk[:, 0:rows_of(3)], app[3][:, :], wapp[:, :], 0.125, 0.0,
                                             ALU.mult, ALU.add, dots[:, 9:10]).then_inc(s_dots, 1)
                    dve.wait_ge(s_sums, g + 1)
                    ch.link(dve.tensor_tensor(logit[:, :], bank[0][:, 0:10], dbias[:, :], ALU.add))
                    ch.link(dve.tensor_reduce(top3[:, :], logit[:, 0:9].rearrange("p (j o) -> p j o", o=3),
                                              AX.X, ALU.max))
                    ch.step(dve.tensor_tensor(logit[:, 0:9].rearrange("p (j o) -> p j o", o=3),
                                              logit[:, 0:9].rearrange("p (j o) -> p j o", o=3),
                                              top3[:, :].unsqueeze(2).to_broadcast([P, 3, 3]), ALU.subtract))
                    ch.link(dve.tensor_scalar(logit[:, 9:10], logit[:, 9:10], -1.0, None, ALU.mult))
                    dve.tensor_copy(top3[:, 0:1], logit[:, 9:10]).then_inc(s_logit, 1)
                    dve.wait_ge(s_exp, g + 1)
                    ch.step(dve.tensor_reduce(den[:, 0:3], expo[:, 0:9].rearrange("p (j o) -> p j o", o=3),
                                              AX.X, ALU.add))
                    ch.link(dve.tensor_scalar(den[:, 3:4], expo[:, 9:10], 1.0, None, ALU.add))
                    ch.link(dve.reciprocal(den[:, :], den[:, :]))
                    ch.step(dve.tensor_tensor(wts[:, 0:9].rearrange("p (j o) -> p j o", o=3),
                                              expo[:, 0:9].rearrange("p (j o) -> p j o", o=3),
                                              den[:, 0:3].unsqueeze(2).to_broadcast([P, 3, 3]), ALU.mult))
                    ch.link(dve.tensor_scalar(wts[:, 9:10], den[:, 3:4], 1.0, None, ALU.mult))
                    for j in (1, 2, 3):
                        for sign, dst in ((1.0, wpos), (-1.0, wneg)):
                            ch.step(dve.tensor_scalar(dst[:, 3 * (j - 1):3 * j], wts[:, 3 * (j - 1):3 * j],
                                                      sign * 0.25 ** j, None, ALU.mult))
                    ch.link(dve.tensor_scalar(wpos[:, 9:10], wts[:, 9:10], 0.25 ** 3, None, ALU.mult))
                    ch.link(dve.tensor_scalar(app[3][:, :], app[3][:, :], wpos[:, 9:10], None, ALU.mult))
                    for j in (3, 2, 1):
                        rows, cols = BR >> j, C >> j
                        a = app[j][:, :].rearrange("p (r c) -> p r c", c=cols)
                        w = [(wpos[:, 3 * (j - 1) + o:3 * (j - 1) + o + 1],
                              wneg[:, 3 * (j - 1) + o:3 * (j - 1) + o + 1]) for o in range(3)]
                        h, v, d = (det[j][:, o, :].rearrange("p (r c) -> p r c", c=cols) for o in range(3))
                        lov = lo[:, 0:2 * rows * cols].rearrange("p (r e c) -> p r e c", e=2, c=cols)
                        hiv = hi[:, 0:2 * rows * cols].rearrange("p (r e c) -> p r e c", e=2, c=cols)
                        ch.step(dve.tensor_scalar(v, v, w[1][0], None, ALU.mult))
                        for e in range(2):
                            ch.step(dve.scalar_tensor_tensor(out=lov[:, :, e, :], in0=h, scalar=w[0][e], in1=a,
                                                             op0=ALU.mult, op1=ALU.add))
                        ch.after(ch.n)
                        for e in range(2):
                            ch.step(dve.scalar_tensor_tensor(out=hiv[:, :, e, :], in0=d, scalar=w[2][e], in1=v,
                                                             op0=ALU.mult, op1=ALU.add))
                        ch.after(ch.n)
                        if j > 1:
                            up = app[j - 1][:, :].rearrange("p (n e) -> p n e", e=2)
                        else:
                            up = img[:, g % 2, :, :].rearrange("p k (c e) -> p (k c) e", e=2)
                        n = 2 * rows * cols
                        ch.step(dve.tensor_tensor(up[:, :, 0], lo[:, 0:n], hi[:, 0:n], ALU.add))
                        ins = dve.tensor_tensor(up[:, :, 1], lo[:, 0:n], hi[:, 0:n], ALU.subtract)
                        if j > 1:
                            ch.link(ins)
                    ins.then_inc(s_rec, 1)
                    dve.wait_ge(s_rec, g + 1)
                    ch.after(ch.n)
                dve.wait_ge(s_q, 16 * len(q_loads))
                for w, q, s in ((fc1, q1, sc1), (fc2, q2, sc2)):
                    ch.link(dve.tensor_scalar(w[:, :, :], q[:, :, :], -128.0, None, ALU.add))
                    ch.link(dve.tensor_tensor(w[:, :, :], w[:, :, :], s[:, :, :], ALU.mult))
                dve.wait_ge(s_load, 16 * len(loads))
                ch.link(dve.tensor_scalar(bqk0[:, 0:MQ], bqk0[:, 0:MQ], 1.0 / D0, None, ALU.mult))
                n1 = INNER // P
                ch.link(dve.tensor_scalar(bqk1[:, n1:2 * n1], bqk1[:, n1:2 * n1], D1 ** -0.5, None, ALU.mult))
                rv = bv1[:, :].rearrange("p (h d) -> p h d", d=D1)
                ch.step(dve.tensor_tensor(rv, rv, relv0[:, :].unsqueeze(1).to_broadcast([P, H1, D1]), ALU.add))
                ch.step(dve.tensor_tensor(rel_v[:, :], rel_v[:, :], relv0[:, :], ALU.subtract))
                dve.wait_ge(s_exp, GROUPS + 1)
                ch.link(dve.tensor_scalar(alphas[:, :, :], alphas[:, :, :], 1.0, None, ALU.add))
                ch.link(dve.reciprocal(alphas[:, :, :], alphas[:, :, :]))

        if stop == "tok":
            return finish_copy(nc, ctx, h_tok, out, sem)
        body = {}

        def bsem(name):
            body[name] = sem(name)
            return body[name]

        load_cur = bsem("layer0_tokens_loaded")
        stats_ready = bsem("stats_ready")
        rstd_ready = bsem("rstd_ready")
        xn_ready = bsem("xn_ready")
        xnT_ps = bsem("xnT_in_psum")
        xnT_ready = bsem("xnT_ready")
        pool_steps = bsem("pool_steps")
        dve_steps = bsem("vector_steps")
        qk0_ps = bsem("qk0_in_psum")
        qk0_ready = bsem("qk0_ready")
        v0_ps = bsem("v0_in_psum")
        v0_ready = bsem("v0_ready")
        s0_ps = bsem("scores0_in_psum")
        max0_ready = bsem("rowmax0_ready")
        p0_ready = bsem("probs0_ready")
        pT0_ps = bsem("probsT0_in_psum")
        pT0_ready = bsem("probsT0_ready")
        o0_ps = bsem("heads0_in_psum")
        o0_ready = bsem("heads0_left_psum")
        y0_ready = bsem("attended0_ready")
        yT0_ps = bsem("attendedT0_in_psum")
        yT0_ready = bsem("attendedT0_ready")
        r0_ps = bsem("projected0_in_psum")
        f1_ps = bsem("hidden_in_psum")
        f1_ready = bsem("hidden_ready")
        f2_ps = bsem("ffn_in_psum")
        cur_done = bsem("layer0_done")
        cur_saved = bsem("layer0_saved")
        v1_ps = bsem("v1_in_psum")
        v1_moved = bsem("v1_moved")
        xnT_moved = bsem("xnT_moved")
        qk1_ps = bsem("qk1_in_psum")
        qk1_ready = bsem("qk1_ready")
        rel_ps = bsem("rel_in_psum")
        rel_ready = bsem("rel_ready")
        rel_out = [bsem(f"rel_written{i}") for i in range(2)]
        rel_back = [bsem(f"rel_read{i}") for i in range(2)]
        s1_ps = bsem("scores1_in_psum")
        s1_ready = bsem("scores1_ready")
        max1_ready = bsem("rowmax1_ready")
        e1_ready = bsem("exp1_ready")
        p1_ready = bsem("probs1_ready")
        low_ready = bsem("low_clip_ready")
        att_out = [bsem(f"att_written{i}") for i in range(2)]
        att_back = [bsem(f"att_read{i}") for i in range(2)]
        pT1_ps = bsem("probsT1_in_psum")
        pT1_ready = bsem("probsT1_ready")
        wT_ps = bsem("bandT_in_psum")
        wT_ready = bsem("bandT_ready")
        av_ps = bsem("av_in_psum")
        av_ready = bsem("av_ready")
        mix_ready = bsem("orders_mixed")
        mT_ps = bsem("mixedT_in_psum")
        mT_ready = bsem("mixedT_ready")
        load_end = bsem("tail_tokens_loaded")
        r1_ps = bsem("projected1_in_psum")
        end_done = bsem("attention1_done")
        end_saved = bsem("attention1_saved")
        stats_end = bsem("tail_stats_ready")
        rstd_end_ready = bsem("tail_rstd_ready")
        xn_end_ready = bsem("tail_xn_ready")
        xnT_end_ps = bsem("tail_xnT_in_psum")
        xnT_end_ready = bsem("tail_xnT_ready")
        lg_ps = bsem("gate_logits_in_psum")
        gmax_ready = bsem("gate_max_ready")
        gexp_ready = bsem("gate_exp_ready")
        g_ready = bsem("gates_ready")
        gT_ps = bsem("gatesT_in_psum")
        gT_ready = bsem("gatesT_ready")
        mg_ps = bsem("merged_in_psum")
        mg_kept = bsem("merged_kept")
        body_sems = sorted(s.num for s in body.values())
        assert body_sems == list(range(body_sems[0], body_sems[0] + len(body_sems)))
        arrived = sem("engines_at_turn_end")
        go = {n: sem(f"next_turn_{n}") for n in ("pool", "act", "dve", "pe")}

        merged = sb("merged", [P, NC, E1, B])

        def turn_end(eng, name):
            eng.drain().then_inc(arrived, 1)
            eng.wait_ge(go[name], 1)
            eng.sem_clear(go[name])

        def all_turns(eng, turn):
            turn(0, None, None)
            turn(1, 0, None)
            with eng.Fori(1, B - 1) as b:
                turn(b + 1, b, b - 1)
            turn(None, B - 1, B - 2)
            turn(None, None, B - 1)

        class Counts:

            def __init__(self, nxt, now, old):
                self.f0, self.f1 = (1 if now is not None else H1), (H1 if nxt is not None else H1 - 1)
                self.pair0 = 1 if now is not None else H1 // 2
                self.g0, self.g1 = (-1 if old is not None else 0), (H1 - 2 if now is not None else -1)

            def fronts(self, h):
                return [h + 1] if self.f0 <= h + 1 <= self.f1 else []

            def rels_early(self, h):
                return [f for f in self.fronts(h) if f == self.f0]

            def rels_ahead(self, h):
                return [h + 2] if self.f0 < h + 2 <= self.f1 else []

            def makes_pair(self, h):
                return h % 2 == 0 and 2 * self.pair0 <= h + 2 <= self.f1

            def backs(self, h):
                return [h - 1] if self.g0 <= h - 1 <= self.g1 else []

            def f(self, f):
                return f - self.f0 + 1

            def g(self, g):
                return g - self.g0 + 1

            def f_like(self, f):
                return (f - self.f0) // 2 + 1

            def g_like(self, g):
                return (g - self.g0) // 2 + 1

        NORM0, TURN0, QK0, V0, V0_TAKE = 0, 2, 4, 8, 10
        PROJ1, ADD1, NORM_END, TURN_END, LOGITS = 12, 15, 16, 17, 18
        GMAX, GATES, GT, MERGE, MCOPY = 20, 22, 23, 24, 26
        HEADS0 = 9
        TURN_Y, PROJ0, ADD0 = 38, 39, 41
        NORM1, NORM2, TURN2, UP, DOWN, ADDF = 43, 44, 45, 46, 50, 54
        NORM3, TURN3, V1 = 55, 56, 58
        BANKS0 = (3, 7)
        BANKS_V = (0, 6, 3, 7)
        FH = NF // 2

        def step0(p):
            k = (p - HEADS0) * 2 // 3
            return k if p >= HEADS0 and HEADS0 + (3 * k + 1) // 2 == p else -99

        MIX_AT = {1: 3, 5: 0, 9: 1, 13: 2}
        TURN_AT = {2: 3, 7: 0, 11: 1, 15: 2}
        GROUP = H1 // 4

        with ExitStack() as stage:
            def ssb(name, shape, dt=F32):
                return stage.enter_context(nc.sbuf_tensor(name, shape, dt))

            big = ssb("big", [P, NF, T])
            qkT0, hid = big, big
            v1_next = big[:, :, :].rearrange("p (t a) n -> p t (a n)", t=NT)
            v0 = ssb("v0", [P, NT, C])
            nmax0 = ssb("nmax0", [P, 2, NT])
            sum0 = ssb("sum0", [P, NT, H0])
            rsum0 = ssb("rsum0", [P, NT, H0])
            probs0 = ssb("probs0", [P, 2, 3 * P])
            probsT0 = ssb("probsT0", [P, 2, 3 * P])
            y0 = ssb("y0", [P, NT, C])
            yT0 = ssb("yT0", [P, NC, T])
            qkT1 = ssb("qkT1", [P, 2, 2, T])
            v1 = ssb("v1", [P, NT, INNER])
            xnT1 = ssb("xnT1", [P, NC, T])
            rel_sb = ssb("rel_sb", [P, 2, NT, PITCH])
            rel_in = ssb("rel_in", [P, 2, NT, T])
            scores = ssb("scores", [P, 2, NT, T])
            work = ssb("work", [P, NT, T])
            top = ssb("top", [P, 2, NT, ROUNDS, 8])
            nmax1 = ssb("nmax1", [P, 2, NT])
            probs1 = ssb("probs1", [P, 2, NT, T])
            sum1 = ssb("sum1", [P, 2, NT])
            rsum1 = ssb("rsum1", [P, 2, NT])
            band = ssb("band", [P, 2, NT, P])
            bandT = ssb("bandT", [P, 2, NT, P])
            probsT1 = ssb("probsT1", [P, 2, NT, T])
            av = ssb("av", [P, ORDER, NT, INNER])
            mixT = ssb("mixT", [P, INNER // P, T])
            end = ssb("end", [P, NT, C])
            xn_end = ssb("xn_end", [P, NT, C])
            xnT_end = ssb("xnT_end", [P, NC, T])
            stats_e = ssb("stats_e", [P, NT, 6])
            meanvar_e = ssb("meanvar_e", [P, NT, 2])
            vareps_e = ssb("vareps_e", [P, NT])
            rstd_e = ssb("rstd_e", [P, NT])
            lg = ssb("lg", [E1, T])
            gsum = ssb("gsum", [E1, 4])
            top_g = ssb("top_g", [E1, 8])
            rest = ssb("rest", [E1, T])
            g_cur = ssb("g_cur", [E1, T])
            gT = ssb("gT", [P, NT, E1])

            block = stage.enter_context(nc.Block())

            @block.sync
            def _(sp):
                def turn(nxt, now, old):
                    n = Counts(nxt, now, old)

                    def rel_write(f):
                        sp.wait_ge(rel_ready, n.f(f))
                        if f - 2 >= n.f0:
                            sp.wait_ge(s1_ready, n.f(f - 2))
                        sp.dma_start(rel_scr[f % 2].rearrange("t p x -> p t x")[:, :, 0:EXTW],
                                     rel_sb[:, f % 2, :, 0:EXTW]).then_inc(rel_out[f % 2], 16)

                    def rel_read(f):
                        sp.wait_ge(rel_out[f % 2], 16 * n.f_like(f))
                        sp.dma_start(rel_in[:, f % 2, :, :], skewed(rel_scr, f % 2, P - 1, -1, T))\
                            .then_inc(rel_back[f % 2], 16)

                    def att_write(g):
                        if g >= 0:
                            sp.wait_ge(p1_ready, g + 1)
                        if g - 2 >= n.g0:
                            sp.wait_ge(att_back[g % 2], 16 * n.g_like(g - 2))
                            sp.wait_ge(wT_ps, n.g(g - 2))
                        sp.dma_start(att_scr[g % 2].rearrange("t p x -> p t x")[:, :, MAXREL:MAXREL + T],
                                     probs1[:, g % 2, :, :]).then_inc(att_out[g % 2], 16)

                    def att_read(g):
                        sp.wait_ge(att_out[g % 2], 16 * n.g_like(g))
                        sp.dma_start(band[:, g % 2, :, 0:BAND], skewed(att_scr, g % 2, 1, 1, BAND, P))\
                            .then_inc(att_back[g % 2], 16)

                    if nxt is not None:
                        sp.dma_start(cur[:, :, :], rows(h_tok, nxt)).then_inc(load_cur, 16)
                    if old is not None:
                        sp.dma_start(end[:, :, :], rows(h_mid, old)).then_inc(load_end, 16)
                    for h in range(H1):
                        for g in n.backs(h):
                            att_write(g)
                        for f in n.rels_early(h):
                            rel_write(f)
                        for f in n.rels_ahead(h - 1):
                            rel_read(f)
                        for g in n.backs(h):
                            att_read(g)
                        for f in n.rels_early(h):
                            rel_read(f)
                        for f in n.rels_ahead(h):
                            rel_write(f)
                        if old is not None and h == MCOPY // 4:
                            sp.wait_ge(end_done, 1)
                            sp.dma_start(rows(h_att, old), end[:, :, :]).then_inc(end_saved, 16)
                            sp.wait_ge(g_ready, 1)
                            sp.dma_start(gates_scr[:, bass.ds(old, 1), :].rearrange("e b t -> e (b t)"),
                                         g_cur[:, :]).then_inc(end_saved, 16)
                        if nxt is not None and h == NORM3 // 4:
                            sp.wait_ge(cur_done, 1)
                            sp.dma_start(rows(h_mid, nxt), cur[:, :, :]).then_inc(cur_saved, 16)
                    if nxt is not None:
                        sp.wait_ge(cur_saved, 16)
                    if old is not None:
                        sp.wait_ge(end_saved, 32)
                    sp.wait_ge(arrived, 4)
                    sp.sem_clear(range(body_sems[0], body_sems[-1] + 1))
                    sp.sem_clear(arrived)
                    for name in go:
                        sp.sem_inc(go[name], 1)

                all_turns(sp, turn)

            @block.gpsimd
            def _(pool):
                def turn(nxt, now, old):
                    n = Counts(nxt, now, old)
                    steps = [0]

                    def rstd_of(k):
                        pool.wait_ge(stats_ready, k + 1)
                        pool.tensor_tensor(rstd[:, :], vareps[:, :], mhalf[:, :], ALU.pow)\
                            .then_inc(rstd_ready, 1)

                    def mix(q, after):
                        pool.wait_ge(av_ready, ORDER * n.g(after))
                        part = [av[:, k, :, :].rearrange("p t (h d) -> p t h d", d=D1)[
                            :, :, GROUP * q:GROUP * (q + 1), :] for k in range(ORDER)]
                        for k in range(ORDER):
                            for t in range(NT):
                                al = alphas[:, k, GROUP * q:GROUP * (q + 1)].unsqueeze(2)
                                pool.tensor_tensor(part[k][:, t], part[k][:, t],
                                                   al.to_broadcast([P, GROUP, D1]), ALU.mult)\
                                    .then_inc(pool_steps, 1)
                        steps[0] += ORDER * NT
                        for k in range(1, ORDER):
                            pool.wait_ge(pool_steps, steps[0])
                            for t in range(NT):
                                pool.tensor_tensor(part[0][:, t], part[0][:, t], part[k][:, t], ALU.add)\
                                    .then_inc(mix_ready if k == ORDER - 1 else pool_steps, 1)
                            steps[0] += NT if k < ORDER - 1 else 0

                    for h in range(H1):
                        if h in MIX_AT:
                            q = MIX_AT[h]
                            if q == 3 and old is not None:
                                mix(3, -1)
                            elif q < 3 and now is not None:
                                mix(q, GROUP * q + GROUP - 1)
                        for p in range(4 * h, 4 * h + 4):
                            if nxt is not None:
                                for k, at in enumerate((NORM0, NORM1, NORM2, NORM3)):
                                    if p == at:
                                        rstd_of(k)
                            if old is not None and p == ADD1:
                                pool.wait_ge(stats_end, 1)
                                pool.tensor_tensor(rstd_e[:, :], vareps_e[:, :], mhalf[:, :], ALU.pow)\
                                    .then_inc(rstd_end_ready, 1)
                        if h == 0 and now is not None:
                            if old is not None:
                                pool.wait_ge(av_ps, 1)
                            pool.tensor_copy(v1[:, :, :], v1_next).then_inc(v1_moved, 1)
                    turn_end(pool, "pool")

                all_turns(pool, turn)

            @block.tensor
            def _(pe):
                def turn_over(dst, src, done):
                    for c in range(NC):
                        for t in range(NT):
                            ins = pe.transpose(dst[:, c * T + t * P:c * T + (t + 1) * P],
                                               src(t, c), ident[:, :])
                    ins.then_inc(done, 1)

                def turn(nxt, now, old):
                    n = Counts(nxt, now, old)

                    def scores0(h):
                        m, at = h // HPM, SLOT * (h % HPM)
                        if h == 0:
                            pe.wait_ge(qk0_ready, MQ)
                        if h >= 2:
                            pe.wait_ge(p0_ready, h - 1)
                        ps = bank[BANKS0[h % 2]]
                        q = qkT0[at:at + D0, m, :]
                        k = qkT0[at:at + D0, MQ + m, :]
                        for col, tq, tk in ((0, 0, 0), (P, 1, 0), (2 * P, 1, 1)):
                            ins = pe.matmul(ps[:, col:col + P], q[:, tq * P:(tq + 1) * P],
                                            k[:, tk * P:(tk + 1) * P], start=True, stop=tq != tk)
                            if tq == tk:
                                ins = pe.matmul(ps[:, col:col + P], ident_b[:, :], causal[:, :],
                                                start=False, stop=True)
                        ins.then_inc(s0_ps, 1)

                    def probs_over0(h):
                        pe.wait_ge(p0_ready, h + 1)
                        if h == 0:
                            pe.wait_ge(v0_ready, 1)
                        else:
                            pe.wait_ge(pT0_ready, h)
                        if h % HPM == 0 and h:
                            pe.wait_ge(o0_ready, h // HPM)
                        for i in range(3):
                            ins = pe.transpose(bank[0][:, i * P:(i + 1) * P],
                                               probs0[:, h % 2, i * P:(i + 1) * P], ident[:, :])
                        ins.then_inc(pT0_ps, 1)

                    def attend0(h):
                        pe.wait_ge(pT0_ready, h + 1)
                        at = [3 * P + t * HPM * D0 + (h % HPM) * D0 for t in range(NT)]
                        o = [bank[0][:, a:a + D0] for a in at]
                        v = [v0[:, t, h * D0:(h + 1) * D0] for t in range(NT)]
                        pT = probsT0[:, h % 2, :]
                        pe.matmul(o[0], pT[:, 0:P], v[0], start=True, stop=True)
                        pe.matmul(o[1], pT[:, P:2 * P], v[0], start=True, stop=False)
                        pe.matmul(o[1], pT[:, 2 * P:3 * P], v[1], start=False, stop=True).then_inc(o0_ps, 1)

                    def layer0(p):
                        if p == TURN0:
                            pe.wait_ge(xn_ready, NT)
                            turn_over(bank[0], lambda t, c: xn[:, t, c * P:(c + 1) * P], xnT_ps)
                        if QK0 <= p < QK0 + MQ:
                            j = p - QK0
                            pe.wait_ge(xnT_ready, 1)
                            if j >= 2:
                                pe.wait_ge(qk0_ready, j - 1)
                            for m in (2 * j, 2 * j + 1):
                                for c in range(NC):
                                    ins = pe.matmul(bank[6 + j % 2][:, T * (m % 2):T * (m % 2 + 1)],
                                                    wqk0[:, c, m * P:(m + 1) * P], xnT[:, c, :],
                                                    start=(c == 0), stop=(c == NC - 1))
                            ins.then_inc(qk0_ps, 1)
                        if p == V0:
                            for t in range(NT):
                                for c in range(NC):
                                    ins = pe.matmul(bank[0][:, t * C:(t + 1) * C], xnT[:, c, t * P:(t + 1) * P],
                                                    wv0[:, c, :], start=(c == 0), stop=(c == NC - 1))
                            ins.then_inc(v0_ps, 1)
                        k = step0(p)
                        if 0 <= k < H0:
                            scores0(k)
                        if 0 <= k - 3 < H0:
                            attend0(k - 3)
                        if 0 <= k - 2 < H0:
                            probs_over0(k - 2)
                        if p == TURN_Y:
                            pe.wait_ge(y0_ready, MQ)
                            turn_over(bank[6], lambda t, c: y0[:, t, c * P:(c + 1) * P], yT0_ps)
                        if p == PROJ0:
                            pe.wait_ge(yT0_ready, 1)
                            for t in range(NT):
                                for c in range(NC):
                                    pe.matmul(bank[7][:, t * C:(t + 1) * C], yT0[:, c, t * P:(t + 1) * P],
                                              wp0[:, c, :], start=(c == 0), stop=False)
                                ins = pe.matmul(bank[7][:, t * C:(t + 1) * C], ones[0:1, :], bp0[:, :],
                                                start=False, stop=True)
                            ins.then_inc(r0_ps, 1)
                        if p == TURN2:
                            pe.wait_ge(xn_ready, 3 * NT)
                            turn_over(bank[6], lambda t, c: xn2[:, t, c * P:(c + 1) * P], xnT_ps)
                        if UP <= p < UP + NF // 2:
                            j = p - UP
                            pe.wait_ge(xnT_ready, 2)
                            if j >= 2:
                                pe.wait_ge(f1_ready, 2 * j - 2)
                            for f in (2 * j, 2 * j + 1):
                                for c in range(NC):
                                    ins = pe.matmul(bank[7 * (1 - j % 2)][:, T * (f % 2):T * (f % 2 + 1)],
                                                    fc1[:, c, f * P:(f + 1) * P], xnT[:, c, :],
                                                    start=(c == 0), stop=(c == NC - 1))
                            ins.then_inc(f1_ps, 1)
                        if DOWN <= p < DOWN + 2 * NT:
                            t, i = (p - DOWN) // 2, (p - DOWN) % 2
                            for f in range(i * FH, (i + 1) * FH):
                                if t == 0:
                                    pe.wait_ge(f1_ready, f + 1)
                                pe.matmul(bank[6][:, t * C:(t + 1) * C], hid[:, f, t * P:(t + 1) * P],
                                          fc2[:, f, :], start=(f == 0), stop=False)
                            if i:
                                pe.matmul(bank[6][:, t * C:(t + 1) * C], ones[0:1, :], fc2b[:, :],
                                          start=False, stop=True).then_inc(f2_ps, 1)
                        if p == TURN3:
                            pe.wait_ge(xn_ready, 4 * NT)
                            turn_over(bank[7], lambda t, c: xn[:, t, c * P:(c + 1) * P], xnT_ps)
                        if V1 <= p < V1 + 2 * NT:
                            t, i = (p - V1) // 2, (p - V1) % 2
                            pe.wait_ge(xnT_ready, 3)
                            for c in range(NC):
                                ins = pe.matmul(bank[BANKS_V[p - V1]][:, :], xnT[:, c, t * P:(t + 1) * P],
                                                wv1[:, c, i * 512:(i + 1) * 512],
                                                start=(c == 0), stop=(c == NC - 1))
                            ins.then_inc(v1_ps, 1)

                    def tail(p):
                        if p in (PROJ1, PROJ1 + 1):
                            t = p - PROJ1
                            pe.wait_ge(mT_ready, 1)
                            for j in range(INNER // P):
                                pe.matmul(bank[6][:, t * C:(t + 1) * C], mixT[:, j, t * P:(t + 1) * P],
                                          wo1[:, j, :], start=(j == 0), stop=False)
                            pe.matmul(bank[6][:, t * C:(t + 1) * C], ones[0:1, :], bo1[:, :],
                                      start=False, stop=True).then_inc(r1_ps, 1)
                        if p == TURN_END:
                            pe.wait_ge(xn_end_ready, NT)
                            turn_over(bank[6], lambda t, c: xn_end[:, t, c * P:(c + 1) * P], xnT_end_ps)
                        if p == LOGITS:
                            pe.wait_ge(xnT_end_ready, 1)
                            for c in range(NC):
                                ins = pe.matmul(bank[6][0:E1, 0:T], gate[:, c, :], xnT_end[:, c, :],
                                                start=(c == 0), stop=(c == NC - 1))
                            ins.then_inc(lg_ps, 1)
                        if p == GT:
                            pe.wait_ge(g_ready, 1)
                            for t in range(NT):
                                ins = pe.transpose(bank[6][:, t * E1:(t + 1) * E1], g_cur[:, t * P:(t + 1) * P],
                                                   ident[0:E1, 0:E1])
                            ins.then_inc(gT_ps, 1)
                        if p == MERGE:
                            pe.wait_ge(gT_ready, 1)
                            for c in range(NC):
                                for t in range(NT):
                                    ins = pe.matmul(bank[6][:, c * E1:(c + 1) * E1],
                                                    xn_end[:, t, c * P:(c + 1) * P], gT[:, t, :],
                                                    start=(t == 0), stop=(t == NT - 1))
                            ins.then_inc(mg_ps, 1)

                    def rel(f):
                        at, j = D1 * (f % 2), f // 2
                        if now is None or j >= 1:
                            pe.wait_ge(qk1_ready, j if now is not None else 1)
                        q = qkT1[at:at + D1, j % 2, 0, :]
                        if f > n.f0:
                            pe.wait_ge(rel_ready, n.f(f - 1))
                        for t in range(NT):
                            ins = pe.matmul(bank[2][:, t * NREL:(t + 1) * NREL], q[:, t * P:(t + 1) * P],
                                            rel_k[at:at + D1, :], start=True, stop=True)
                        ins.then_inc(rel_ps, 1)

                    def front(f):
                        at, j = D1 * (f % 2), f // 2
                        q = qkT1[at:at + D1, j % 2, 0, :]
                        k = qkT1[at:at + D1, j % 2, 1, :]
                        pe.wait_ge(rel_back[f % 2], 16 * n.f_like(f))
                        if f > n.f0:
                            pe.wait_ge(s1_ready, n.f(f - 1))
                        pe.matmul(bank[1][:, :], ident[:, :], flat(rel_in[:, f % 2]), start=True, stop=False)
                        for t in range(NT):
                            ins = pe.matmul(bank[1][:, t * T:(t + 1) * T], q[:, t * P:(t + 1) * P], k,
                                            start=False, stop=t == NT - 1)
                        ins.then_inc(s1_ps, 1)

                    def qk1(j, f):
                        if f >= n.f0:
                            pe.wait_ge(rel_ready, n.f(f))
                        if j == 1:
                            pe.wait_ge(xnT_moved, 1)
                        src = xnT1
                        if j == H1 // 2:
                            pe.wait_ge(xnT_ready, 3)
                            src = xnT
                        for i in range(2):
                            for c in range(NC):
                                at = i * INNER + (j % (H1 // 2)) * P
                                ins = pe.matmul(bank[2][:, i * T:(i + 1) * T], wqk1[:, c, at:at + P],
                                                src[:, c, :], start=(c == 0), stop=(c == NC - 1))
                        ins.then_inc(qk1_ps, 1)

                    def probs_over(g):
                        if g >= 0:
                            pe.wait_ge(p1_ready, g + 1)
                        if g > n.g0:
                            pe.wait_ge(pT1_ready, n.g(g - 1))
                        pe.wait_ge(mT_ready, mixes_before(g + 1, old)) if mixes_before(g + 1, old) else None
                        for kc in range(NT):
                            for t in range(NT):
                                ins = pe.transpose(bank[4][:, kc * T + t * P:kc * T + (t + 1) * P],
                                                   probs1[:, g % 2, t, kc * P:(kc + 1) * P], ident[:, :])
                        ins.then_inc(pT1_ps, 1)

                    def band_over(g):
                        pe.wait_ge(att_back[g % 2], 16 * n.g_like(g))
                        if g >= 0:
                            pe.wait_ge(low_ready, g + 1)
                        if g > n.g0:
                            pe.wait_ge(av_ready, ORDER * n.g(g - 1))
                        for t in range(NT):
                            ins = pe.transpose(bank[5][:, t * P:(t + 1) * P], band[:, g % 2, t, :], ident[:, :])
                        ins.then_inc(wT_ps, 1)

                    def order(g, k):
                        done = ORDER * (n.g(g) - 1) + k
                        if k == 0:
                            pe.wait_ge(pT1_ready, n.g(g))
                            pe.wait_ge(wT_ready, n.g(g))
                            if g == 0:
                                pe.wait_ge(v1_moved, 1)
                        if k:
                            pe.wait_ge(av_ready, done)
                        outs = []
                        for t in range(NT):
                            at = 2 * P + (done % 2) * P + t * D1
                            outs.append(bank[5][:, at:at + D1])
                            for kc in range(NT):
                                r = v1[:, kc, :] if k == 0 else av[:, k - 1, kc, :]
                                hh = g % H1
                                ins = pe.matmul(outs[t], probsT1[:, g % 2, kc, t * P:(t + 1) * P],
                                                r[:, hh * D1:(hh + 1) * D1], start=(kc == 0),
                                                stop=(k > 0 and kc == NT - 1))
                            if k == 0:
                                ins = pe.matmul(outs[t], bandT[:, g % 2, t, :], rel_v[:, :],
                                                start=False, stop=True)
                        ins.then_inc(av_ps, 1)

                    def mixed_over(h):
                        q = TURN_AT[h]
                        pe.wait_ge(mix_ready, NT * mixes_before(h + 1, old))
                        pe.wait_ge(pT1_ready, n.g(min(h - 1, n.g1)))
                        turn_over(bank[4], lambda t, c: av[:, 0, t, (2 * q + c) * P:(2 * q + c + 1) * P], mT_ps)

                    def point(p):
                        if old is not None:
                            tail(p)
                        if nxt is not None:
                            layer0(p)

                    for h in range(H1):
                        for f in n.rels_early(h):
                            rel(f)
                        for g in n.backs(h):
                            probs_over(g)
                        point(4 * h)
                        if n.makes_pair(h):
                            qk1(h // 2 + 1, h + 1)
                        point(4 * h + 1)
                        for g in n.backs(h):
                            band_over(g)
                        for f in n.fronts(h):
                            front(f)
                        for g in n.backs(h):
                            order(g, 0)
                        for f in n.rels_ahead(h):
                            rel(f)
                        point(4 * h + 2)
                        for g in n.backs(h):
                            order(g, 1)
                        point(4 * h + 3)
                        for g in n.backs(h):
                            order(g, 2)
                        if h in TURN_AT and (old if TURN_AT[h] == 3 else now) is not None:
                            mixed_over(h)
                    turn_end(pe, "pe")

                all_turns(pe, turn)

            @block.scalar
            def _(act):
                def leave(dst, src, done, **kw):
                    act.activation(dst, src, ACT.Copy, **kw).then_inc(done, 1)

                def turn(nxt, now, old):
                    n = Counts(nxt, now, old)

                    def exp0(h):
                        act.wait_ge(max0_ready, h + 1)
                        if h >= 2:
                            act.wait_ge(pT0_ps, h - 1)
                        ps = bank[BANKS0[h % 2]]
                        for t, a, z in ((0, 0, P), (1, P, 3 * P)):
                            ins = act.activation(probs0[:, h % 2, a:z], ps[:, a:z], ACT.Exp,
                                                 bias=nmax0[:, h % 2, t:t + 1], accum_out=sum0[:, t, h:h + 1])
                        ins.then_inc(p0_ready, 1)

                    def layer0(p):
                        if p == TURN0:
                            act.wait_ge(xnT_ps, 1)
                            leave(flat(xnT), bank[0][:, :], xnT_ready)
                        if QK0 <= p < QK0 + MQ:
                            j = p - QK0
                            if j == 0 and now is not None:
                                act.wait_ge(v1_moved, 1)
                            act.wait_ge(qk0_ps, j + 1)
                            for m in (2 * j, 2 * j + 1):
                                ins = act.activation(
                                    qkT0[:, m, :], bank[6 + j % 2][:, T * (m % 2):T * (m % 2 + 1)],
                                    ACT.Identity, bias=bqk0[:, m:m + 1], scale=1.0 / D0 if m < MQ else 1.0)
                            ins.then_inc(qk0_ready, 1)
                        k = step0(p)
                        if 0 <= k - 1 < H0:
                            exp0(k - 1)
                        if 0 <= k - 3 < H0 and (k - 3) % HPM == HPM - 1:
                            q = (k - 3) // HPM
                            act.wait_ge(o0_ps, (q + 1) * HPM)
                            leave(y0[:, :, q * HPM * D0:(q + 1) * HPM * D0],
                                  bank[0][:, 3 * P:4 * P].rearrange("p (t n) -> p t n", t=NT), o0_ready)
                        if 0 <= k - 2 < H0:
                            h = k - 2
                            act.wait_ge(pT0_ps, h + 1)
                            if h >= 2:
                                act.wait_ge(o0_ps, h - 1)
                            leave(probsT0[:, h % 2, :], bank[0][:, 0:3 * P], pT0_ready)
                        if p == TURN_Y:
                            act.wait_ge(yT0_ps, 1)
                            leave(flat(yT0), bank[6][:, :], yT0_ready)
                        if p == TURN2:
                            act.wait_ge(xnT_ps, 2)
                            for c in range(NC):
                                ins = act.activation(xnT[:, c, :], bank[6][:, c * T:(c + 1) * T], ACT.Identity,
                                                     bias=beta[:, c:c + 1], scale=gamma[:, c:c + 1])
                            ins.then_inc(xnT_ready, 1)
                        if UP <= p < UP + NF // 2:
                            j = p - UP
                            act.wait_ge(f1_ps, j + 1)
                            for f in (2 * j, 2 * j + 1):
                                act.activation(hid[:, f, :], bank[7 * (1 - j % 2)][:, T * (f % 2):T * (f % 2 + 1)],
                                               ACT.Silu, bias=fc1b[:, f:f + 1]).then_inc(f1_ready, 1)
                        if p == TURN3:
                            act.wait_ge(xnT_ps, 3)
                            leave(flat(xnT), bank[7][:, :], xnT_ready)

                    def tail(p):
                        if p == TURN_END:
                            act.wait_ge(xnT_end_ps, 1)
                            leave(flat(xnT_end), bank[6][:, :], xnT_end_ready)
                        if p == GMAX:
                            act.wait_ge(gmax_ready, 1)
                            act.activation(lg[:, :], lg[:, :], ACT.Exp, bias=gsum[:, 0:1],
                                           accum_out=gsum[:, 1:2]).then_inc(gexp_ready, 1)
                        if p == GT:
                            act.wait_ge(gT_ps, 1)
                            leave(flat(gT), bank[6][:, 0:NT * E1], gT_ready)

                    def rel_leave(f):
                        act.wait_ge(rel_ps, n.f(f))
                        if f - 2 >= n.f0:
                            act.wait_ge(rel_out[f % 2], 16 * n.f_like(f - 2))
                        for t in range(NT):
                            low, high = P - 1 - MAXREL + P * t, P - 1 + MAXREL + P * t
                            dst, src = rel_sb[:, f % 2, t, :], bank[2][:, t * NREL:(t + 1) * NREL]
                            act.activation(dst[:, 0:low], src[:, 0:1].to_broadcast([P, low]), ACT.Copy)
                            act.activation(dst[:, high + 1:EXTW],
                                           src[:, NREL - 1:NREL].to_broadcast([P, EXTW - high - 1]), ACT.Copy)
                            ins = act.activation(dst[:, low:high + 1], src, ACT.Copy)
                        ins.then_inc(rel_ready, 1)

                    def scores_leave(f):
                        act.wait_ge(s1_ps, n.f(f))
                        if f >= 2 and now is not None:
                            act.wait_ge(p1_ready, f - 1)
                        leave(flat(scores[:, f % 2]), bank[1][:, :], s1_ready)

                    def qk_out(j):
                        act.wait_ge(qk1_ps, j if now is not None else 1)
                        for i in range(2):
                            m = i * (INNER // P) + j % (H1 // 2)
                            ins = act.activation(qkT1[:, j % 2, i, :], bank[2][:, i * T:(i + 1) * T],
                                                 ACT.Identity, bias=bqk1[:, m:m + 1],
                                                 scale=1.0 if i == 0 else D1 ** -0.5)
                        ins.then_inc(qk1_ready, 1)

                    def exp1(h):
                        act.wait_ge(max1_ready, h + 1)
                        if h - 2 >= n.g0:
                            act.wait_ge(pT1_ps, n.g(h - 2))
                            act.wait_ge(att_out[h % 2], 16 * n.g_like(h - 2))
                        for t in range(NT):
                            ins = act.activation(probs1[:, h % 2, t, :], scores[:, h % 2, t, :], ACT.Exp,
                                                 bias=nmax1[:, h % 2, t:t + 1])
                        ins.then_inc(e1_ready, 1)

                    def av_out(g, k):
                        done = ORDER * (n.g(g) - 1) + k
                        act.wait_ge(av_ps, done + 1)
                        for t in range(NT):
                            at = 2 * P + (done % 2) * P + t * D1
                            hh = g % H1
                            ins = act.activation(av[:, k, t, hh * D1:(hh + 1) * D1], bank[5][:, at:at + D1],
                                                 ACT.Copy, scale=rsum1[:, g % 2, t:t + 1])
                        ins.then_inc(av_ready, 1)

                    def point(p):
                        if old is not None:
                            tail(p)
                        if nxt is not None:
                            layer0(p)

                    if now is not None:
                        leave(flat(xnT1), flat(xnT), xnT_moved)
                        if nxt is not None:
                            act.wait_ge(xnT_moved, 1)
                    for h in range(H1):
                        for f in n.rels_early(h):
                            rel_leave(f)
                        for g in n.backs(h):
                            act.wait_ge(pT1_ps, n.g(g))
                            leave(flat(probsT1[:, g % 2]), bank[4][:, :], pT1_ready)
                        if now is not None:
                            exp1(h)
                        point(4 * h)
                        if n.makes_pair(h):
                            qk_out(h // 2 + 1)
                        point(4 * h + 1)
                        for g in n.backs(h):
                            act.wait_ge(wT_ps, n.g(g))
                            leave(flat(bandT[:, g % 2]), bank[5][:, 0:NT * P], wT_ready)
                        for f in n.fronts(h):
                            scores_leave(f)
                        for g in n.backs(h):
                            av_out(g, 0)
                        for f in n.rels_ahead(h):
                            rel_leave(f)
                        point(4 * h + 2)
                        for g in n.backs(h):
                            av_out(g, 1)
                        point(4 * h + 3)
                        for g in n.backs(h):
                            av_out(g, 2)
                        if h in TURN_AT and (old if TURN_AT[h] == 3 else now) is not None:
                            q = TURN_AT[h]
                            act.wait_ge(mT_ps, mixes_before(h + 1, old))
                            leave(flat(mixT[:, 2 * q:2 * q + 2]), bank[4][:, :], mT_ready)
                    turn_end(act, "act")

                all_turns(act, turn)

            @block.vector
            def _(dve):
                def turn(nxt, now, old):
                    n = Counts(nxt, now, old)
                    ch = Chain(dve, dve_steps)

                    def norm_stats(src, st, mv, ve, done):
                        for t in range(NT):
                            ch.step(dve.bn_stats(st[:, t, :], src[:, t, :]))
                        ch.after(ch.n)
                        for t in range(NT):
                            ch.step(dve.bn_aggr(mv[:, t, :], st[:, t, :]))
                        ch.after(ch.n)
                        dve.tensor_scalar(ve[:, :], mv[:, :, 1], EPS, None, ALU.add).then_inc(done, 1)

                    def norm_apply(k, src, dst, mv, rs, ready, done):
                        dve.wait_ge(ready, k + 1)
                        for t in range(NT):
                            dve.tensor_scalar(dst[:, t, :], src[:, t, :], mv[:, t, 0:1], rs[:, t:t + 1],
                                              ALU.subtract, ALU.mult).then_inc(done, 1)
                        dve.wait_ge(done, NT * (k + 1))

                    def stats0(src):
                        norm_stats(src, stats, meanvar, vareps, stats_ready)

                    def apply0(k, src, dst):
                        norm_apply(k, src, dst, meanvar, rstd, rstd_ready, xn_ready)

                    def layer0(p):
                        if p == NORM0:
                            dve.wait_ge(load_cur, 16)
                            stats0(cur)
                        if p == NORM0 + 1:
                            apply0(0, cur, xn)
                        if p == V0_TAKE:
                            dve.wait_ge(v0_ps, 1)
                            for t in range(NT):
                                ins = dve.tensor_tensor(v0[:, t, :], bank[0][:, t * C:(t + 1) * C], bv0[:, :],
                                                        ALU.add)
                            ins.then_inc(v0_ready, 1)
                        k = step0(p)
                        if 0 <= k - 1 < H0:
                            h = k - 1
                            dve.wait_ge(s0_ps, h + 1)
                            if h >= 2:
                                dve.wait_ge(p0_ready, h - 1)
                            for t, a, z in ((0, 0, P), (1, P, 3 * P)):
                                ins = dve.tensor_reduce(nmax0[:, h % 2, t:t + 1], bank[BANKS0[h % 2]][:, a:z], AX.X,
                                                        ALU.max, negate=True)
                            ins.then_inc(max0_ready, 1)
                        if 0 <= k - 4 < H0 and (k - 4) % HPM == HPM - 1:
                            q = (k - 4) // HPM
                            hs = slice(q * HPM, (q + 1) * HPM)
                            dve.wait_ge(p0_ready, (q + 1) * HPM)
                            ch.link(dve.reciprocal(rsum0[:, :, hs], sum0[:, :, hs]))
                            dve.wait_ge(o0_ready, q + 1)
                            yq = y0[:, :, :].rearrange("p t (h d) -> p t h d", d=D0)[:, :, hs, :]
                            dve.tensor_tensor(
                                yq, yq, rsum0[:, :, hs].unsqueeze(3).to_broadcast([P, NT, HPM, D0]), ALU.mult)\
                                .then_inc(y0_ready, 1)
                        if p == ADD0:
                            dve.wait_ge(r0_ps, 1)
                            ch.link(dve.tensor_tensor(flat(cur), flat(cur), bank[7][:, :], ALU.add))
                            stats0(cur)
                        if p == NORM1:
                            apply0(1, cur, xn)
                            stats0(xn)
                        if p == NORM2:
                            apply0(2, xn, xn2)
                            ch.link(dve.tensor_tensor(flat(cur), flat(cur), flat(xn), ALU.add))
                        if p == ADDF:
                            dve.wait_ge(f2_ps, NT)
                            dve.scalar_tensor_tensor(out=flat(cur), in0=bank[6][:, :], scalar=0.5, in1=flat(cur),
                                                     op0=ALU.mult, op1=ALU.add).then_inc(cur_done, 1)
                            dve.wait_ge(cur_done, 1)
                            stats0(cur)
                        if p == NORM3:
                            apply0(3, cur, xn)

                    def take_v1():
                        for t in range(NT):
                            for i in range(2):
                                dve.wait_ge(v1_ps, 2 * t + i + 1)
                                dve.tensor_tensor(v1_next[:, t, i * 512:(i + 1) * 512], bank[BANKS_V[2 * t + i]][:, :],
                                                  bv1[:, i * 512:(i + 1) * 512], ALU.add)

                    def tail(p):
                        if p == ADD1:
                            dve.wait_ge(load_end, 16)
                            dve.wait_ge(r1_ps, NT)
                            dve.tensor_tensor(flat(end), flat(end), bank[6][:, :], ALU.add).then_inc(end_done, 1)
                            dve.wait_ge(end_done, 1)
                            norm_stats(end, stats_e, meanvar_e, vareps_e, stats_end)
                        if p == NORM_END:
                            norm_apply(0, end, xn_end, meanvar_e, rstd_e, rstd_end_ready, xn_end_ready)
                        if p == GMAX:
                            dve.wait_ge(lg_ps, 1)
                            ch.link(dve.tensor_scalar(lg[:, :], bank[6][0:E1, 0:T], gate_b[:, :], None, ALU.add))
                            dve.tensor_reduce(gsum[:, 0:1], lg[:, :], AX.X, ALU.max, negate=True)\
                                .then_inc(gmax_ready, 1)
                        if p == GATES:
                            dve.wait_ge(gexp_ready, 1)
                            ch.link(dve.reciprocal(gsum[:, 2:3], gsum[:, 1:2]))
                            ch.link(dve.tensor_scalar(lg[:, :], lg[:, :], gsum[:, 2:3], None, ALU.mult))
                            ch.link(dve.max(top_g[:, :], lg[:, :]))
                            ch.link(dve.match_replace(rest[:, :], top_g[:, :], lg[:, :], 0.0))
                            dve.tensor_tensor(g_cur[:, :], lg[:, :], rest[:, :], ALU.subtract).then_inc(g_ready, 1)
                        if p == MCOPY:
                            dve.wait_ge(mg_ps, 1)
                            dve.tensor_copy(merged[:, :, :, bass.ds(old, 1)].rearrange("p c e b -> p (c e) b"),
                                            bank[6][:, 0:NC * E1].rearrange("p (n b) -> p n b", b=1))\
                                .then_inc(mg_kept, 1)

                    def point(p):
                        if old is not None:
                            tail(p)
                        if nxt is not None:
                            layer0(p)

                    def threshold(h):
                        if h >= 1:
                            dve.wait_ge(s1_ready, n.f(h))
                        if h >= 2:
                            dve.wait_ge(e1_ready, h - 1)
                        last = {}
                        for r in range(ROUNDS):
                            for t in range(NT):
                                src = scores[:, h % 2, t, :] if r == 0 else work[:, t, :]
                                if r:
                                    ch.after(last[t])
                                last[t] = ch.step(dve.max(top[:, h % 2, t, r, :], src))
                            if r == 0:
                                ch.after(ch.n)
                                dve.tensor_scalar(nmax1[:, h % 2, :], top[:, h % 2, :, 0, 0], -1.0, None,
                                                  ALU.mult).then_inc(max1_ready, 1)
                            if r < ROUNDS - 1:
                                for t in range(NT):
                                    src = scores[:, h % 2, t, :] if r == 0 else work[:, t, :]
                                    ch.after(last[t])
                                    last[t] = ch.step(dve.match_replace(work[:, t, :], top[:, h % 2, t, r, :],
                                                                        src, NEG))
                            if r % 2:
                                point(4 * h + r // 2)

                    def select(h):
                        dve.wait_ge(e1_ready, h + 1)
                        ch.after(ch.n)
                        for t in range(NT):
                            ins = dve.scalar_tensor_tensor(
                                out=probs1[:, h % 2, t, :], in0=scores[:, h % 2, t, :],
                                scalar=top[:, h % 2, t, ROUNDS - 1, 7:8], in1=probs1[:, h % 2, t, :],
                                op0=ALU.is_ge, op1=ALU.mult, accum_out=sum1[:, h % 2, t:t + 1])
                        ins.then_inc(p1_ready, 1)
                        dve.wait_ge(p1_ready, h + 1)
                        if h - 2 >= n.g0:
                            dve.wait_ge(av_ready, ORDER * n.g(h - 2))
                            dve.wait_ge(wT_ps, n.g(h - 2))
                        ch.step(dve.reciprocal(rsum1[:, h % 2, :], sum1[:, h % 2, :]))
                        for t in range(NT):
                            m = MAXREL + P * t
                            ins = dve.tensor_tensor_reduce(
                                work[:, t, 0:m], probs1[:, h % 2, t, 0:m], low_mask[:, t, 0:m], 1.0, 0.0,
                                ALU.mult, ALU.add, band[:, h % 2, t, BAND:P])
                        ins.then_inc(low_ready, 1)
                        dve.wait_ge(low_ready, h + 1)

                    for h in range(H1):
                        if now is not None:
                            threshold(h)
                        else:
                            for p in range(4 * h, 4 * h + 4):
                                point(p)
                        if now is not None:
                            select(h)
                    if nxt is not None:
                        take_v1()
                    turn_end(dve, "dve")

                all_turns(dve, turn)

        if stop in ("att0", "ffn0", "att1"):
            return finish_copy(nc, ctx, h_mid if stop == "ffn0" else h_att, out, sem)

        with ExitStack() as stage:
            def ssb(name, shape, dt=F32):
                return stage.enter_context(nc.sbuf_tensor(name, shape, dt))

            w1_all = ssb("w1_all", [P, WBUFS, NC, HID])
            w1 = [w1_all[:, j] for j in range(WBUFS)]
            w2 = [ssb(f"w2_{i}", [P, NH, C]) for i in range(WBUFS)]
            token_in = ssb("token_in", [P, 2, NC, B])
            hid_rows = ssb("hid_rows", [B, 2, HID])
            act_in = ssb("act_in", [P, 2, NH, B])
            act_out = ssb("act_out", [P, 2, NH, B])
            out_rows = ssb("out_rows", [B, E1, C])
            o_all = w1_all[0:E1].rearrange("e w c n -> e (w c n)")[:, 0:B * C].rearrange("e (b c) -> e b c", b=B)
            b2_rows = ssb("b2_rows", [E1, C])
            gates = wqk1[0:E1, :, :].rearrange("e c n -> e (c n)").rearrange("e (b t) -> e b t", b=B)
            gates_loaded = sem("gates_loaded")
            w1_loaded = [sem(f"w1_loaded{i}") for i in range(WBUFS)]
            w2_loaded = [sem(f"w2_loaded{i}") for i in range(WBUFS)]
            picked = sem("expert_tokens_picked")
            up_ps = sem("expert_hidden_in_psum")
            hid_ready = sem("expert_hidden_rows_ready")
            hT_ps = sem("expert_hiddenT_in_psum")
            biased = sem("expert_hidden_biased")
            gelu_ready = sem("expert_hidden_ready")
            down_ps = sem("expert_out_in_psum")
            out_kept = sem("expert_out_kept")
            out_written = sem("expert_out_written")
            out_read = sem("expert_out_read")
            out_biased = sem("expert_out_biased")
            tok_loaded = [sem(f"tokens_loaded{i}") for i in range(WBUFS)]
            sc_ps = sem("scattered_in_psum")
            sum_ready = sem("tokens_ready")
            saved = sem("tokens_saved")
            TURNS = E1 // WBUFS
            HALF = HID // 2

            PER = B // WBUFS

            def tokens(b):
                return w2[b // PER][:, :, :].rearrange("p k n -> p (k n)")[
                    :, (b % PER) * NT * C:(b % PER + 1) * NT * C]

            def all_experts(eng, step):
                for j in range(WBUFS):
                    step(0, j)
                with eng.Fori(1, TURNS) as i:
                    for j in range(WBUFS):
                        step(i, j)

            def reuses(i, j):
                return not isinstance(i, int) or j >= 2

            def before(i, j):
                return (j - 1) % WBUFS, i * WBUFS + j, not isinstance(i, int) or j >= 3

            LAST = (WBUFS - 1, E1, True)

            block = stage.enter_context(nc.Block())

            @block.sync
            def _(sp):
                def load_up(j, e):
                    sp.dma_start(w1[j][:, :, :], A["w1"][bass.ds(e, 1), 0:C, :].rearrange(
                        "e (c p) n -> p (e c) n", p=P)).then_inc(w1_loaded[j], 16)

                def load_down(j, e):
                    sp.dma_start(w2[j][:, :, :], A["w2"][bass.ds(e, 1), 0:HID, :].rearrange(
                        "e (c p) n -> p (e c) n", p=P)).then_inc(w2_loaded[j], 16)

                for j in range(WBUFS):
                    load_up(j, j)
                    load_down(j, j)
                sp.dma_start(gates[:, :, :], gates_scr).then_inc(gates_loaded, 16)
                sp.dma_start(b2_rows[:, :], A["w2"][:, HID, :]).then_inc(gates_loaded, 16)
                with sp.Fori(0, TURNS - 1) as i:
                    for j in range(WBUFS):
                        sp.wait_ge(up_ps, i * WBUFS + j + 1)
                        load_up(j, (i + 1) * WBUFS + j)
                        sp.wait_ge(down_ps, i * WBUFS + j + 1)
                        load_down(j, (i + 1) * WBUFS + j)
                for j in range(WBUFS):
                    sp.wait_ge(down_ps, E1 - WBUFS + j + 1)
                    sp.dma_start(w2[j][:, :, :], h_att[j * PER * T:(j + 1) * PER * T, :].rearrange(
                        "(t p) c -> p t c", p=P)).then_inc(tok_loaded[j], 16)
                sp.wait_ge(out_kept, E1)
                sp.dma_start(expert_scr, out_rows[:, :, :]).then_inc(out_written, 16)
                sp.wait_ge(out_written, 16)
                sp.dma_start(o_all[:, :, :], expert_scr.rearrange("b e c -> e b c")).then_inc(out_read, 16)
                for b in range(B):
                    sp.wait_ge(sum_ready, b + 1)
                    sp.dma_start(out[b].rearrange("(t p) c -> p t c", p=P),
                                 tokens(b).rearrange("p (t c) -> p t c", t=NT)).then_inc(saved, 16)
                sp.wait_ge(saved, 16 * B)

            @block.tensor
            def _(pe):
                def down(j, n, reused, loads):
                    pe.wait_ge(gelu_ready, n)
                    pe.wait_ge(w2_loaded[j], 16 * loads)
                    if reused:
                        pe.wait_ge(out_kept, n - 2)
                    for k in range(NH):
                        ins = pe.matmul(bank[6 + j % 2][0:B, 0:C], act_out[:, j % 2, k, :], w2[j][:, k, :],
                                        start=(k == 0), stop=(k == NH - 1))
                    ins.then_inc(down_ps, 1)

                def hidden_there(j, n, reused):
                    pe.wait_ge(hid_ready, n)
                    if reused:
                        pe.wait_ge(biased, n - 2)

                def turn_hidden(j, n, reused):
                    for k in range(NH):
                        ins = pe.transpose(bank[4 + j % 2][:, k * B:(k + 1) * B],
                                           hid_rows[:, j % 2, k * P:(k + 1) * P], ident[0:B, 0:B])
                    ins.then_inc(hT_ps, 1)

                def step(i, j):
                    e = i * WBUFS + j
                    first = isinstance(i, int) and j == 0
                    if not first:
                        hidden_there(*before(i, j))
                    pe.wait_ge(picked, e + 1)
                    pe.wait_ge(w1_loaded[j], 16 * i + 16)
                    for half in range(2):
                        for c in range(NC):
                            ins = pe.matmul(bank[2 * (j % 2) + half][0:B, :], token_in[:, j % 2, c, :],
                                            w1[j][:, c, half * HALF:(half + 1) * HALF],
                                            start=(c == 0), stop=(c == NC - 1))
                        if half == 0 and not first:
                            turn_hidden(*before(i, j))
                    ins.then_inc(up_ps, 1)
                    if not first:
                        down(*before(i, j), i + 1 if j else i)

                all_experts(pe, step)
                hidden_there(*LAST)
                turn_hidden(*LAST)
                down(*LAST, TURNS)
                pe.wait_ge(gates_loaded, 32)
                pe.wait_ge(out_biased, 1)
                for b in range(B):
                    if b == 0:
                        pe.wait_ge(hid_ready, E1)
                    if b >= 4:
                        pe.wait_ge(sum_ready, b - 3)
                    for t in range(NT):
                        ins = pe.matmul(bank[b % 4][:, t * C:(t + 1) * C], gates[:, b, t * P:(t + 1) * P],
                                        o_all[:, b, :], start=True, stop=True)
                    ins.then_inc(sc_ps, 1)

            @block.vector
            def _(dve):
                def bias_up(j, n, reused):
                    dve.wait_ge(hT_ps, n)
                    if reused:
                        dve.wait_ge(gelu_ready, n - 2)
                    dve.tensor_tensor(act_in[:, j % 2, :, :],
                                      bank[4 + j % 2][:, 0:NH * B].rearrange("p (k b) -> p k b", b=B),
                                      b1_all[:, bass.ds(n - 1, 1), :].rearrange("p e k -> p (e k)")
                                      .unsqueeze(2).to_broadcast([P, NH, B]), ALU.add).then_inc(biased, 1)

                def keep(j, n, reused):
                    dve.wait_ge(down_ps, n)
                    dve.tensor_copy(out_rows[:, bass.ds(n - 1, 1), :].rearrange("p e c -> p (e c)"),
                                    bank[6 + j % 2][0:B, 0:C]).then_inc(out_kept, 1)

                def step(i, j):
                    e = i * WBUFS + j
                    first = isinstance(i, int) and j == 0
                    if reuses(i, j):
                        dve.wait_ge(up_ps, e - 1)
                    dve.tensor_copy(token_in[:, j % 2, :, :],
                                    merged[:, :, bass.ds(e, 1), :].rearrange("p c e b -> p c (e b)"))\
                        .then_inc(picked, 1)
                    if not first:
                        bias_up(*before(i, j))
                    dve.wait_ge(up_ps, e + 1)
                    if reuses(i, j):
                        dve.wait_ge(hT_ps, e - 1)
                    for half in range(2):
                        ins = dve.tensor_copy(hid_rows[:, j % 2, half * HALF:(half + 1) * HALF],
                                              bank[2 * (j % 2) + half][0:B, :])
                    ins.then_inc(hid_ready, 1)
                    if not first:
                        keep(*before(i, j))

                all_experts(dve, step)
                bias_up(*LAST)
                keep(*LAST)
                dve.wait_ge(out_read, 16)
                dve.wait_ge(gates_loaded, 32)
                dve.tensor_tensor(o_all[:, :, :], o_all[:, :, :],
                                  b2_rows[:, :].unsqueeze(1).to_broadcast([E1, B, C]), ALU.add)\
                    .then_inc(out_biased, 1)
                for b in range(B):
                    dve.wait_ge(sc_ps, b + 1)
                    dve.wait_ge(tok_loaded[b // PER], 16)
                    dve.tensor_tensor(tokens(b), tokens(b), bank[b % 4][:, :], ALU.add).then_inc(sum_ready, 1)

            @block.scalar
            def _(act):
                def gelu(j, n, reused):
                    act.wait_ge(biased, n)
                    if reused:
                        act.wait_ge(down_ps, n - 2)
                    act.activation(flat(act_out[:, j % 2]), flat(act_in[:, j % 2]), ACT.Gelu)\
                        .then_inc(gelu_ready, 1)

                def step(i, j):
                    if not (isinstance(i, int) and j == 0):
                        gelu(*before(i, j))

                all_experts(act, step)
                gelu(*LAST)


def rows_of(j):
    return BR * C >> 2 * j


def flat(x):
    a = x if isinstance(x, bass.AP) else x[tuple(slice(None) for _ in x.shape)]
    return a.rearrange("p a b -> p (a b)")


def rows(x, b):
    return x[bass.ds(b * T, T), :].rearrange("(t p) c -> p t c", p=P)


def mixes_before(h, old):
    return sum(at < h for at in (2, 7, 11, 15)) - (old is None and h > 2)


def skewed(scr, half, col, step, n, tile_step=0):
    a = scr[half].rearrange("t p x -> p t x")
    return bass.AP(tensor=a.tensor, offset=a.offset + col,
                   ap=[[PITCH + step, P], [P * PITCH + tile_step, NT], [1, n]])


def finish_copy(nc, ctx, src, out, sem):
    s = sem("copied")
    with nc.Block() as block:
        @block.sync
        def _(sp):
            sp.dma_start(out.rearrange("b t c -> (b t) c"), src).then_inc(s, 16)
            sp.wait_ge(s, 16)


def layout(inputs):
    import numpy as np
    f = {k: np.asarray(v) for k, v in inputs.items()}
    a = {}
    a["x"] = f["x"][..., 0]
    for j, name, n in ((1, "Wd3", BR // 2), (2, "Wd2", BR // 4), (3, "Wd1", BR // 8)):
        w = f["L0_tok_" + name].reshape(3, RB, n, C >> j, 3)
        a[f"wdet{j}"] = np.ascontiguousarray(w.transpose(1, 4, 0, 2, 3)).reshape(RB, 3, -1)
    a["wapp"] = f["L0_tok_Wa"].reshape(RB, C >> 3)
    a["dbias"] = np.concatenate([f["L0_tok_bd3"], f["L0_tok_bd2"], f["L0_tok_bd1"], f["L0_tok_ba"]])
    w, b = f["L0_attn_W_attn"], f["L0_attn_b_attn"]
    wqk = np.zeros((C, 2 * MQ * HPM, SLOT), w.dtype)
    wqk[:, :, :D0] = w[:2 * C].T.reshape(C, 2 * H0, D0)
    a["wqk0"] = wqk.reshape(C, -1)
    bqk = np.zeros((2 * H0, SLOT), b.dtype)
    bqk[:, :D0] = b[:2 * C].reshape(2 * H0, D0)
    a["bqk0"] = np.ascontiguousarray(bqk.reshape(2 * MQ, P).T)
    a["wv0"] = np.ascontiguousarray(w[2 * C:].T)
    a["bv0"] = b[2 * C:]
    a["wp0"] = np.ascontiguousarray(f["L0_attn_W_proj"].T)
    a["bp0"] = f["L0_attn_b_proj"]
    a["gamma"] = np.ascontiguousarray(f["L0_ffn_ln_gamma"].reshape(NC, P).T)
    a["beta"] = np.ascontiguousarray(f["L0_ffn_ln_beta"].reshape(NC, P).T)
    a["fc1_q"] = f["L0_ffn_fc1_q"]
    a["fc2_q"] = f["L0_ffn_fc2_q"]
    a["fc1_s"] = f["L0_ffn_fc1_scales"]
    a["fc2_s"] = f["L0_ffn_fc2_scales"]
    a["fc1b"] = np.ascontiguousarray(f["L0_ffn_fc1_bias"].reshape(NF, P).T)
    a["fc2b"] = f["L0_ffn_fc2_bias"]
    w, b = f["L1_attn_Wqkv"], f["L1_attn_bqkv"]
    a["wqk1"] = np.ascontiguousarray(w[:2 * INNER].T)
    a["bqk1"] = np.ascontiguousarray(b[:2 * INNER].reshape(-1, P).T)
    a["wv1"] = np.ascontiguousarray(w[2 * INNER:].T)
    a["bv1"] = b[2 * INNER:]
    a["wo1"] = np.ascontiguousarray(f["L1_attn_Wout"].T)
    a["bo1"] = f["L1_attn_bout"]
    at = 2 * MAXREL - np.arange(NREL)
    a["rel_k"] = np.ascontiguousarray(np.concatenate([f["L1_attn_rel_k_emb"][at].T] * 2))
    a["rel_v"] = f["L1_attn_rel_v_emb"][np.concatenate([2 * MAXREL - 1 - np.arange(BAND), [2 * MAXREL]])]
    a["relv0"] = f["L1_attn_rel_v_emb"][0]
    a["alphas"] = f["L1_attn_alphas_raw"]
    a["gate_w"] = np.ascontiguousarray(f["L1_ffn_gate_w"].T)
    a["gate_b"] = f["L1_ffn_gate_b"]
    w1, w2 = f["L1_ffn_w1"], f["L1_ffn_w2"]
    a["w1"] = w1
    a["w2"] = w2
    a["b1"] = np.ascontiguousarray(w1[:, C].reshape(E1, NH, P).transpose(2, 0, 1))
    return {k: np.ascontiguousarray(v) for k, v in a.items()}


def kernel(**inputs):
    import numpy as _np
    import concourse.bacc as _bacc
    from concourse import mybir as _mybir
    from concourse.bass_utils import run_bass_kernel_spmd as _run

    nc = _bacc.Bacc("TRN2", target_bir_lowering=False, num_devices=1)
    arrays = {f"in_{k}": v for k, v in layout(inputs).items()}
    aps = {k[3:]: nc.dram_tensor(k, v.shape, _mybir.dt.from_np(v.dtype), kind="ExternalInput").ap()
           for k, v in arrays.items()}
    out = nc.dram_tensor("out_tokens", (B, T, C), _mybir.dt.from_np(_np.dtype("float32")),
                         kind="ExternalOutput").ap()
    build(nc, aps, out)
    r = _run(nc, [arrays], core_ids=[0])
    return r.results[0]["out_tokens"]
```
